# Optimizing a Trainium2 kernel written in Bass

```python
import numpy as np
import jax
import jax.numpy as jnp

def _softmax(x, axis=-1):
    return jax.nn.softmax(x, axis=axis)

def _gelu(x):
    return jax.nn.gelu(x, approximate=True)

def _silu(x):
    return jax.nn.silu(x)

def _sigmoid(x):
    return jax.nn.sigmoid(x)

def _layernorm(x, axis=-1, eps=1e-05):
    m = jnp.mean(x, axis=axis, keepdims=True)
    v = jnp.var(x, axis=axis, keepdims=True)
    return (x - m) / jnp.sqrt(v + eps)

def _scatter_add(tgt, idx, src, axis=0):
    return tgt.at[idx].add(src)

def _segment_sum(src, seg, n):
    return jax.ops.segment_sum(src, seg, n)
kernel_name = 'mk_gnn_ffn_d1_gnn_r8_32ab7c'

def setup_inputs(seed: int=0):
    np.random.seed(seed)
    _w = jnp.asarray

    def _rec_inputs():
        import jax
        import jax.numpy as jnp
        _gk = jax.random.key(seed)
        x = -0.0002117 + 1 * jax.random.normal(jax.random.fold_in(_gk, 1), (12500, 256), jnp.float32)
        _s = jax.random.randint(jax.random.fold_in(_gk, 2), (100000,), 0, 12500, jnp.int32)
        _d = jax.random.randint(jax.random.fold_in(_gk, 3), (100000,), 0, 12500, jnp.int32)
        _loop = jnp.arange(12500, dtype=jnp.int32)
        src = jnp.concatenate([_s, _d, _loop])
        dst = jnp.concatenate([_d, _s, _loop])
        _o = jnp.argsort(dst, stable=True)
        src = src[_o]
        dst = dst[_o]
        return (x, src, dst)
    x, src, dst = _rec_inputs()

    def _L0_gnn_setup():
        import jax, jax.numpy as jnp
        import numpy as np
        N_NODES = 12500
        N_EDGES = 400000
        D_IN = 256
        D_OUT = 256
        LEAKY_SLOPE = 0.01
        key = jax.random.key(seed)
        ks = jax.random.split(key, 8)
        s_in = 1.0 / np.sqrt(D_IN)
        s_out = 1.0 / np.sqrt(D_OUT)
        return {'features': jax.random.normal(ks[0], (N_NODES, D_IN), dtype=jnp.float32), 'indices': jax.random.randint(ks[1], (2, N_EDGES), 0, N_NODES, dtype=jnp.int64), 'W_layer': jax.random.uniform(ks[2], (D_OUT, D_IN), jnp.float32, -s_in, s_in), 'b_layer': jax.random.uniform(ks[3], (D_OUT,), jnp.float32, -s_in, s_in), 'w_a1': jax.random.uniform(ks[4], (1, D_OUT), jnp.float32, -s_out, s_out), 'b_a1': jax.random.uniform(ks[5], (1,), jnp.float32, -s_out, s_out), 'w_a2': jax.random.uniform(ks[6], (1, D_OUT), jnp.float32, -s_out, s_out), 'b_a2': jax.random.uniform(ks[7], (1,), jnp.float32, -s_out, s_out)}
    _L0_gnn_all = _L0_gnn_setup()
    _L0_gnn_in = {k: v for k, v in _L0_gnn_all.items() if k in ('W_layer', 'b_layer', 'w_a1', 'b_a1', 'w_a2', 'b_a2')}
    del _L0_gnn_all

    def _L0_ffn_setup():
        import jax, jax.numpy as jnp
        import numpy as np
        B, N, D = (16, 512, 256)
        NUM_EXPERTS, TOP_K, HEADS = (4, 2, 4)
        N_EDGES = 131072
        LN_EPS = 1e-05

        def _layernorm(x, g, b):
            mu = x.mean(-1, keepdims=True)
            var = ((x - mu) ** 2).mean(-1, keepdims=True)
            return (x - mu) * jax.lax.rsqrt(var + LN_EPS) * g + b

        def _forward(x, edge_index, W_gat, att_src, att_dst, b_gat, ln_gamma, ln_beta, W1, b1, W2, b2):
            Bc, Nc, Dc = x.shape
            M = Bc * Nc
            x_flat = x.reshape(M, Dc)
            h = (x_flat @ W_gat).reshape(M, HEADS, NUM_EXPERTS)
            loops = jnp.arange(M, dtype=edge_index.dtype)
            src = jnp.concatenate([edge_index[0], loops])
            dst = jnp.concatenate([edge_index[1], loops])
            a_src = (h * att_src).sum(-1)
            a_dst = (h * att_dst).sum(-1)
            e = jax.nn.leaky_relu(a_src[src] + a_dst[dst], negative_slope=0.2)
            e_max = jax.ops.segment_max(e, dst, num_segments=M)
            ee = jnp.exp(e - e_max[dst])
            denom = jax.ops.segment_sum(ee, dst, num_segments=M)
            alpha = ee / (denom[dst] + 1e-16)
            msg = h[src] * alpha[:, :, None]
            agg = jax.ops.segment_sum(msg, dst, num_segments=M).reshape(M, HEADS * NUM_EXPERTS) + b_gat
            scores = _layernorm(agg, ln_gamma, ln_beta).reshape(M, HEADS, NUM_EXPERTS).mean(1)
            scores = scores.reshape(Bc, Nc, NUM_EXPERTS)
            topk_s, topk_i = jax.lax.top_k(scores, TOP_K)
            w = jax.nn.softmax(topk_s, axis=-1)
            out = jnp.zeros_like(x)
            for ei in range(NUM_EXPERTS):
                g = jnp.where(topk_i == ei, w, 0.0).sum(-1)
                hh = jax.nn.gelu(x @ W1[ei] + b1[ei], approximate=False)
                out = out + g[..., None] * (hh @ W2[ei] + b2[ei])
            return out
        key = jax.random.key(seed)
        ks = jax.random.split(key, 8)
        s = 0.05
        return {'x': jax.random.normal(ks[0], (B, N, D), jnp.float32), 'W_gat': jax.random.normal(ks[1], (D, HEADS * NUM_EXPERTS), jnp.float32) * s, 'att_src': jax.random.normal(ks[2], (HEADS, NUM_EXPERTS), jnp.float32) * s, 'att_dst': jax.random.normal(ks[3], (HEADS, NUM_EXPERTS), jnp.float32) * s, 'b_gat': jnp.zeros((HEADS * NUM_EXPERTS,), jnp.float32), 'ln_gamma': jnp.ones((HEADS * NUM_EXPERTS,), jnp.float32), 'ln_beta': jnp.zeros((HEADS * NUM_EXPERTS,), jnp.float32), 'W1': jax.random.normal(ks[4], (NUM_EXPERTS, D, 2 * D), jnp.float32) * s, 'b1': jnp.zeros((NUM_EXPERTS, 2 * D), jnp.float32), 'W2': jax.random.normal(ks[5], (NUM_EXPERTS, 2 * D, D), jnp.float32) * s, 'b2': jnp.zeros((NUM_EXPERTS, D), jnp.float32), 'edge_index': jax.random.randint(ks[6], (2, N_EDGES), 0, B * N, jnp.int32)}
    _L0_ffn_all = _L0_ffn_setup()
    _L0_ffn_in = {k: v for k, v in _L0_ffn_all.items() if k in ('W_gat', 'att_src', 'att_dst', 'b_gat', 'ln_gamma', 'ln_beta', 'W1', 'b1', 'W2', 'b2', 'edge_index')}
    del _L0_ffn_all
    return {'x': x, 'src': src, 'dst': dst, 'L0_gnn_W_layer': _L0_gnn_in['W_layer'], 'L0_gnn_b_layer': _L0_gnn_in['b_layer'], 'L0_gnn_w_a1': _L0_gnn_in['w_a1'], 'L0_gnn_b_a1': _L0_gnn_in['b_a1'], 'L0_gnn_w_a2': _L0_gnn_in['w_a2'], 'L0_gnn_b_a2': _L0_gnn_in['b_a2'], 'L0_ffn_W_gat': _L0_ffn_in['W_gat'], 'L0_ffn_att_src': _L0_ffn_in['att_src'], 'L0_ffn_att_dst': _L0_ffn_in['att_dst'], 'L0_ffn_b_gat': _L0_ffn_in['b_gat'], 'L0_ffn_ln_gamma': _L0_ffn_in['ln_gamma'], 'L0_ffn_ln_beta': _L0_ffn_in['ln_beta'], 'L0_ffn_W1': _L0_ffn_in['W1'], 'L0_ffn_b1': _L0_ffn_in['b1'], 'L0_ffn_W2': _L0_ffn_in['W2'], 'L0_ffn_b2': _L0_ffn_in['b2'], 'L0_ffn_edge_index': _L0_ffn_in['edge_index']}

def reference(x, src, dst, L0_gnn_W_layer, L0_gnn_b_layer, L0_gnn_w_a1, L0_gnn_b_a1, L0_gnn_w_a2, L0_gnn_b_a2, L0_ffn_W_gat, L0_ffn_att_src, L0_ffn_att_dst, L0_ffn_b_gat, L0_ffn_ln_gamma, L0_ffn_ln_beta, L0_ffn_W1, L0_ffn_b1, L0_ffn_W2, L0_ffn_b2, L0_ffn_edge_index):
    import jax
    import jax.numpy as jnp

    def _L0_gnn_ref(features, indices, W_layer, b_layer, w_a1, b_a1, w_a2, b_a2):
        import jax, jax.numpy as jnp
        import numpy as np
        N_NODES = 12500
        N_EDGES = 400000
        D_IN = 256
        D_OUT = 256
        LEAKY_SLOPE = 0.01
        n = features.shape[0]
        h = features @ W_layer.T + b_layer
        a1 = (h @ w_a1.T + b_a1)[:, 0]
        a2 = (h @ w_a2.T + b_a2)[:, 0]
        row = indices[0]
        col = indices[1]
        v = jax.nn.leaky_relu(a1[row] + a2[col], negative_slope=LEAKY_SLOPE)
        m = jax.ops.segment_max(v, row, num_segments=n)
        ev = jnp.exp(v - m[row])
        s = jax.ops.segment_sum(ev, row, num_segments=n)
        att = ev / s[row]
        out = jax.ops.segment_sum(att[:, None] * h[col], row, num_segments=n)
        return out

    def _L0_ffn_ref(x, W_gat, att_src, att_dst, b_gat, ln_gamma, ln_beta, W1, b1, W2, b2, edge_index):
        import jax, jax.numpy as jnp
        import numpy as np
        B, N, D = (16, 512, 256)
        NUM_EXPERTS, TOP_K, HEADS = (4, 2, 4)
        N_EDGES = 131072
        LN_EPS = 1e-05

        def _layernorm(x, g, b):
            mu = x.mean(-1, keepdims=True)
            var = ((x - mu) ** 2).mean(-1, keepdims=True)
            return (x - mu) * jax.lax.rsqrt(var + LN_EPS) * g + b

        def _forward(x, edge_index, W_gat, att_src, att_dst, b_gat, ln_gamma, ln_beta, W1, b1, W2, b2):
            Bc, Nc, Dc = x.shape
            M = Bc * Nc
            x_flat = x.reshape(M, Dc)
            h = (x_flat @ W_gat).reshape(M, HEADS, NUM_EXPERTS)
            loops = jnp.arange(M, dtype=edge_index.dtype)
            src = jnp.concatenate([edge_index[0], loops])
            dst = jnp.concatenate([edge_index[1], loops])
            a_src = (h * att_src).sum(-1)
            a_dst = (h * att_dst).sum(-1)
            e = jax.nn.leaky_relu(a_src[src] + a_dst[dst], negative_slope=0.2)
            e_max = jax.ops.segment_max(e, dst, num_segments=M)
            ee = jnp.exp(e - e_max[dst])
            denom = jax.ops.segment_sum(ee, dst, num_segments=M)
            alpha = ee / (denom[dst] + 1e-16)
            msg = h[src] * alpha[:, :, None]
            agg = jax.ops.segment_sum(msg, dst, num_segments=M).reshape(M, HEADS * NUM_EXPERTS) + b_gat
            scores = _layernorm(agg, ln_gamma, ln_beta).reshape(M, HEADS, NUM_EXPERTS).mean(1)
            scores = scores.reshape(Bc, Nc, NUM_EXPERTS)
            topk_s, topk_i = jax.lax.top_k(scores, TOP_K)
            w = jax.nn.softmax(topk_s, axis=-1)
            out = jnp.zeros_like(x)
            for ei in range(NUM_EXPERTS):
                g = jnp.where(topk_i == ei, w, 0.0).sum(-1)
                hh = jax.nn.gelu(x @ W1[ei] + b1[ei], approximate=False)
                out = out + g[..., None] * (hh @ W2[ei] + b2[ei])
            return out
        return _forward(x, edge_index, W_gat, att_src, att_dst, b_gat, ln_gamma, ln_beta, W1, b1, W2, b2)
    edge_index = jnp.stack([src, dst])
    x = x + _L0_gnn_ref(_layernorm(x, axis=-1), edge_index, L0_gnn_W_layer, L0_gnn_b_layer, L0_gnn_w_a1, L0_gnn_b_a1, L0_gnn_w_a2, L0_gnn_b_a2)
    x = x + _L0_ffn_ref(_layernorm(x, axis=-1)[None], L0_ffn_W_gat, L0_ffn_att_src, L0_ffn_att_dst, L0_ffn_b_gat, L0_ffn_ln_gamma, L0_ffn_ln_beta, L0_ffn_W1, L0_ffn_b1, L0_ffn_W2, L0_ffn_b2, L0_ffn_edge_index)[0]
    return x

_drawn_inputs = setup_inputs


def setup_inputs(seed=0):
    import zlib

    import numpy as np

    out = dict(_drawn_inputs(seed))
    spreads = {'L0_ffn_b_gat': (0.0, 0.1),
     'L0_ffn_ln_gamma': (1.0, 0.2),
     'L0_ffn_ln_beta': (0.0, 0.1),
     'L0_ffn_b1': (0.0, 0.1),
     'L0_ffn_b2': (0.0, 0.1)}
    factors = {}
    for name, (base, spread) in spreads.items():
        noise = np.random.default_rng([zlib.crc32(name.encode()), seed]).standard_normal(out[name].shape)
        drawn = base * np.exp(spread * noise) if base else spread * noise
        out[name] = jnp.asarray(drawn.astype(out[name].dtype))
    for name, factor in factors.items():
        out[name] = (out[name] * factor).astype(out[name].dtype)
    return out
```

```python
from contextlib import ExitStack, contextmanager

import numpy as np

import concourse.bass as bass
from concourse import mybir

FP32 = mybir.dt.float32
I32 = mybir.dt.int32
ALU = mybir.AluOpType
ACT = mybir.ActivationFunctionType
AX = mybir.AxisListType

P = 128
NODES = 12500
D = 256
TILES = -(-NODES // P)
PADDED = TILES * P
LAST = NODES - (TILES - 1) * P
W = 2048
HEADER_PARTS = 125
HEADERS = NODES // HEADER_PARTS
EXPERTS, HEADS, HID = 4, 4, 512
HE = HEADS * EXPERTS
EPS = 1e-5
BIG = 1e30
TAG = 0x20000000
TAG_FLOAT = float(np.array([TAG], np.int32).view(np.float32)[0])
LOW = (1 << 14) - 1
PAD_ROW = PADDED - 1
GW_IN = 24
ROW = D + 2
U = 16


class Graph:
    def __init__(self, edges, step_unit):
        self.edges = edges
        self.tiles = -(-(edges + NODES) // P)
        self.cols = 16 * -(-self.tiles // 16)
        self.steps = U * -(-(self.tiles + TILES - 1) // U)
        self.jj = -(-(self.cols + TILES) // P)
        self.q = self.jj * P


GNN = Graph(212500, U)
GATE = Graph(131072, U)


class Tally:

    def __init__(self, sem, start=0):
        self.sem, self.base, self.local = sem, start, 0

    def add(self, ins, k=1):
        ins.then_inc(self.sem, k)
        self.local += k
        return self.base + self.local

    @property
    def n(self):
        return self.base + self.local


@contextmanager
def loop(eng, count, *tallies):
    starts = [t.n for t, _ in tallies]
    with eng.Fori(0, count) as i:
        for (t, per), s in zip(tallies, starts):
            t.base, t.local = s + i * per, 0
        yield i
    for (t, per), s in zip(tallies, starts):
        assert t.local == per, (t.local, per)
        t.base, t.local = s + count * per, 0


def halves(v, j):
    x = v.rearrange("p (x b l) -> p x b l", b=2, l=1 << j)
    return x[:, :, 0, :], x[:, :, 1, :]


def turn_buffers():
    c, order = 0, []
    for k in range(1, 11):
        c = (c + k) % 2
    c = (c + 1 + 11) % 2
    for k in range(12, 19):
        c = (c + 1) % 2
        order.append(c)
        c = (c + 1 + (k - 12)) % 2
        order.append(c)
        c = (c + 1 + 10) % 2
    order.append(c)
    return order


def program(nc, a, out, consts):
    ctx = ExitStack()
    with ctx:
        def sb(name, shape, dt=FP32):
            return ctx.enter_context(nc.sbuf_tensor(name, shape, dt))

        def sem(name):
            return ctx.enter_context(nc.semaphore(name))

        def dram(name, shape, dt=FP32):
            return nc.dram_tensor(name, shape, dt, kind="Internal").ap()

        h_table = dram("h_table", (PADDED, ROW))
        stash = dram("stash", (GNN.steps // 8, P, 8, D))
        x1_rows = dram("x1_rows", (PADDED, D))
        xT_tiles = dram("xT_tiles", (TILES, P, 2 * P))
        gate_table = dram("gate_table", (PADDED, GW_IN))
        y_rows = dram("y_rows", (PADDED, EXPERTS * D))
        gnn_blocks = dram("gnn_blocks", (P, GNN.jj), I32)
        gate_blocks = dram("gate_blocks", (P, GATE.jj), I32)
        gate_blocks_f = dram("gate_blocks_f", (1, GATE.q))
        last_steps = dram("last_steps", (TILES, 1), I32)

        R1 = sb("R1", [P, GATE.q * GW_IN])
        WK = sb("WK", [P, 17552])
        FK = sb("FK", [P, GATE.q])
        FI = sb("FI", [P, GATE.q])
        S, E, A = WK[:, 0:4112], WK[:, 4112:11792], WK[:, 11792:17552]
        sort_bufs = [S[:, 0:W], S[:, W:2 * W]]
        spare = E[:, 0:1024]
        XR = R1[:, 0:TILES * D].rearrange("p (t d) -> p t d", d=D)
        ACC = R1[:, 0:TILES * 257].rearrange("p (t d) -> p t d", d=257)
        G = R1[:, :].rearrange("p (q w) -> p q w", w=GW_IN)
        KS = A[:, 0:GNN.q]
        GI, GR = A[:, GNN.q:2 * GNN.q], A[:, 2 * GNN.q:3 * GNN.q]
        ident, iota_row = sb("ident", [P, P]), sb("iota_row", [P, P])
        signs, part_id = sb("signs", [P, 8]), sb("part_id", [P, 1])
        stat = sb("stat", [P, TILES, 2])
        rstd, shift = sb("rstd", [P, TILES]), sb("shift", [P, TILES])
        eps = sb("eps", [P, 1])
        att, att_prod = sb("att", [P, 2, HE]), sb("att_prod", [P, 2, HE])
        gate_w = sb("gate_w", [P, 2, GW_IN])
        idx_slots = sb("idx_slots", [P, U], I32)
        waited = sb("waited", [P, 1 + 2 * GNN.steps // U])
        col, row, carry = sb("col", [P, 2]), sb("row", [1, 2 * P]), sb("carry", [1, P + 1])
        ccol = sb("ccol", [P, 1])
        ps = ctx.enter_context(nc.psum_tensor("ps", [P, 8 * 512], FP32))

        nb = A[:, GNN.q:]
        xn = [nb[:, s * 256:(s + 1) * 256] for s in range(2)]
        xT = [nb[:, 512 + s * 256:768 + s * 256] for s in range(2)]
        lin = [nb[:, 1024 + s * 258:1024 + (s + 1) * 258] for s in range(2)]
        w_nat = nb[:, 1540:2052].rearrange("p (k d) -> p k d", k=2)
        wa = nb[:, 2052:2056].rearrange("p (k w) -> p k w", k=2)
        bcol = nb[:, 2056:2058]
        ba = nb[0:1, 2058:2060]
        proj = nb[:, 2400:2916].rearrange("p (k n) -> p k n", k=2)
        bias_row, ones_row = nb[0:1, 2916:3174], nb[0:1, 3400:3528]
        bn = E[:, 1024:1024 + 6 * TILES].rearrange("p (t s) -> p t s", s=6)
        psT = [ps[:, 2048 + s * 512:2048 + s * 512 + 256] for s in range(2)]
        psL = [ps[:, 3072 + s * 512:3072 + s * 512 + 258] for s in range(2)]

        consts_in, w_in = sem("consts_in"), sem("w_in")
        x_in = [sem(f"x_in{c}") for c in range(7)]
        filled, keys_in = sem("filled"), sem("keys_in")
        dve_done, to_turn, turned = sem("dve_done"), sem("to_turn"), sem("turned")
        stat_ready, std_ready = sem("stat_ready"), sem("std_ready")
        prep_turned, prep_copied, proj_ready = sem("prep_turned"), sem("prep_copied"), sem("proj_ready")
        xn_ready, xn_turned, xT_ready = sem("xn_ready"), sem("xn_turned"), sem("xT_ready")
        lin_ready, lin_copied = sem("lin_ready"), sem("lin_copied")
        rows_out = [sem(f"rows_out{s}") for s in range(2)]
        xT_out = [sem(f"xT_out{s}") for s in range(2)]
        stashed = [sem(f"stashed{h}") for h in range(2)]
        rows_in = [sem(f"rows_in{h}") for h in range(4)]
        a_kept = sem("a_kept")
        idx_ready, idx_staged = sem("idx_ready"), sem("idx_staged")
        landed = [sem(f"landed{s}") for s in range(U)]
        rows_kept = sem("rows_kept")
        blocks_ready, blocks_out, blocks_in = sem("blocks_ready"), sem("blocks_out"), sem("blocks_in")
        hot_ready, summed, added = sem("hot_ready"), sem("summed"), sem("added")
        ones_set = sem("ones_set")
        xg_in = [sem(f"xg_in{s}") for s in range(2)]
        xg_last = sem("xg_last")
        xg_used, x1_ready, x1_out = sem("xg_used"), sem("x1_ready"), sem("x1_out")
        gate_w_in, gate_w_ready = sem("gate_w_in"), sem("gate_w_ready")
        weights_in = sem("weights_in")
        xe_in = [sem(f"xe_in{s}") for s in range(2)]
        hid_ready, gelu_done = sem("hid_ready"), sem("gelu_done")
        y_ready, y_copied = sem("y_ready"), sem("y_copied")
        y_out = [sem(f"y_out{s}") for s in range(2)]
        exp_ready, exp_done = sem("exp_ready"), sem("exp_done")
        agg_ready, agg_done = sem("agg_ready"), sem("agg_done")
        gate_in, gates_need = sem("gate_in"), sem("gates_need")
        fin_in = [sem(f"fin_in{s}") for s in range(4)]
        fin_ready = sem("fin_ready")
        fin_out = [sem(f"fin_out{s}") for s in range(4)]

        block = ctx.enter_context(nc.Block())
        NP2 = TILES // 2
        GNN_KEPT = 2 * GNN.steps // U
        GATE_KEPT = 2 * GATE.steps // U
        GNN_HOTS = GNN.steps + 8

        g_scan = [R1[:, i * GNN.q:(i + 1) * GNN.q] for i in range(16)]
        a12 = R1[:, 14 * GNN.q:16 * GNN.q].rearrange("p (q w) -> p q w", w=2)
        f_scan = [WK[:, i * GATE.q:(i + 1) * GATE.q] for i in range(13)]
        first_rows = R1[:, 0:U * ROW].rearrange("p (s w) -> p s w", w=ROW)
        gbuf = [v.rearrange("p (s w) -> p s w", w=257) for v in
                (S[:, 0:U * 257], R1[:, TILES * 257:TILES * 257 + U * 257])]
        hot = E[:, 0:U * P].rearrange("p (s n) -> p s n", n=P)
        blk_row = E[0:1, 2048:2048 + GNN.q]
        gate_slots = WK[:, 16400:16400 + U * GW_IN].rearrange("p (s w) -> p s w", w=GW_IN)
        xin = [E[:, 4096 + s * 1792:4096 + (s + 1) * 1792].rearrange("p (t d) -> p t d", d=D)
               for s in range(2)]
        w1 = WK[:, 0:4096].rearrange("p (k f) -> p k f", k=2)
        w2 = WK[:, 4096:8192].rearrange("p (c d) -> p c d", d=D)
        hidT = WK[:, 8192:10240].rearrange("p (s f n) -> p s f n", s=2, f=4)
        xe = WK[:, 10240:11264].rearrange("p (s t k n) -> p s t k n", s=2, t=2, k=2)
        ystage = WK[:, 11264:15360].rearrange("p (s t e d) -> p s t e d", s=2, t=2, e=EXPERTS)
        b2_all = WK[:, 15360:16384].rearrange("p (e d) -> p e d", e=EXPERTS)
        b1_cols = sb("b1_cols", [P, 16])
        keep, block_rows = f_scan[11], f_scan[12]
        last_col, last_row = sb("last_col", [P, 1], I32), sb("last_row", [1, TILES], I32)

        def tiles_of(first, n):
            return WK[:, first:first + TILES * n].rearrange("p (t n) -> p t n", n=n)

        sums, agg, squares = tiles_of(6400, 20), tiles_of(8400, HE), tiles_of(10000, HE)
        den, scores, gates, beaten = (tiles_of(11600 + 400 * i, 4) for i in range(4))
        mu, var = WK[:, 13200:13200 + TILES], WK[:, 13300:13300 + TILES]
        gat_bias, gamma, beta = (WK[:, 13400 + HE * i:13400 + HE * (i + 1)] for i in range(3))
        yin = R1[:, 0:4096].rearrange("p (s n) -> p s n", s=4)
        x1in, mixed = (R1[:, 4096 + 1024 * i:5120 + 1024 * i].rearrange("p (s n) -> p s n", s=4) for i in range(2))
        GROUPS = TILES // 2

        @block.sync
        def _(sp):
            for dst_, src_ in ((ident, consts["ident"]), (iota_row, consts["iota_row"]),
                               (signs, consts["signs"]), (part_id, consts["part_id"])):
                sp.dma_start(dst_[:, :], src_).then_inc(consts_in, 16)
            sp.wait_ge(filled, 4)

            def load_keys(rows, cols, parts):
                n = rows.shape[0] // parts
                r, c = (sort_bufs[i].bitcast(I32) for i in range(2))
                sp.dma_start(r[0:parts, 0:n], rows.rearrange("(p c) -> p c", p=parts)).then_inc(keys_in, 16)
                sp.dma_start(c[0:parts, 0:n], cols.rearrange("(p c) -> p c", p=parts)).then_inc(keys_in, 16)
                sp.dma_start(r[0:HEADER_PARTS, n:n + HEADERS], consts["headers"]).then_inc(keys_in, 16)

            load_keys(a["src"], a["dst"], HEADER_PARTS)
            x_tiles = a["x"][0:(TILES - 1) * P, :].rearrange("(t p) d -> p t d", p=P)
            for c in range(7):
                n = 14 if c < 6 else 13
                sp.dma_start(XR[:, 14 * c:14 * c + n, :], x_tiles[:, 14 * c:14 * c + n, :]).then_inc(x_in[c], 16)
            sp.dma_start(XR[0:LAST, TILES - 1, :], a["x"][(TILES - 1) * P:, :]).then_inc(x_in[6], 16)
            sp.dma_start(w_nat, a["W_layer"].rearrange("(k p) d -> p k d", p=P)).then_inc(w_in, 16)
            for i, name in enumerate(("w_a1", "w_a2")):
                sp.dma_start(wa[:, :, i], a[name][0, :].rearrange("(k p) -> p k", p=P),
                         allow_slow_non_contiguous=True).then_inc(w_in, 16)
            sp.dma_start(bcol, a["b_layer"].rearrange("(k p) -> p k", p=P),
                         allow_slow_non_contiguous=True).then_inc(w_in, 16)
            sp.dma_start(bias_row[0:1, 0:D], a["b_layer"].rearrange("(o n) -> o n", o=1)).then_inc(w_in, 16)
            for i, name in enumerate(("b_a1", "b_a2")):
                sp.dma_start(ba[:, i:i + 1], a[name].rearrange("(o n) -> o n", o=1)).then_inc(w_in, 16)

            def rows(table, width, base, pair):
                for s in range(2):
                    sp.wait_ge(lin_copied, base + pair * 2 + s + 1)
                    sp.dma_start(table[bass.ds((pair * 2 + s) * P, P), :], lin[s][:, 0:width]).then_inc(rows_out[s], 16)

            with sp.Fori(0, NP2) as i:
                rows(h_table, ROW, 0, i)
            sp.wait_ge(filled, 8)
            load_keys(a["edge_index"][1, :], a["edge_index"][0, :], P)
            sp.dma_start(gate_w[:, :, 0:HE], a["W_gat"].rearrange("(k p) n -> p k n", p=P)).then_inc(gate_w_in, 16)
            for w, name in enumerate(("att_src", "att_dst")):
                sp.dma_start(att[:, w, :], a[name].rearrange("h e -> (h e)").partition_broadcast(P)).then_inc(gate_w_in, 16)

            with sp.Fori(0, GNN.steps // U) as i:
                for h in range(2):
                    for s in range(8 * h, 8 * h + 8):
                        sp.wait_ge(landed[s], (i + 1) * 16)
                    sp.dma_start(stash[bass.ds(2 * i + h, 1)].rearrange("o p s d -> p (o s) d"),
                                 first_rows[:, 8 * h:8 * h + 8, 0:D]).then_inc(stashed[h], 16)

            sp.wait_ge(blocks_ready, 1)
            sp.dma_start(gnn_blocks, g_scan[9][:, 0:GNN.jj].bitcast(I32)).then_inc(blocks_out, 16)
            sp.wait_ge(blocks_out, 16)
            sp.wait_ge(ones_set, 1)
            sp.dma_start(blk_row.bitcast(I32), gnn_blocks.rearrange("p (o j) -> o (p j)", o=1)).then_inc(blocks_in, 16)

            for h in range(2):
                sp.wait_ge(stashed[h], 16 * (GNN.steps // U))

            def rows_back(n, h):
                sp.dma_start(gbuf[h // 2][:, 8 * (h % 2):8 * (h % 2) + 8, 0:D],
                             stash[bass.ds(n, 1)].rearrange("o p s d -> p (o s) d")).then_inc(rows_in[h], 16)

            for h in range(4):
                rows_back(h, h)
            with sp.Fori(1, GNN.steps // 32) as i:
                for h in range(4):
                    sp.wait_ge(summed, (i - 1) * 32 + 8 * h + 8)
                    rows_back(4 * i + h, h)

            for s in range(2):
                sp.dma_start(xin[s], x_tiles[:, 7 * s:7 * s + 7, :]).then_inc(xg_in[s], 16)
            with sp.Fori(0, 5) as i:
                for s in range(2):
                    sp.wait_ge(xg_used, 2 * i + s + 1)
                    sp.dma_start(xin[s], x_tiles[:, bass.ds((2 * i + 2 + s) * 7, 7), :]).then_inc(xg_in[s], 16)
            sp.wait_ge(xg_used, 11)
            sp.dma_start(xin[0], x_tiles[:, 84:91, :]).then_inc(xg_in[0], 16)
            sp.wait_ge(xg_used, 12)
            sp.dma_start(xin[1][:, 0:6, :], x_tiles[:, 91:97, :]).then_inc(xg_in[1], 16)
            sp.dma_start(xin[1][0:LAST, 6, :], a["x"][(TILES - 1) * P:, :]).then_inc(xg_last, 16)
            x1_view = x1_rows.rearrange("(t p) d -> p t d", p=P)
            for c in range(7):
                sp.wait_ge(xg_used, 2 * c + 2)
                sp.dma_start(x1_view[:, 14 * c:14 * c + 14, :], ACC[:, 14 * c:14 * c + 14, 0:D]).then_inc(x1_out, 16)

            with sp.Fori(0, NP2) as i:
                for s in range(2):
                    t = i * 2 + s
                    sp.wait_ge(xT_ready, TILES + t + 1)
                    sp.dma_start(xT_tiles[bass.ds(t, 1), :, :].rearrange("o p n -> (o p) n"), xT[s]).then_inc(xT_out[s], 16)
                rows(gate_table, GW_IN, TILES, i)

            sp.wait_ge(x1_out, 16 * 7)
            for s in range(2):
                sp.wait_ge(rows_out[s], 16 * 2 * NP2)
                sp.wait_ge(xT_out[s], 16 * NP2)
            for k in range(2):
                sp.dma_start(w1[:, k, :].rearrange("p (e f) -> p e f", e=EXPERTS),
                             a["W1"].rearrange("e (k p) f -> k p e f", p=P)[k]).then_inc(weights_in, 16)
            sp.dma_start(w2, a["W2"].rearrange("e f d -> (e f) d").rearrange("(c p) d -> p c d", p=P)).then_inc(weights_in, 16)
            sp.dma_start(b1_cols[:, :], a["b1"].rearrange("e f -> (e f)").rearrange("(c p) -> p c", p=P),
                         allow_slow_non_contiguous=True).then_inc(weights_in, 16)
            sp.dma_start(b2_all.rearrange("p e d -> p (e d)"),
                         a["b2"].rearrange("e d -> (e d)").partition_broadcast(P)).then_inc(weights_in, 16)

            def load_xe(g, s):
                sp.dma_start(xe[:, s].rearrange("p t k n -> p t (k n)"),
                             xT_tiles[bass.ds(g * 2, 2), :, :].rearrange("t p n -> p t n")).then_inc(xe_in[s], 16)

            def store_y(g, s):
                sp.dma_start(y_rows[bass.ds(g * 2 * P, 2 * P), :].rearrange("(t p) n -> p t n", p=P),
                             ystage[:, s].rearrange("p t e d -> p t (e d)")).then_inc(y_out[s], 16)

            load_xe(0, 0)
            load_xe(1, 1)

            def next_group(g, s, load):
                sp.wait_ge(y_copied, (g + 1) * EXPERTS)
                store_y(g, s)
                if load:
                    load_xe(g + 2, s)

            with sp.Fori(0, GROUPS // 2 - 1) as i:
                for s in range(2):
                    next_group(i * 2 + s, s, True)
            next_group(GROUPS - 3, 0, True)
            next_group(GROUPS - 2, 1, False)
            next_group(GROUPS - 1, 0, False)

            sp.wait_ge(blocks_ready, 2)
            sp.dma_start(gate_blocks, f_scan[11][:, 0:GATE.jj].bitcast(I32)).then_inc(gate_in, 16)
            sp.wait_ge(gate_in, 16)
            sp.dma_start(f_scan[12][0:1, :].bitcast(I32), gate_blocks.rearrange("p (o j) -> o (p j)", o=1)).then_inc(gate_in, 16)
            sp.wait_ge(blocks_ready, 3)
            sp.dma_start(gate_blocks_f, f_scan[11][0:1, :]).then_inc(gate_in, 16)
            sp.wait_ge(gate_in, 48)
            sp.wait_ge(blocks_ready, 4)
            sp.dma_start(block_rows, gate_blocks_f[0, :].partition_broadcast(P)).then_inc(gate_in, 16)
            sp.wait_ge(blocks_ready, 5)
            for ap_, name in ((gat_bias, "b_gat"), (gamma, "ln_gamma"), (beta, "ln_beta")):
                sp.dma_start(ap_, a[name].partition_broadcast(P)).then_inc(gates_need, 16)
            sp.dma_start(last_steps, last_col[0:TILES, :],
                         allow_slow_non_contiguous=True).then_inc(gate_in, 16)
            sp.wait_ge(gate_in, 80)
            sp.dma_start(last_row[:, :], last_steps.rearrange("t o -> o t"),
                         allow_slow_non_contiguous=True).then_inc(gate_in, 16)

            for s in range(2):
                sp.wait_ge(y_out[s], 16 * (GROUPS // 2 + (1 - s)))
            sp.wait_ge(blocks_ready, 6)

            def load_mix(t, s):
                sp.dma_start(yin[:, s, :], y_rows[bass.ds(t * P, P), :]).then_inc(fin_in[s], 16)
                sp.dma_start(x1in[:, s, :], x1_rows[bass.ds(t * P, P), :]).then_inc(fin_in[s], 16)

            for s in range(4):
                load_mix(s, s)
            with sp.Fori(0, 23) as i:
                for s in range(4):
                    sp.wait_ge(fin_out[s], 16 * (i + 1))
                    load_mix(4 * i + 4 + s, s)
            for s in range(2):
                sp.wait_ge(fin_out[s], 16 * 24)
                load_mix(96 + s, s)

        @block.gpsimd
        def _(pool):
            r, c = (sort_bufs[i].bitcast(I32) for i in range(2))
            pool.memset(waited[:, :], 0.0)
            pool.memset(r, PAD_ROW).then_inc(filled, 1)
            pool.memset(c, 1).then_inc(filled, 1)
            pool.wait_ge(filled, 2)
            pool.memset(c[0:HEADER_PARTS, 1700:1700 + HEADERS], 0).then_inc(filled, 1)
            pool.memset(XR[:, TILES - 1, :], 0.0).then_inc(filled, 1)

            staged = Tally(idx_staged, 2 * GNN.steps // U)

            def hold(n):
                pool.tensor_tensor(waited[:, bass.ds(n, 1)] if not isinstance(n, int) else waited[:, n:n + 1], waited[:, 0:1], waited[:, 0:1], ALU.add)

            kept = Tally(rows_kept)
            slots_used = [0]

            def gather(s, table, dest):
                pool.indirect_dma_start(dest, None, table,
                                        bass.IndirectOffsetOnAxis(ap=idx_slots[:, s:s + 1], axis=0)
                                        ).then_inc(landed[s], 16)

            def gather_resident(g, table, idx, slot, dest):
                turns = g.steps // U
                base = slots_used[0]

                def keep(i, h):
                    for s in range(8 * h, 8 * h + 8):
                        pool.wait_ge(landed[s], (i + 1 + base) * 16)
                    return kept.add(pool.tensor_copy(dest(i, h), slot(h)))

                def stage(i, h):
                    pool.wait_ge(idx_staged, staged.add(pool.tensor_copy(
                        idx_slots[:, 8 * h:8 * h + 8], idx[:, bass.ds(i * U + 8 * h, 8)])))
                    pool.tensor_tensor(waited[:, 0:1], waited[:, 0:1], waited[:, 0:1], ALU.add)
                    for s in range(8 * h, 8 * h + 8):
                        gather(s, table, slot(h)[:, s - 8 * h] if len(slot(h).shape) == 3 else slot(h)[:, s - 8 * h:s - 8 * h + 1])

                for h in range(2):
                    stage(0, h)
                with loop(pool, turns - 1, (staged, 2), (kept, 2)) as i:
                    for h in range(2):
                        pool.wait_ge(rows_kept, keep(i, h))
                        stage(i + 1, h)
                for h in range(2):
                    keep(turns - 1, h)
                slots_used[0] += turns

            for s in range(2):
                pool.wait_ge(rows_out[s], 16 * NP2)

            def first_half(i, h, first):
                pool.wait_ge(idx_staged, 2 * i + h + 1)
                if not first:
                    pool.wait_ge(stashed[h], i * 16)
                    pool.wait_ge(a_kept, 2 * i + h - 1)
                hold(2 * i + h + 1)
                for s in range(8 * h, 8 * h + 8):
                    gather(s, h_table, first_rows[:, s, :])

            for h in range(2):
                first_half(0, h, True)
            with pool.Fori(1, GNN.steps // U) as i:
                for h in range(2):
                    first_half(i, h, False)
            slots_used[0] += GNN.steps // U

            for s in range(2):
                pool.wait_ge(rows_out[s], 16 * 2 * NP2)
            pool.wait_ge(x1_out, 16 * 7)
            pool.wait_ge(xn_ready, 2 * TILES)
            pool.memset(R1[:, GATE.steps * GW_IN:], 0.0)
            gather_resident(GATE, gate_table, FI.bitcast(I32),
                            lambda h: gate_slots[:, 8 * h:8 * h + 8, :],
                            lambda i, h: G[:, bass.ds(i * U + 8 * h, 8), :])

        @block.scalar
        def _(act):
            act.wait_ge(stat_ready, 1)
            act.activation(rstd[:, :], stat[:, :, 1], ACT.Sqrt, bias=eps[:, :]).then_inc(std_ready, 1)

            for k in range(4):
                act.wait_ge(prep_turned, 4)
                act.copy(proj[:, k % 2, (k // 2) * P:(k // 2 + 1) * P], ps[:, 2048 + k * P:2048 + (k + 1) * P]).then_inc(prep_copied, 1)
            act.wait_ge(prep_turned, 5)
            for kd in range(2):
                act.copy(proj[:, kd, D:D + 2], ps[:, 2560 + 2 * kd:2562 + 2 * kd]).then_inc(prep_copied, 1)
            act.copy(bias_row[0:1, D:D + 2], ps[0:1, 3072:3074]).then_inc(prep_copied, 1)

            def node_linear(phase, src):
                base, width = phase * TILES, (258, GW_IN)[phase]
                act.wait_ge(std_ready, 2 + 2 * phase)

                def pair(i, first):
                    for s in range(2):
                        t = i * 2 + s
                        if not first:
                            act.wait_ge(xn_turned, base + t - 1)
                        act.activation(xn[s], src(t), ACT.Identity, bias=shift[:, bass.ds(t, 1)],
                                       scale=rstd[:, bass.ds(t, 1)]).then_inc(xn_ready, 1)
                    for s in range(2):
                        t = i * 2 + s
                        act.wait_ge(xn_turned, base + t + 1)
                        if not first:
                            act.wait_ge(lin_ready, base + t - 1)
                            if phase:
                                act.wait_ge(xT_out[s], i * 16)
                        act.copy(xT[s], psT[s]).then_inc(xT_ready, 1)
                    for s in range(2):
                        t = i * 2 + s
                        act.wait_ge(lin_ready, base + t + 1)
                        if not first:
                            act.wait_ge(rows_out[s], (phase * NP2 + i) * 16)
                        act.copy(lin[s][:, 0:width], psL[s][:, 0:width]).then_inc(lin_copied, 1)

                pair(0, True)
                with act.Fori(1, NP2) as i:
                    pair(i, False)

            node_linear(0, lambda t: XR[:, bass.ds(t, 1), :].rearrange("p o d -> p (o d)"))

            act.wait_ge(idx_ready, 1)

            def stage(i, h):
                act.copy(idx_slots[:, 8 * h:8 * h + 8], GI.bitcast(I32)[:, bass.ds(i * U + 8 * h, 8)]).then_inc(idx_staged, 1)

            def keep_a(i, h):
                for s in range(8 * h, 8 * h + 8):
                    act.wait_ge(landed[s], (i + 1) * 16)
                act.copy(a12[:, bass.ds(i * U + 8 * h, 8), :], first_rows[:, 8 * h:8 * h + 8, D:ROW]).then_inc(a_kept, 1)

            for h in range(2):
                stage(0, h)
            with act.Fori(0, GNN.steps // U - 1) as i:
                for h in range(2):
                    keep_a(i, h)
                    stage(i + 1, h)
            for h in range(2):
                keep_a(GNN.steps // U - 1, h)

            act.wait_ge(exp_ready, 1)
            act.activation(g_scan[12], g_scan[11], ACT.Exp).then_inc(exp_done, 1)

            act.wait_ge(stat_ready, 2)
            act.activation(rstd[:, :], stat[:, :, 1], ACT.Sqrt, bias=eps[:, :]).then_inc(std_ready, 1)
            node_linear(1, lambda t: ACC[:, bass.ds(t, 1), 0:D].rearrange("p o d -> p (o d)"))

            act.wait_ge(weights_in, 16 * 5)
            act.preload_act_table(ACT.Gelu)

            def gelu(n, e, first):
                if not first:
                    act.wait_ge(y_ready, n - 1)
                for f in range(4):
                    act.wait_ge(hid_ready, n * 4 + (f | 1) + 1)
                    act.activation(hidT[:, e % 2, f, :], ps[:, (e % 2) * 1024 + f * 256:(e % 2) * 1024 + (f + 1) * 256],
                                   ACT.Gelu, bias=b1_cols[:, 4 * e + f:4 * e + f + 1]).then_inc(gelu_done, 1)

            for e in range(EXPERTS):
                gelu(e, e, e < 2)
            with act.Fori(1, GROUPS) as g:
                for e in range(EXPERTS):
                    gelu(g * EXPERTS + e, e, False)

            for hd in range(HEADS):
                act.wait_ge(exp_ready, 2 + hd)
                act.activation(f_scan[10], f_scan[9], ACT.Exp).then_inc(exp_done, 1)

            def keep_sums(i):
                act.wait_ge(agg_ready, (i + 1) * U)
                act.copy(G[:, bass.ds(i * U, U), 0:20],
                         ps[:, 0:U * 20].rearrange("p (s w) -> p s w", w=20)).then_inc(agg_done, 1)

            with act.Fori(0, GATE.steps // U) as i:
                keep_sums(i)

            act.wait_ge(exp_ready, 6)
            act.activation(mu, var, ACT.Sqrt, bias=eps[:, :]).then_inc(exp_done, 1)
            act.wait_ge(exp_ready, 7)
            act.activation(gates, scores, ACT.Exp).then_inc(exp_done, 1)

            def store(t, s, rows=P):
                act.wait_ge(fin_ready, t + 1)
                o = out[bass.ds(t * P, P), :] if rows == P else out[(TILES - 1) * P:, :]
                act.dma_start(o, mixed[0:rows, s, :]).then_inc(fin_out[s], 16)

            with act.Fori(0, 24) as i:
                for s in range(4):
                    store(4 * i + s, s)
            store(96, 0)
            store(97, 1, LAST)
            for s in range(4):
                act.wait_ge(fin_out[s], 16 * (25 if s < 2 else 24))

        @block.vector
        def _(dve):
            done, ask = Tally(dve_done), Tally(to_turn)

            def link(ins, tally=None):
                tally = tally or done
                dve.wait_ge(tally.sem, tally.add(ins))

            back = [0]

            def answer(n=1):
                back[0] += n
                dve.wait_ge(turned, back[0])

            dve.memset(eps[:, :], EPS).then_inc(dve_done, 1)
            dve.memset(ones_row[:, :], 1.0).then_inc(dve_done, 1)
            done.local = 2
            dve.wait_ge(consts_in, 64)

            for c in range(7):
                dve.wait_ge(x_in[c], 16 if c < 6 else 32)
                with loop(dve, 2, (done, 7)) as i:
                    for s in range(7):
                        t = 14 * c + 7 * i + s
                        done.add(dve.bn_stats(bn[:, bass.ds(t, 1), :].rearrange("p o s -> p (o s)"),
                                              XR[:, bass.ds(t, 1), :].rearrange("p o d -> p (o d)")))
            dve.wait_ge(dve_done, done.n)

            def statistics():
                mean, var_ = stat[:, :, 0], stat[:, :, 1]
                link(dve.tensor_tensor(var_, bn[:, :, 1], bn[:, :, 4], ALU.subtract))
                link(dve.tensor_tensor(mean, bn[:, :, 1], bn[:, :, 4], ALU.add))
                link(dve.tensor_scalar(mean, mean, 0.5, None, ALU.mult))
                link(dve.tensor_tensor(var_, var_, var_, ALU.mult))
                link(dve.tensor_tensor(bn[:, :, 2], bn[:, :, 2], bn[:, :, 5], ALU.add))
                link(dve.tensor_scalar(bn[:, :, 2], bn[:, :, 2], 1.0 / D, None, ALU.mult))
                link(dve.scalar_tensor_tensor(var_, var_, 0.25, bn[:, :, 2], ALU.mult, ALU.add))

            def scales(std_count):
                dve.wait_ge(std_ready, std_count)
                link(dve.reciprocal(rstd[:, :], rstd[:, :]))
                dve.scalar_tensor_tensor(shift[:, :], stat[:, :, 0], -1.0, rstd[:, :], ALU.mult, ALU.mult).then_inc(std_ready, 1)

            statistics()
            dve.engine_nop().then_inc(stat_ready, 1)
            scales(1)
            dve.wait_ge(prep_copied, 7)
            dve.wait_ge(w_in, 16 * 7)
            dve.tensor_add(bias_row[0:1, D:D + 2], bias_row[0:1, D:D + 2], ba).then_inc(proj_ready, 1)

            def sort(g):
                cur = [0]
                n = g.edges // (HEADER_PARTS if g is GNN else P)
                parts = HEADER_PARTS if g is GNN else P
                r, c = (sort_bufs[i].bitcast(I32) for i in range(2))
                link(dve.tensor_scalar(c[0:parts, 0:n], c[0:parts, 0:n], 1, None, ALU.add))
                link(dve.tensor_scalar(r, r, 14, TAG, ALU.logical_shift_left, ALU.bitwise_or))
                link(dve.tensor_tensor(r, r, c, ALU.bitwise_or))

                def stage(j, tally=None):
                    (lo, hi), (olo, ohi) = halves(sort_bufs[cur[0]], j), halves(sort_bufs[1 - cur[0]], j)
                    done.add(dve.tensor_tensor(olo, lo, hi, ALU.min))
                    link(dve.tensor_tensor(ohi, lo, hi, ALU.max), tally)
                    cur[0] = 1 - cur[0]

                def directed_stage(j, k):
                    split = dict(d=2, m=1 << (k - 1 - j), b=2, l=1 << j)
                    va, vb = (sort_bufs[x].rearrange("p (h d m b l) -> p h d m b l", **split)
                              for x in (cur[0], 1 - cur[0]))
                    for d in range(2):
                        lo, hi = va[:, :, d, :, 0, :], va[:, :, d, :, 1, :]
                        done.add(dve.tensor_tensor(vb[:, :, d, :, d, :], lo, hi, ALU.min))
                        done.add(dve.tensor_tensor(vb[:, :, d, :, 1 - d, :], lo, hi, ALU.max))
                    dve.wait_ge(dve_done, done.n)
                    cur[0] = 1 - cur[0]

                def flip(k, tally=None):
                    link(dve.tensor_scalar(sort_bufs[1 - cur[0]], sort_bufs[cur[0]], signs[:, k - 11:k - 10],
                                           None, ALU.mult), tally)
                    cur[0] = 1 - cur[0]

                for k in range(1, 11):
                    for j in range(k - 1, -1, -1):
                        directed_stage(j, k)
                flip(11)
                for j in range(10, -1, -1):
                    stage(j)
                for k in range(12, 19):
                    flip(k, ask)
                    m = k - 12
                    for h in range(2):
                        answer()
                        lo, hi = halves(ps[:, h * 1024:(h + 1) * 1024], m)
                        olo, ohi = halves(sort_bufs[1 - cur[0]][:, h * 1024:(h + 1) * 1024], m)
                        sv = spare[:, h * 512:(h + 1) * 512].rearrange("p (x l) -> p x l", l=1 << m)
                        link(dve.tensor_copy(sv, hi))
                        done.add(dve.tensor_tensor(olo, lo, sv, ALU.min))
                        link(dve.tensor_tensor(ohi, lo, sv, ALU.max), ask if m == 0 and h else None)
                    cur[0] = 1 - cur[0]
                    for mm in range(m - 1, -1, -1):
                        stage(mm, None if mm else ask)
                    answer(2)
                    o = sort_bufs[1 - cur[0]]
                    link(dve.tensor_copy(spare, ps[:, 1024:2048]))
                    done.add(dve.tensor_tensor(o[:, 0:1024], ps[:, 0:1024], spare, ALU.min))
                    link(dve.tensor_tensor(o[:, 1024:2048], ps[:, 0:1024], spare, ALU.max))
                    cur[0] = 1 - cur[0]
                    for j in range(9, -1, -1):
                        stage(j, ask if k == 18 and j == 0 else None)
                answer(2)

            def spread(g, keys):
                link(dve.memset(keys, 0.0))
                n = g.cols // 16
                link(dve.tensor_copy(keys[:, 0:g.cols].rearrange("p (q c) -> p c q", c=16),
                                     ps[:, 0:2048].rearrange("p (c q) -> p c q", c=16)[:, :, 0:n]))
                bufs = [E[:, i * g.q:(i + 1) * g.q].bitcast(I32) for i in range(4)]
                cu, at = keys.bitcast(I32), -1
                for bit in range(6, -1, -1):
                    by = 1 << bit
                    mask, moving = bufs[0], bufs[1]
                    at = 2 if at != 2 else 3
                    new = bufs[at]
                    link(dve.tensor_scalar(mask, cu, 31 - 21 - bit, 31, ALU.logical_shift_left, ALU.arith_shift_right))
                    link(dve.tensor_tensor(moving, cu, mask, ALU.bitwise_and))
                    link(dve.tensor_tensor(new, cu, moving, ALU.bitwise_xor))
                    o = new if bit else keys.bitcast(I32)
                    if not bit:
                        link(dve.tensor_copy(o[:, 0:by], new[:, 0:by]))
                    link(dve.tensor_tensor(o[:, by:], new[:, by:], moving[:, :-by], ALU.bitwise_or))
                    cu = o

            dve.wait_ge(filled, 4)
            dve.wait_ge(keys_in, 48)
            sort(GNN)
            spread(GNN, KS)

            def gather_index(g, keys, dest, scratch, last):
                k_int = keys.bitcast(I32)
                e0, e1, e2 = (scratch[:, i * g.q:(i + 1) * g.q].bitcast(I32) for i in range(3))
                link(dve.tensor_scalar(e0, k_int, LOW, None, ALU.bitwise_and))
                link(dve.tensor_scalar(e1, k_int, 14, LOW, ALU.logical_shift_right, ALU.bitwise_and))
                link(dve.tensor_scalar(e2, e0, 0, None, ALU.is_equal))
                link(dve.tensor_scalar(e1, e1, 1, None, ALU.add))
                link(dve.tensor_tensor(e1, e1, e2, ALU.mult))
                link(dve.tensor_tensor(e0, e0, e1, ALU.add))
                last(dve.tensor_scalar(dest.bitcast(I32), e0, -1, 0, ALU.add, ALU.max))

            for s in range(2):
                dve.wait_ge(rows_out[s], 16 * NP2)
            gather_index(GNN, KS, GI, E, lambda ins: ins.then_inc(idx_ready, 1))
            link(dve.memset(a12[:, GNN.steps:, :], 0.0))

            r, c = (sort_bufs[i].bitcast(I32) for i in range(2))
            link(dve.memset(r, PAD_ROW))
            link(dve.memset(c, 1))
            dve.memset(c[0:HEADER_PARTS, 1024:1024 + HEADERS], 0).then_inc(filled, 4)
            dve.wait_ge(filled, 8)
            dve.wait_ge(keys_in, 96)
            sort(GATE)
            spread(GATE, FK[:, :])
            gather_index(GATE, FK[:, :], FI[:, :], E, link)

            dve.wait_ge(gate_w_in, 48)
            for w in range(2):
                link(dve.tensor_tensor(att_prod[:, :, :], gate_w[:, :, 0:HE], att[:, w:w + 1, :].broadcast_to([P, 2, HE]), ALU.mult))
                link(dve.tensor_reduce(gate_w[:, :, HE + 4 * w:HE + 4 * w + 4],
                                       att_prod[:, :, :].rearrange("p k (h e) -> p k h e", e=EXPERTS), AX.X, ALU.add))
            dve.engine_nop().then_inc(gate_w_ready, 1)

            def to_scan(g, dest, source=None):
                answer()
                link(dve.tensor_copy(dest, ps[:, 0:g.q]))

            def seg_scan(res, d0, d1, op0, op1, neutral, reverse=False):
                v = (lambda z: z[:, ::-1]) if reverse else (lambda z: z)
                end = 0 if reverse else res.shape[1] - 1
                link(dve.tensor_tensor_scan(v(res), v(d0), v(d1), neutral, op0, op1))
                link(dve.tensor_reduce(col[:, 1:2], d0, AX.X, ALU.min))
                link(dve.tensor_copy(col[:, 0:1], res[:, end:end + 1]), ask)
                answer()
                link(dve.tensor_copy(row[:, :], ps[0:1, 0:2 * P]))
                start = P if reverse else 0
                link(dve.memset(carry[0:1, start:start + 1], neutral))
                o = carry[0:1, 0:P] if reverse else carry[0:1, 1:P + 1]
                link(dve.tensor_tensor_scan(v(o), v(row[:, P:2 * P]), v(row[:, 0:P]), neutral, op0, op1), ask)
                answer()
                link(dve.tensor_copy(ccol[:, :], ps[:, 0:1]))
                link(dve.tensor_tensor_scan(v(res), v(d0), v(d1), ccol[:, :], op0, op1))

            def next_first(dest, flags, after):
                n = flags.shape[1]
                link(dve.tensor_scalar(dest[:, 0:n - 1], flags[:, 1:n], -BIG, None, ALU.mult))
                link(dve.tensor_copy(col[:, 0:1], flags[:, 0:1]), ask)
                answer()
                link(dve.memset(carry[0:1, P - 1:P], after))
                link(dve.tensor_copy(carry[0:1, 0:P - 1], ps[0:1, 1:P]), ask)
                answer()
                link(dve.tensor_scalar(dest[:, n - 1:n], ps[:, 0:1], -BIG, None, ALU.mult))

            def block_of_steps(g, keys_f, dest, tmp):
                link(dve.tensor_reduce(tmp[:, 0:g.jj], keys_f.rearrange("p (j n) -> p j n", n=P), AX.X, ALU.max))
                link(dve.tensor_scalar(tmp[:, 0:g.jj].bitcast(I32), tmp[:, 0:g.jj].bitcast(I32), 21, 127,
                                       ALU.logical_shift_right, ALU.bitwise_and))
                dve.tensor_scalar(dest[:, 0:g.jj].bitcast(I32), tmp[:, 0:g.jj].bitcast(I32), TILES - 1, None,
                                  ALU.min).then_inc(blocks_ready, 1)

            def marks_of(g, kf, tmp, head, edge, reset, nhead, reset_next):
                link(dve.tensor_scalar(tmp.bitcast(I32), kf.bitcast(I32), TAG | LOW, None, ALU.bitwise_and))
                link(dve.tensor_scalar(head, tmp, TAG_FLOAT, None, ALU.is_equal))
                link(dve.tensor_scalar(edge, tmp, TAG_FLOAT, None, ALU.is_gt if g is GNN else ALU.is_ge))
                link(dve.tensor_scalar(reset, head, -BIG, None, ALU.mult))
                link(dve.tensor_scalar(nhead, head, -1.0, 1.0, ALU.mult, ALU.add))
                next_first(reset_next, head, 1.0)

            KF, HD, ED, RS, RN, NH, VF, VF2, V2, MF, MB, T1, T2 = g_scan[0:13]
            dve.wait_ge(a_kept, GNN_KEPT)
            for h in range(2):
                dve.wait_ge(stashed[h], 16 * (GNN.steps // U))
            link(dve.engine_nop(), ask)
            to_scan(GNN, KF)
            marks_of(GNN, KF, T1, HD, ED, RS, NH, RN)
            block_of_steps(GNN, KF, MF, MB)
            link(dve.tensor_scalar(T1.bitcast(I32), KS.bitcast(I32), 14, 127, ALU.logical_shift_right, ALU.bitwise_and))
            link(dve.tensor_copy(GR, T1.bitcast(I32)))
            link(dve.memset(gbuf[0][:, :, D], 1.0))
            dve.wait_ge(blocks_out, 16)
            link(dve.engine_nop(), ask)
            to_scan(GNN, VF)
            link(dve.engine_nop(), ask)
            to_scan(GNN, VF2)

            def attention(slope, head_v, edge, reset, nhead, reset_next, a_dst_in, a_src_in,
                          adst, v2, mf, mb, t1, out_exp, count):
                link(dve.tensor_tensor(t1, head_v, a_dst_in, ALU.mult))
                seg_scan(adst, nhead, t1, ALU.mult, ALU.add, 0.0)
                link(dve.tensor_scalar(v2, edge, 1.0, BIG, ALU.subtract, ALU.mult))
                link(dve.tensor_tensor(t1, a_src_in, edge, ALU.mult))
                link(dve.tensor_tensor(v2, v2, t1, ALU.add))
                seg_scan(mf, reset, v2, ALU.add, ALU.max, -BIG)
                seg_scan(mb, reset_next, mf, ALU.add, ALU.max, -BIG, reverse=True)
                link(dve.tensor_tensor(mb, mb, adst, ALU.add))
                link(dve.scalar_tensor_tensor(mf, mb, slope, mb, ALU.mult, ALU.max))
                link(dve.tensor_tensor(v2, v2, adst, ALU.add))
                link(dve.scalar_tensor_tensor(mb, v2, slope, v2, ALU.mult, ALU.max))
                dve.tensor_tensor(t1, mb, mf, ALU.subtract).then_inc(exp_ready, 1)
                dve.wait_ge(exp_done, count)
                link(dve.tensor_tensor(out_exp, out_exp, edge, ALU.mult), ask)

            attention(0.01, HD, ED, RS, NH, RN, VF, VF2, VF, V2, MF, MB, T1, T2, 1)
            answer()
            link(dve.tensor_copy(KS.rearrange("p (k j) -> p j k", j=GNN.jj),
                                 ps[:, 0:GNN.q].rearrange("p (j k) -> p j k", k=P)))

            link(dve.memset(gbuf[1][:, :, D], 1.0))
            dve.engine_nop().then_inc(ones_set, 1)
            link(dve.memset(R1[:, 0:TILES * 257], 0.0))
            hots, adds = Tally(hot_ready), Tally(added)
            adds.add(dve.memset(col[:, 0:1], 0.0), 8)
            dve.wait_ge(blocks_in, 16)

            def one_hots(half_first, h, weights=True):
                for s in range(8 * h, 8 * h + 8):
                    q = half_first + s - 8 * h
                    hots.add(dve.tensor_scalar(hot[:, s, :], iota_row[:, :], GR[:, bass.ds(q, 1)],
                                               KS[:, bass.ds(q, 1)], ALU.is_equal, ALU.mult))

            one_hots(0, 0)
            turns = GNN.steps // U
            with loop(dve, turns, (hots, U), (adds, U)) as i:
                _, blocks = nc.values_load_multi_w_load_instructions(
                    blk_row.bitcast(I32)[0:1, bass.ds(i * U, U)],
                    engines=[mybir.EngineType.DVE], min_val=0, max_val=TILES - 1,
                    skip_runtime_bounds_check_because="block_of_steps masks and clamps each to 0..TILES - 1")
                for h in range(2):
                    one_hots(i * U + 8 * (h + 1), 1 - h)
                    for s in range(8):
                        b = blocks[8 * h + s]
                        dve.wait_ge(summed, i * U + 8 * h + s + 1)
                        target = R1[:, bass.ds(b * 257, 257)]
                        dve.wait_ge(added, adds.add(dve.tensor_tensor(
                            target, target, ps[:, s * 512:s * 512 + 257], ALU.add)))

            rden = E[:, 3970:3970 + TILES]
            link(dve.tensor_scalar(rden, ACC[:, :, D], 1e-30, None, ALU.max))
            link(dve.reciprocal(rden, rden))
            used = Tally(xg_used)

            def residual(i, s):
                dve.wait_ge(xg_in[s], (i + 1) * 16)
                tiles = [14 * i + 7 * s + z for z in range(7)]
                x1 = [ACC[:, bass.ds(t, 1), 0:D].rearrange("p o d -> p (o d)") for t in tiles]
                for z, t in enumerate(tiles):
                    done.add(dve.scalar_tensor_tensor(x1[z], x1[z], rden[:, bass.ds(t, 1)], xin[s][:, z, :], ALU.mult, ALU.add))
                dve.wait_ge(dve_done, done.n)
                used.add(dve.memset(col[:, 0:1], 0.0))
                for z, t in enumerate(tiles):
                    done.add(dve.bn_stats(bn[:, bass.ds(t, 1), :].rearrange("p o s -> p (o s)"), x1[z]))

            with loop(dve, 6, (done, 28), (used, 2)) as i:
                for s in range(2):
                    residual(i, s)
            residual(6, 0)
            dve.wait_ge(xg_last, 16)
            residual(6, 1)
            dve.wait_ge(dve_done, done.n)
            statistics()
            dve.engine_nop().then_inc(stat_ready, 1)
            scales(3)

            dve.wait_ge(weights_in, 16 * 5)
            ys = Tally(y_copied)

            def y_copy(n, e, s):
                dve.wait_ge(y_ready, n + 1)
                ys.add(dve.tensor_tensor(ystage[:, s, :, e, :],
                                         ps[:, 2048 + e * 512:2560 + e * 512].rearrange("p (t d) -> p t d", t=2),
                                         b2_all[:, e:e + 1, :].broadcast_to([P, 2, D]), ALU.add))

            for g in range(2):
                for e in range(EXPERTS):
                    y_copy(g * EXPERTS + e, e, g)
            with loop(dve, GROUPS // 2 - 1, (ys, 8)) as i:
                for s in range(2):
                    dve.wait_ge(y_out[s], 16 * (i + 1))
                    for e in range(EXPERTS):
                        y_copy((2 * i + 2 + s) * EXPERTS + e, e, s)
            dve.wait_ge(y_out[0], 16 * (GROUPS // 2))
            for e in range(EXPERTS):
                y_copy((GROUPS - 1) * EXPERTS + e, e, 0)

            fKF, fH, fE, fRS, fRN, fNH, fVS, fVD, fV2, fT1, fX, fMF, fMB = f_scan
            dve.wait_ge(rows_kept, GATE_KEPT)
            for s in range(2):
                dve.wait_ge(y_out[s], 16 * (GROUPS // 2 + (1 - s)))
            link(dve.engine_nop(), ask)
            to_scan(GATE, fKF)
            marks_of(GATE, fKF, fT1, fH, fE, fRS, fNH, fRN)
            block_of_steps(GATE, fKF, fMF, fMB)
            link(dve.tensor_scalar(FI[:, :].bitcast(I32), FK[:, :].bitcast(I32), 14, 127,
                                   ALU.logical_shift_right, ALU.bitwise_and))
            link(dve.tensor_copy(FK[:, :], FI[:, :].bitcast(I32)))
            dve.wait_ge(gate_in, 32)
            link(dve.tensor_copy(fMF[0:1, :], fMB[0:1, :].bitcast(I32)))
            link(dve.tensor_tensor_scan(fMB[0:1, :], fMF[0:1, :], fMF[0:1, :], 0.0, ALU.max, ALU.max))
            link(dve.tensor_copy(fMF[0:1, :], fMB[0:1, :]))
            dve.engine_nop().then_inc(blocks_ready, 1)
            dve.wait_ge(gate_in, 48)
            link(dve.engine_nop(), ask)
            for hd in range(HEADS):
                to_scan(GATE, fVS)
                link(dve.engine_nop(), ask)
                to_scan(GATE, fVD)
                attention(0.2, fH, fE, fRS, fNH, fRN, fVD, fVS, fVD, fV2, fMF, fMB, fT1, fX, 2 + hd)
                answer()
                link(dve.tensor_copy(G[:, :, HE + hd].rearrange("p (k j) -> p j k", j=GATE.jj),
                                     ps[:, 0:GATE.q].rearrange("p (j k) -> p j k", k=P)),
                     ask if hd < HEADS - 1 else None)
            for hd in range(HEADS):
                part = G[:, :, hd * 4:hd * 4 + 4]
                link(dve.tensor_tensor(part, part, G[:, :, HE + hd:HE + hd + 1].broadcast_to([P, GATE.q, 4]), ALU.mult))

            dve.engine_nop().then_inc(blocks_ready, 1)
            dve.wait_ge(gate_in, 64)
            n = GATE.steps
            link(dve.memset(keep[:, 0:1], 0.0))
            link(dve.tensor_tensor(keep[:, 1:n], block_rows[:, 1:n], block_rows[:, 0:n - 1], ALU.is_equal))
            upto = f_scan[10][:, 0:n]
            link(dve.tensor_scalar(upto, block_rows[:, 0:n], part_id[:, :], None, ALU.is_le))
            link(dve.tensor_reduce(ccol[:, :], upto, AX.X, ALU.add))
            link(dve.tensor_scalar(last_col[:, :], ccol[:, :], -1.0, None, ALU.add))
            dve.engine_nop().then_inc(blocks_ready, 1)

            hots2 = Tally(hot_ready, hots.n)

            def plain_hots(i, h):
                for s in range(8 * h, 8 * h + 8):
                    hots2.add(dve.tensor_scalar(hot[:, s, :], iota_row[:, :], FK[:, bass.ds(i * U + s, 1)],
                                                None, ALU.is_equal))

            plain_hots(0, 0)
            plain_hots(0, 1)
            with loop(dve, GATE.steps // U - 1, (hots2, U)) as i:
                for h in range(2):
                    dve.wait_ge(agg_ready, i * U + 8 * h + 8)
                    plain_hots(i + 1, h)
            dve.wait_ge(agg_done, GATE.steps // U)
            for w in range(20):
                ch = G[:, 0:GATE.steps, w]
                link(dve.tensor_tensor_scan(ch, keep[:, 0:GATE.steps], ch, 0.0, ALU.mult, ALU.add))
            dve.wait_ge(gate_in, 96)
            with loop(dve, TILES // 7, (done, 7)) as i:
                _, lasts = nc.values_load_multi_w_load_instructions(
                    last_row[0:1, bass.ds(i * 7, 7)], engines=[mybir.EngineType.DVE],
                    min_val=0, max_val=GATE.steps - 1)
                for s in range(7):
                    done.add(dve.tensor_copy(sums[:, bass.ds((i * 7 + s), 1), :].rearrange("p o w -> p (o w)"),
                                             R1[:, bass.ds(lasts[s] * GW_IN, 20)]))
            dve.wait_ge(dve_done, done.n)
            dve.wait_ge(gates_need, 48)

            link(dve.tensor_scalar(den, sums[:, :, HE:HE + 4], 1e-16, None, ALU.add))
            link(dve.reciprocal(den, den))
            for hd in range(HEADS):
                link(dve.tensor_tensor(agg[:, :, hd * 4:hd * 4 + 4], sums[:, :, hd * 4:hd * 4 + 4],
                                       den[:, :, hd:hd + 1].broadcast_to([P, TILES, 4]), ALU.mult))

            def per_score(v):
                return v.rearrange("p (o n) -> p o n", o=1).broadcast_to([P, TILES, HE])

            link(dve.tensor_tensor(agg, agg, per_score(gat_bias), ALU.add))
            link(dve.tensor_reduce(mu, agg, AX.X, ALU.add))
            link(dve.tensor_scalar(mu, mu, 1.0 / HE, None, ALU.mult))
            mu3 = mu.rearrange("p (t o) -> p t o", o=1).broadcast_to([P, TILES, HE])
            link(dve.tensor_tensor(agg, agg, mu3, ALU.subtract))
            link(dve.tensor_tensor(squares, agg, agg, ALU.mult))
            link(dve.tensor_reduce(var, squares, AX.X, ALU.add))
            dve.tensor_scalar(var, var, 1.0 / HE, None, ALU.mult).then_inc(exp_ready, 1)
            dve.wait_ge(exp_done, 6)
            link(dve.reciprocal(mu, mu))
            link(dve.tensor_tensor(agg, agg, mu3, ALU.mult))
            link(dve.tensor_tensor(agg, agg, per_score(gamma), ALU.mult))
            link(dve.tensor_tensor(agg, agg, per_score(beta), ALU.add))
            link(dve.tensor_reduce(scores, agg.rearrange("p t (h e) -> p t e h", e=EXPERTS), AX.X, ALU.add))
            link(dve.tensor_scalar(scores, scores, 1.0 / HEADS, None, ALU.mult))
            link(dve.memset(beaten, 0.0))
            for i in range(EXPERTS):
                for j in range(i + 1, EXPERTS):
                    link(dve.tensor_tensor(var, scores[:, :, i], scores[:, :, j], ALU.is_ge))
                    link(dve.tensor_tensor(beaten[:, :, j], beaten[:, :, j], var, ALU.add))
                    link(dve.tensor_scalar(var, var, -1.0, 1.0, ALU.mult, ALU.add))
                    link(dve.tensor_tensor(beaten[:, :, i], beaten[:, :, i], var, ALU.add))
            link(dve.tensor_reduce(mu, scores, AX.X, ALU.max))
            mu4 = mu.rearrange("p (t o) -> p t o", o=1).broadcast_to([P, TILES, EXPERTS])
            dve.tensor_tensor(scores, scores, mu4, ALU.subtract).then_inc(exp_ready, 1)
            link(dve.tensor_scalar(beaten, beaten, 1.5, None, ALU.is_lt))
            dve.wait_ge(exp_done, 7)
            link(dve.tensor_tensor(beaten, beaten, gates, ALU.mult))
            link(dve.tensor_reduce(mu, beaten, AX.X, ALU.add))
            link(dve.reciprocal(mu, mu))
            link(dve.tensor_tensor(gates, beaten, mu4, ALU.mult))
            dve.engine_nop().then_inc(blocks_ready, 1)

            fins = Tally(fin_ready)

            def mix(t, s, n):
                dve.wait_ge(fin_in[s], 32 * n)
                for e in range(EXPERTS):
                    o = dve.scalar_tensor_tensor(mixed[:, s, :], yin[:, s, e * D:(e + 1) * D],
                                                 gates[:, bass.ds(t, 1), e:e + 1].rearrange("p o e -> p (o e)"),
                                                 x1in[:, s, :] if e == 0 else mixed[:, s, :], ALU.mult, ALU.add)
                    if e < EXPERTS - 1:
                        link(o)
                    else:
                        fins.add(o)

            with loop(dve, 24, (done, 12), (fins, 4)) as i:
                for s in range(4):
                    mix(4 * i + s, s, i + 1)
            for s in range(2):
                mix(96 + s, s, 25)

        @block.tensor
        def _(pe):
            asked = [0]

            def asked_for():
                asked[0] += 1
                pe.wait_ge(to_turn, asked[0])

            pe.wait_ge(consts_in, 64)
            pe.wait_ge(w_in, 16 * 7)
            pe.wait_ge(dve_done, 2)
            for k in range(4):
                kd, kn = k % 2, k // 2
                pe.transpose(ps[:, 2048 + k * P:2048 + (k + 1) * P], w_nat[:, kn, kd * P:(kd + 1) * P],
                             ident[:, :]).then_inc(prep_turned, 1)
            for kd in range(2):
                for kn in range(2):
                    pe.matmul(ps[:, 2560 + 2 * kd:2562 + 2 * kd], w_nat[:, kn, kd * P:(kd + 1) * P], wa[:, kn, :],
                              start=kn == 0, stop=kn == 1)
            for kn in range(2):
                ins = pe.matmul(ps[0:1, 3072:3074], bcol[:, kn:kn + 1], wa[:, kn, :], start=kn == 0, stop=kn == 1)
            ins.then_inc(prep_turned, 1)
            pe.wait_ge(proj_ready, 1)

            def node_linear(phase):
                base, width = phase * TILES, (258, GW_IN)[phase]
                weights = (proj, gate_w)[phase]

                def pair(i, first):
                    for s in range(2):
                        t = i * 2 + s
                        pe.wait_ge(xn_ready, base + t + 1)
                        if not first:
                            pe.wait_ge(xT_ready, base + t - 1)
                        for k in range(2):
                            ins = pe.transpose(psT[s][:, k * P:(k + 1) * P], xn[s][:, k * P:(k + 1) * P], ident[:, :])
                        ins.then_inc(xn_turned, 1)
                    for s in range(2):
                        t = i * 2 + s
                        pe.wait_ge(xT_ready, base + t + 1)
                        if not first:
                            pe.wait_ge(lin_copied, base + t - 1)
                        for k in range(2):
                            ins = pe.matmul(psL[s][:, 0:width], xT[s][:, k * P:(k + 1) * P], weights[:, k, 0:width],
                                            start=k == 0, stop=phase == 1 and k == 1)
                        if phase == 0:
                            ins = pe.matmul(psL[s], ones_row[:, :], bias_row[:, :], start=False, stop=True)
                        ins.then_inc(lin_ready, 1)

                pair(0, True)
                with pe.Fori(1, NP2) as i:
                    pair(i, False)

            node_linear(0)
            def sort_turns():
                for c in turn_buffers():
                    asked_for()
                    for i in range(16):
                        ins = pe.transpose(ps[:, i * P:(i + 1) * P], sort_bufs[c][:, i * P:(i + 1) * P], ident[:, :])
                        if i in (7, 15):
                            ins.then_inc(turned, 1)

            def turn(source, g):
                asked_for()
                v = source.rearrange("p (k j) -> p j k", j=g.jj)
                for j in range(g.jj):
                    ins = pe.transpose(ps[:, j * P:(j + 1) * P], v[:, j, :], ident[:, :])
                ins.then_inc(turned, 1)

            def turn_back(source, g):
                asked_for()
                for j in range(g.jj):
                    ins = pe.transpose(ps[:, j * P:(j + 1) * P], source[:, j * P:(j + 1) * P], ident[:, :])
                ins.then_inc(turned, 1)

            def carries():
                asked_for()
                pe.transpose(ps[0:1, 0:P], col[:, 0:1], ident[:, :])
                pe.transpose(ps[0:1, P:2 * P], col[:, 1:2], ident[:, :]).then_inc(turned, 1)

            def carry_back(first):
                asked_for()
                pe.transpose(ps[:, 0:1], carry[0:1, first:first + P], ident[0:1, 0:1]).then_inc(turned, 1)

            def first_flags():
                asked_for()
                pe.transpose(ps[0:1, 0:P], col[:, 0:1], ident[:, :]).then_inc(turned, 1)
                carry_back(0)

            def attention_turns():
                carries(); carry_back(0)
                carries(); carry_back(0)
                carries(); carry_back(1)

            sort_turns()
            sort_turns()
            turn(KS, GNN)
            first_flags()
            turn(a12[:, :, 0], GNN)
            turn(a12[:, :, 1], GNN)
            attention_turns()
            turn_back(g_scan[12], GNN)

            with pe.Fori(0, GNN.steps // 32) as i:
                for s in range(32):
                    q = i * 32 + s
                    pe.wait_ge(hot_ready, q + 1)
                    if s % 8 == 0:
                        pe.wait_ge(rows_in[s // 8], (i + 1) * 16)
                    pe.wait_ge(added, q + 1)
                    pe.matmul(ps[:, (s % 8) * 512:(s % 8) * 512 + 257], hot[:, s % U, :], gbuf[s // U][:, s % U, :],
                              start=True, stop=True).then_inc(summed, 1)

            pe.wait_ge(gate_w_ready, 1)
            pe.wait_ge(added, GNN.steps + 8)
            node_linear(1)

            pe.wait_ge(weights_in, 16 * 5)
            pe.wait_ge(lin_copied, 2 * TILES)

            def hidden(n, e, s, first):
                for f in range(4):
                    if not first:
                        pe.wait_ge(gelu_done, (n - 2) * 4 + (f | 1) + 1)
                    for k in range(2):
                        ins = pe.matmul(ps[:, (e % 2) * 1024 + f * 256:(e % 2) * 1024 + (f + 1) * 256],
                                        w1[:, k, e * HID + f * P:e * HID + (f + 1) * P],
                                        xe[:, s, :, k, :], start=k == 0, stop=k == 1)
                    ins.then_inc(hid_ready, 1)

            def outputs(n, e, first):
                pe.wait_ge(gelu_done, (n + 1) * 4)
                if not first:
                    pe.wait_ge(y_copied, n - 3)
                for t in range(2):
                    for f in range(4):
                        ins = pe.matmul(ps[:, 2048 + e * 512 + t * 256:2048 + e * 512 + (t + 1) * 256],
                                        hidT[:, e % 2, f, t * P:(t + 1) * P], w2[:, 4 * e + f, :],
                                        start=f == 0, stop=f == 3)
                ins.then_inc(y_ready, 1)

            def group(g, s, first_group, i=None):
                for e in range(EXPERTS):
                    n = g * EXPERTS + e
                    if e < EXPERTS - 1:
                        hidden(n + 1, e + 1, s, first_group and e + 1 < 2)
                    elif i is not None:
                        pe.wait_ge(xe_in[1 - s], 16 * (i + 1 + s))
                        hidden(n + 1, 0, 1 - s, False)
                    outputs(n, e, first_group)

            pe.wait_ge(xe_in[0], 16)
            hidden(0, 0, 0, True)
            group(0, 0, True, 0)
            group(1, 1, False, 0)
            with pe.Fori(1, GROUPS // 2) as i:
                for s in range(2):
                    group(i * 2 + s, s, False, i)
            group(GROUPS - 1, 0, False)

            turn(FK[:, :], GATE)
            first_flags()
            for hd in range(HEADS):
                turn(G[:, :, HE + hd], GATE)
                turn(G[:, :, HE + 4 + hd], GATE)
                attention_turns()
                turn_back(f_scan[10], GATE)
            with pe.Fori(0, GATE.steps // U) as i:
                for s in range(U):
                    pe.wait_ge(hot_ready, GNN_HOTS + i * U + s + 1)
                    if s == 0:
                        pe.wait_ge(agg_done, i)
                    pe.matmul(ps[:, s * 20:(s + 1) * 20], hot[:, s, :],
                              G[:, bass.ds(i * U + s, 1), 0:20].rearrange("p o w -> p (o w)"),
                              start=True, stop=True).then_inc(agg_ready, 1)


def shape_constants():
    part = np.arange(P)

    def sign(k):
        return np.where((part >> (k - 11)) & 1, -1.0, 1.0)

    signs = np.stack([sign(11)] + [sign(k) * sign(k - 1) for k in range(12, 19)], axis=1)
    return {
        "ident": np.eye(P, dtype=np.float32),
        "iota_row": np.tile(part.astype(np.float32), (P, 1)),
        "signs": signs.astype(np.float32),
        "part_id": part.astype(np.float32)[:, None],
        "headers": np.arange(NODES, dtype=np.int32).reshape(HEADER_PARTS, HEADERS),
    }


def kernel(**inputs):
    import concourse.bacc as bacc
    from concourse.bass_utils import run_bass_kernel_spmd

    nc = bacc.Bacc("TRN2", target_bir_lowering=False, num_devices=1)
    arrays, a, consts = {}, {}, {}
    for full, array in inputs.items():
        name = full.removeprefix("L0_gnn_").removeprefix("L0_ffn_")
        array = np.ascontiguousarray(array)
        arrays[f"in_{name}"] = array
        a[name] = nc.dram_tensor(f"in_{name}", array.shape, mybir.dt.from_np(array.dtype), kind="ExternalInput").ap()
    for name, array in shape_constants().items():
        arrays[f"const_{name}"] = array
        consts[name] = nc.dram_tensor(f"const_{name}", array.shape, mybir.dt.from_np(array.dtype),
                                      kind="ExternalInput").ap()
    out = nc.dram_tensor("out", (NODES, D), FP32, kind="ExternalOutput").ap()
    program(nc, a, out, consts)
    return run_bass_kernel_spmd(nc, [arrays], core_ids=[0]).results[0]["out"]
```

```python
from contextlib import ExitStack, contextmanager

import numpy as np

import concourse.bass as bass
from concourse import mybir

FP32 = mybir.dt.float32
I32 = mybir.dt.int32
ALU = mybir.AluOpType
ACT = mybir.ActivationFunctionType
AX = mybir.AxisListType

P = 128
NODES = 12500
D = 256
TILES = -(-NODES // P)
PADDED = TILES * P
LAST = NODES - (TILES - 1) * P
W = 2048
HEADER_PARTS = 125
HEADERS = NODES // HEADER_PARTS
EXPERTS, HEADS, HID = 4, 4, 512
HE = HEADS * EXPERTS
EPS = 1e-5
BIG = 1e30
TAG = 0x20000000
TAG_FLOAT = float(np.array([TAG], np.int32).view(np.float32)[0])
LOW = (1 << 14) - 1
PAD_ROW = PADDED - 1
GW_IN = 24
ROW = D + 1
U = 16


class Graph:
    def __init__(self, edges, step_unit):
        self.edges = edges
        self.tiles = -(-(edges + NODES) // P)
        self.cols = 16 * -(-self.tiles // 16)
        self.steps = U * -(-(self.tiles + TILES - 1) // U)
        self.jj = -(-(self.cols + TILES) // P)
        self.q = self.jj * P


GNN = Graph(212500, U)
CHUNKS = -(-GNN.steps // P)
LAST_STEPS = GNN.steps - (CHUNKS - 1) * P
CHUNK_ASKS, CHUNK_DONE = 10, 62
EXP_FIRST, EXP_EVERY, EXP_MEANWHILE = 36, 7, 11
GATE = Graph(131072, U)


class Tally:

    def __init__(self, sem, start=0):
        self.sem, self.base, self.local = sem, start, 0
        self.made = 0

    def add(self, ins, k=1):
        ins.then_inc(self.sem, k)
        return self.pass_by(k)

    def pass_by(self, k=1):
        self.local += k
        self.made += k
        return self.n

    @property
    def n(self):
        return self.base + self.local


@contextmanager
def loop(eng, count, *tallies):
    starts, made = [t.n for t, _ in tallies], [t.made for t, _ in tallies]
    with eng.Fori(0, count) as i:
        for (t, per), s in zip(tallies, starts):
            t.base, t.local = s + i * per, 0
        yield i
    for (t, per), s, m in zip(tallies, starts, made):
        assert t.made - m == per, (t.made - m, per)
        t.base, t.local, t.made = s + count * per, 0, m + count * per


def halves(v, j):
    x = v.rearrange("p (x b l) -> p x b l", b=2, l=1 << j)
    return x[:, :, 0, :], x[:, :, 1, :]


def turn_buffers():
    c, order = 0, []
    for k in range(1, 11):
        c = (c + k) % 2
    c = (c + 1 + 11) % 2
    for k in range(12, 19):
        c = (c + 1) % 2
        order.append(c)
        c = (c + 1 + (k - 12)) % 2
        order.append(c)
        c = (c + 1 + 10) % 2
    order.append(c)
    return order


def program(nc, a, out, consts):
    ctx = ExitStack()
    with ctx:
        def sb(name, shape, dt=FP32):
            return ctx.enter_context(nc.sbuf_tensor(name, shape, dt))

        def sem(name):
            return ctx.enter_context(nc.semaphore(name))

        def dram(name, shape, dt=FP32):
            return nc.dram_tensor(name, shape, dt, kind="Internal").ap()

        h_table = dram("h_table", (2 * PADDED, ROW))
        stash = dram("stash", (GNN.steps // 8, P, 8, D))
        x1_rows = dram("x1_rows", (PADDED, D))
        xT_tiles = dram("xT_tiles", (TILES, P, 2 * P))
        gate_table = dram("gate_table", (PADDED, GW_IN))
        y_rows = dram("y_rows", (PADDED, EXPERTS * D))
        gate_blocks = dram("gate_blocks", (P, GATE.jj), I32)
        gate_blocks_f = dram("gate_blocks_f", (1, GATE.q))
        last_steps = dram("last_steps", (TILES, 1), I32)

        R1 = sb("R1", [P, GATE.q * GW_IN])
        WK = sb("WK", [P, 17552])
        FK = sb("FK", [P, GATE.q])
        FI = sb("FI", [P, GATE.q])
        S, E, A = WK[:, 0:4112], WK[:, 4112:11792], WK[:, 11792:17552]
        sort_bufs = [S[:, 0:W], S[:, W:2 * W]]
        spare = E[:, 0:1024]
        XR = R1[:, 0:TILES * D].rearrange("p (t d) -> p t d", d=D)
        ACC = R1[:, 0:TILES * 257].rearrange("p (t d) -> p t d", d=257)
        G = R1[:, :].rearrange("p (q w) -> p q w", w=GW_IN)
        KS = A[:, 0:GNN.q]
        GI, SC = A[:, GNN.q:2 * GNN.q], A[:, 2 * GNN.q:3 * GNN.q]
        ident, iota_row = sb("ident", [P, P]), sb("iota_row", [P, P])
        signs, part_id = sb("signs", [P, 8]), sb("part_id", [P, 1])
        stat = sb("stat", [P, TILES, 2])
        rstd, shift = sb("rstd", [P, TILES]), sb("shift", [P, TILES])
        eps = sb("eps", [P, 1])
        att, att_prod = sb("att", [P, 2, HE]), sb("att_prod", [P, 2, HE])
        gate_w = sb("gate_w", [P, 2, GW_IN])
        idx_slots = sb("idx_slots", [P, U], I32)
        waited = sb("waited", [P, 1 + 2 * GNN.steps // U])
        ones_row = sb("ones_row", [1, P])
        state = sb("state", [1, 4])
        joined, factor = sb("joined", [1, 2]), sb("factor", [P, 4])
        joined_block = sb("joined_block", [1, 1], I32)
        step_blocks = sb("step_blocks", [1, P], I32)
        col, row, carry = sb("col", [P, 2]), sb("row", [1, 2 * P]), sb("carry", [1, P + 1])
        ccol = sb("ccol", [P, 1])
        ps = ctx.enter_context(nc.psum_tensor("ps", [P, 8 * 512], FP32))

        nb = A[:, GNN.q:]
        xn = [nb[:, s * 256:(s + 1) * 256] for s in range(2)]
        xT = [nb[:, 512 + s * 256:768 + s * 256] for s in range(2)]
        lin = [nb[:, 1024 + s * 258:1024 + (s + 1) * 258] for s in range(2)]
        w_nat = nb[:, 1540:2052].rearrange("p (k d) -> p k d", k=2)
        wa = nb[:, 2052:2056].rearrange("p (k w) -> p k w", k=2)
        bcol = nb[:, 2056:2058]
        ba = nb[0:1, 2058:2060]
        proj = nb[:, 2400:2916].rearrange("p (k n) -> p k n", k=2)
        bias_row = nb[0:1, 2916:3174]
        bn = E[:, 1024:1024 + 6 * TILES].rearrange("p (t s) -> p t s", s=6)
        psT = [ps[:, 2048 + s * 512:2048 + s * 512 + 256] for s in range(2)]
        psL = [ps[:, 3072 + s * 512:3072 + s * 512 + 258] for s in range(2)]

        consts_in, w_in = sem("consts_in"), sem("w_in")
        x_in = [sem(f"x_in{c}") for c in range(7)]
        filled, keys_in = sem("filled"), sem("keys_in")
        dve_done, to_turn, turned = sem("dve_done"), sem("to_turn"), sem("turned")
        stat_ready, std_ready = sem("stat_ready"), sem("std_ready")
        prep_turned, prep_copied, proj_ready = sem("prep_turned"), sem("prep_copied"), sem("proj_ready")
        xn_ready, xn_turned, xT_ready = sem("xn_ready"), sem("xn_turned"), sem("xT_ready")
        lin_ready, lin_copied = sem("lin_ready"), sem("lin_copied")
        rows_out = [sem(f"rows_out{s}") for s in range(2)]
        xT_out = [sem(f"xT_out{s}") for s in range(2)]
        stashed = [sem(f"stashed{h}") for h in range(2)]
        rows_in = [sem(f"rows_in{h}") for h in range(4)]
        a_kept = sem("a_kept")
        idx_ready, idx_staged = sem("idx_ready"), sem("idx_staged")
        landed = [sem(f"landed{s}") for s in range(U)]
        rows_kept = sem("rows_kept")
        blocks_ready = sem("blocks_ready")
        hot_ready, summed, added = sem("hot_ready"), sem("summed"), sem("added")
        ones_set = sem("ones_set")
        xg_in = [sem(f"xg_in{s}") for s in range(2)]
        xg_last = sem("xg_last")
        xg_used, x1_ready, x1_out = sem("xg_used"), sem("x1_ready"), sem("x1_out")
        gate_w_in, gate_w_ready = sem("gate_w_in"), sem("gate_w_ready")
        weights_in = sem("weights_in")
        xe_in = [sem(f"xe_in{s}") for s in range(2)]
        hid_ready, gelu_done = sem("hid_ready"), sem("gelu_done")
        y_ready, y_copied = sem("y_ready"), sem("y_copied")
        y_out = [sem(f"y_out{s}") for s in range(2)]
        exp_ready, exp_done = sem("exp_ready"), sem("exp_done")
        agg_ready, agg_done = sem("agg_ready"), sem("agg_done")
        gate_in, gates_need = sem("gate_in"), sem("gates_need")
        fin_in = [sem(f"fin_in{s}") for s in range(4)]
        fin_ready = sem("fin_ready")
        fin_out = [sem(f"fin_out{s}") for s in range(4)]

        block = ctx.enter_context(nc.Block())
        NP2 = TILES // 2
        GATE_KEPT = 2 * GATE.steps // U
        GNN_HOTS = GNN.steps

        f_scan = [WK[:, i * GATE.q:(i + 1) * GATE.q] for i in range(13)]
        R1_FREE = TILES * 257
        first_rows = R1[:, R1_FREE:R1_FREE + U * ROW].rearrange("p (s w) -> p s w", w=ROW)
        gbuf = [v.rearrange("p (s w) -> p s w", w=257) for v in
                (S[:, 0:U * 257], E[:, 2048:2048 + U * 257])]
        hot = E[:, 0:U * P].rearrange("p (s n) -> p s n", n=P)
        c_scan = [R1[:, R1_FREE + U * ROW + i * P:R1_FREE + U * ROW + (i + 1) * P] for i in range(8)]
        c_scan += [E[:, 6160 + i * P:6160 + (i + 1) * P] for i in range(8)]
        c_keys, c_scores, c_rows, c_weights = c_scan[12:16]
        gate_slots = WK[:, 16400:16400 + U * GW_IN].rearrange("p (s w) -> p s w", w=GW_IN)
        xin = [E[:, 4096 + s * 1792:4096 + (s + 1) * 1792].rearrange("p (t d) -> p t d", d=D)
               for s in range(2)]
        w1 = WK[:, 0:4096].rearrange("p (k f) -> p k f", k=2)
        w2 = WK[:, 4096:8192].rearrange("p (c d) -> p c d", d=D)
        hidT = WK[:, 8192:10240].rearrange("p (s f n) -> p s f n", s=2, f=4)
        xe = WK[:, 10240:11264].rearrange("p (s t k n) -> p s t k n", s=2, t=2, k=2)
        ystage = WK[:, 11264:15360].rearrange("p (s t e d) -> p s t e d", s=2, t=2, e=EXPERTS)
        b2_all = WK[:, 15360:16384].rearrange("p (e d) -> p e d", e=EXPERTS)
        b1_cols = sb("b1_cols", [P, 16])
        keep, block_rows = f_scan[11], f_scan[12]
        last_col, last_row = sb("last_col", [P, 1], I32), sb("last_row", [1, TILES], I32)

        def tiles_of(first, n):
            return WK[:, first:first + TILES * n].rearrange("p (t n) -> p t n", n=n)

        sums, agg, squares = tiles_of(6400, 20), tiles_of(8400, HE), tiles_of(10000, HE)
        den, scores, gates, beaten = (tiles_of(11600 + 400 * i, 4) for i in range(4))
        mu, var = WK[:, 13200:13200 + TILES], WK[:, 13300:13300 + TILES]
        gat_bias, gamma, beta = (WK[:, 13400 + HE * i:13400 + HE * (i + 1)] for i in range(3))
        yin = R1[:, 0:4096].rearrange("p (s n) -> p s n", s=4)
        x1in, mixed = (R1[:, 4096 + 1024 * i:5120 + 1024 * i].rearrange("p (s n) -> p s n", s=4) for i in range(2))
        GROUPS = TILES // 2

        @block.sync
        def _(sp):
            for dst_, src_ in ((ident, consts["ident"]), (iota_row, consts["iota_row"]),
                               (signs, consts["signs"]), (part_id, consts["part_id"])):
                sp.dma_start(dst_[:, :], src_).then_inc(consts_in, 16)
            sp.wait_ge(filled, 4)

            def load_keys(rows, cols, parts):
                n = rows.shape[0] // parts
                r, c = (sort_bufs[i].bitcast(I32) for i in range(2))
                sp.dma_start(r[0:parts, 0:n], rows.rearrange("(p c) -> p c", p=parts)).then_inc(keys_in, 16)
                sp.dma_start(c[0:parts, 0:n], cols.rearrange("(p c) -> p c", p=parts)).then_inc(keys_in, 16)
                sp.dma_start(r[0:HEADER_PARTS, n:n + HEADERS], consts["headers"]).then_inc(keys_in, 16)

            load_keys(a["src"], a["dst"], HEADER_PARTS)
            x_tiles = a["x"][0:(TILES - 1) * P, :].rearrange("(t p) d -> p t d", p=P)
            for c in range(7):
                n = 14 if c < 6 else 13
                sp.dma_start(XR[:, 14 * c:14 * c + n, :], x_tiles[:, 14 * c:14 * c + n, :]).then_inc(x_in[c], 16)
            sp.dma_start(XR[0:LAST, TILES - 1, :], a["x"][(TILES - 1) * P:, :]).then_inc(x_in[6], 16)
            sp.dma_start(w_nat, a["W_layer"].rearrange("(k p) d -> p k d", p=P)).then_inc(w_in, 16)
            for i, name in enumerate(("w_a2", "w_a1")):
                sp.dma_start(wa[:, :, i], a[name][0, :].rearrange("(k p) -> p k", p=P),
                         allow_slow_non_contiguous=True).then_inc(w_in, 16)
            sp.dma_start(bcol, a["b_layer"].rearrange("(k p) -> p k", p=P),
                         allow_slow_non_contiguous=True).then_inc(w_in, 16)
            sp.dma_start(bias_row[0:1, 0:D], a["b_layer"].rearrange("(o n) -> o n", o=1)).then_inc(w_in, 16)
            for i, name in enumerate(("b_a2", "b_a1")):
                sp.dma_start(ba[:, i:i + 1], a[name].rearrange("(o n) -> o n", o=1)).then_inc(w_in, 16)

            def rows(table, width, base, pair):
                for s in range(2):
                    sp.wait_ge(lin_copied, base + pair * 2 + s + 1)
                    sp.dma_start(table[bass.ds((pair * 2 + s) * P, P), :], lin[s][:, 0:width]).then_inc(rows_out[s], 16)
                    if table is h_table:
                        sp.dma_start(table[bass.ds((pair * 2 + s) * P + PADDED, P), :],
                                     lin[s][:, 1:1 + width]).then_inc(rows_out[s], 16)

            with sp.Fori(0, NP2) as i:
                rows(h_table, ROW, 0, i)
            sp.wait_ge(filled, 8)
            load_keys(a["edge_index"][1, :], a["edge_index"][0, :], P)
            sp.dma_start(gate_w[:, :, 0:HE], a["W_gat"].rearrange("(k p) n -> p k n", p=P)).then_inc(gate_w_in, 16)
            for w, name in enumerate(("att_src", "att_dst")):
                sp.dma_start(att[:, w, :], a[name].rearrange("h e -> (h e)").partition_broadcast(P)).then_inc(gate_w_in, 16)

            sp.wait_ge(ones_set, 1)

            def rows_back(j, h):
                sp.wait_ge(stashed[h % 2], (2 * j + h // 2 + 1) * 16)
                sp.dma_start(gbuf[h // 2][:, 8 * (h % 2):8 * (h % 2) + 8, 0:D],
                             stash[bass.ds(4 * j + h, 1)].rearrange("o p s d -> p (o s) d")).then_inc(rows_in[h], 16)

            for h in range(4):
                rows_back(0, h)
            with sp.Fori(1, GNN.steps // 32) as i:
                for h in range(4):
                    sp.wait_ge(summed, (i - 1) * 32 + 8 * h + 8)
                    rows_back(i, h)

            sp.wait_ge(summed, GNN.steps)
            for s in range(2):
                sp.dma_start(xin[s], x_tiles[:, 7 * s:7 * s + 7, :]).then_inc(xg_in[s], 16)
            with sp.Fori(0, 5) as i:
                for s in range(2):
                    sp.wait_ge(xg_used, 2 * i + s + 1)
                    sp.dma_start(xin[s], x_tiles[:, bass.ds((2 * i + 2 + s) * 7, 7), :]).then_inc(xg_in[s], 16)
            sp.wait_ge(xg_used, 11)
            sp.dma_start(xin[0], x_tiles[:, 84:91, :]).then_inc(xg_in[0], 16)
            sp.wait_ge(xg_used, 12)
            sp.dma_start(xin[1][:, 0:6, :], x_tiles[:, 91:97, :]).then_inc(xg_in[1], 16)
            sp.dma_start(xin[1][0:LAST, 6, :], a["x"][(TILES - 1) * P:, :]).then_inc(xg_last, 16)
            x1_view = x1_rows.rearrange("(t p) d -> p t d", p=P)
            for c in range(7):
                sp.wait_ge(xg_used, 2 * c + 2)
                sp.dma_start(x1_view[:, 14 * c:14 * c + 14, :], ACC[:, 14 * c:14 * c + 14, 0:D]).then_inc(x1_out, 16)

            with sp.Fori(0, NP2) as i:
                for s in range(2):
                    t = i * 2 + s
                    sp.wait_ge(xT_ready, TILES + t + 1)
                    sp.dma_start(xT_tiles[bass.ds(t, 1), :, :].rearrange("o p n -> (o p) n"), xT[s]).then_inc(xT_out[s], 16)
                rows(gate_table, GW_IN, TILES, i)

            sp.wait_ge(x1_out, 16 * 7)
            for s in range(2):
                sp.wait_ge(rows_out[s], 16 * 3 * NP2)
                sp.wait_ge(xT_out[s], 16 * NP2)
            for k in range(2):
                sp.dma_start(w1[:, k, :].rearrange("p (e f) -> p e f", e=EXPERTS),
                             a["W1"].rearrange("e (k p) f -> k p e f", p=P)[k]).then_inc(weights_in, 16)
            sp.dma_start(w2, a["W2"].rearrange("e f d -> (e f) d").rearrange("(c p) d -> p c d", p=P)).then_inc(weights_in, 16)
            sp.dma_start(b1_cols[:, :], a["b1"].rearrange("e f -> (e f)").rearrange("(c p) -> p c", p=P),
                         allow_slow_non_contiguous=True).then_inc(weights_in, 16)
            sp.dma_start(b2_all.rearrange("p e d -> p (e d)"),
                         a["b2"].rearrange("e d -> (e d)").partition_broadcast(P)).then_inc(weights_in, 16)

            def load_xe(g, s):
                sp.dma_start(xe[:, s].rearrange("p t k n -> p t (k n)"),
                             xT_tiles[bass.ds(g * 2, 2), :, :].rearrange("t p n -> p t n")).then_inc(xe_in[s], 16)

            def store_y(g, s):
                sp.dma_start(y_rows[bass.ds(g * 2 * P, 2 * P), :].rearrange("(t p) n -> p t n", p=P),
                             ystage[:, s].rearrange("p t e d -> p t (e d)")).then_inc(y_out[s], 16)

            load_xe(0, 0)
            load_xe(1, 1)

            def next_group(g, s, load):
                sp.wait_ge(y_copied, (g + 1) * EXPERTS)
                store_y(g, s)
                if load:
                    load_xe(g + 2, s)

            with sp.Fori(0, GROUPS // 2 - 1) as i:
                for s in range(2):
                    next_group(i * 2 + s, s, True)
            next_group(GROUPS - 3, 0, True)
            next_group(GROUPS - 2, 1, False)
            next_group(GROUPS - 1, 0, False)

            sp.wait_ge(blocks_ready, 1)
            sp.dma_start(gate_blocks, f_scan[11][:, 0:GATE.jj].bitcast(I32)).then_inc(gate_in, 16)
            sp.wait_ge(gate_in, 16)
            sp.dma_start(f_scan[12][0:1, :].bitcast(I32), gate_blocks.rearrange("p (o j) -> o (p j)", o=1)).then_inc(gate_in, 16)
            sp.wait_ge(blocks_ready, 2)
            sp.dma_start(gate_blocks_f, f_scan[11][0:1, :]).then_inc(gate_in, 16)
            sp.wait_ge(gate_in, 48)
            sp.wait_ge(blocks_ready, 3)
            sp.dma_start(block_rows, gate_blocks_f[0, :].partition_broadcast(P)).then_inc(gate_in, 16)
            sp.wait_ge(blocks_ready, 4)
            for ap_, name in ((gat_bias, "b_gat"), (gamma, "ln_gamma"), (beta, "ln_beta")):
                sp.dma_start(ap_, a[name].partition_broadcast(P)).then_inc(gates_need, 16)
            sp.dma_start(last_steps, last_col[0:TILES, :],
                         allow_slow_non_contiguous=True).then_inc(gate_in, 16)
            sp.wait_ge(gate_in, 80)
            sp.dma_start(last_row[:, :], last_steps.rearrange("t o -> o t"),
                         allow_slow_non_contiguous=True).then_inc(gate_in, 16)

            for s in range(2):
                sp.wait_ge(y_out[s], 16 * (GROUPS // 2 + (1 - s)))
            sp.wait_ge(blocks_ready, 5)

            def load_mix(t, s):
                sp.dma_start(yin[:, s, :], y_rows[bass.ds(t * P, P), :]).then_inc(fin_in[s], 16)
                sp.dma_start(x1in[:, s, :], x1_rows[bass.ds(t * P, P), :]).then_inc(fin_in[s], 16)

            for s in range(4):
                load_mix(s, s)
            with sp.Fori(0, 23) as i:
                for s in range(4):
                    sp.wait_ge(fin_out[s], 16 * (i + 1))
                    load_mix(4 * i + 4 + s, s)
            for s in range(2):
                sp.wait_ge(fin_out[s], 16 * 24)
                load_mix(96 + s, s)

        @block.gpsimd
        def _(pool):
            r, c = (sort_bufs[i].bitcast(I32) for i in range(2))
            pool.memset(waited[:, :], 0.0)
            pool.memset(r, PAD_ROW).then_inc(filled, 1)
            pool.memset(c, 0).then_inc(filled, 1)
            pool.memset(XR[:, TILES - 1, :], 0.0).then_inc(filled, 2)

            staged = Tally(idx_staged, 2 + 2 * GNN.steps // U)

            def hold(n):
                pool.tensor_tensor(waited[:, bass.ds(n, 1)] if not isinstance(n, int) else waited[:, n:n + 1], waited[:, 0:1], waited[:, 0:1], ALU.add)

            kept = Tally(rows_kept)
            slots_used = [0]

            def gather(s, table, dest):
                pool.indirect_dma_start(dest, None, table,
                                        bass.IndirectOffsetOnAxis(ap=idx_slots[:, s:s + 1], axis=0)
                                        ).then_inc(landed[s], 16)

            def gather_resident(g, table, idx, slot, dest):
                turns = g.steps // U
                base = slots_used[0]

                def keep(i, h):
                    for s in range(8 * h, 8 * h + 8):
                        pool.wait_ge(landed[s], (i + 1 + base) * 16)
                    return kept.add(pool.tensor_copy(dest(i, h), slot(h)))

                def stage(i, h):
                    pool.wait_ge(idx_staged, staged.add(pool.tensor_copy(
                        idx_slots[:, 8 * h:8 * h + 8], idx[:, bass.ds(i * U + 8 * h, 8)])))
                    pool.tensor_tensor(waited[:, 0:1], waited[:, 0:1], waited[:, 0:1], ALU.add)
                    for s in range(8 * h, 8 * h + 8):
                        gather(s, table, slot(h)[:, s - 8 * h] if len(slot(h).shape) == 3 else slot(h)[:, s - 8 * h:s - 8 * h + 1])

                for h in range(2):
                    stage(0, h)
                with loop(pool, turns - 1, (staged, 2), (kept, 2)) as i:
                    for h in range(2):
                        pool.wait_ge(rows_kept, keep(i, h))
                        stage(i + 1, h)
                for h in range(2):
                    keep(turns - 1, h)
                slots_used[0] += turns

            for s in range(2):
                pool.wait_ge(rows_out[s], 32 * NP2)

            def first_half(i, h, first):
                pool.wait_ge(idx_staged, 2 * i + h + 1)
                if not first:
                    pool.wait_ge(stashed[h], i * 16)
                    pool.wait_ge(a_kept, 2 * i + h - 1)
                hold(2 * i + h + 1)
                for s in range(8 * h, 8 * h + 8):
                    gather(s, h_table, first_rows[:, s, :])

            for h in range(2):
                first_half(0, h, True)
            with pool.Fori(1, GNN.steps // U) as i:
                for h in range(2):
                    first_half(i, h, False)
            slots_used[0] += GNN.steps // U

            for s in range(2):
                pool.wait_ge(rows_out[s], 16 * 3 * NP2)
            pool.wait_ge(x1_out, 16 * 7)
            pool.wait_ge(xn_ready, 2 * TILES)
            pool.memset(R1[:, GATE.steps * GW_IN:], 0.0)
            gather_resident(GATE, gate_table, FI.bitcast(I32),
                            lambda h: gate_slots[:, 8 * h:8 * h + 8, :],
                            lambda i, h: G[:, bass.ds(i * U + 8 * h, 8), :])

        @block.scalar
        def _(act):
            act.wait_ge(stat_ready, 1)
            act.activation(rstd[:, :], stat[:, :, 1], ACT.Sqrt, bias=eps[:, :]).then_inc(std_ready, 1)

            for k in range(4):
                act.wait_ge(prep_turned, 4)
                act.copy(proj[:, k % 2, (k // 2) * P:(k // 2 + 1) * P], ps[:, 2048 + k * P:2048 + (k + 1) * P]).then_inc(prep_copied, 1)
            act.wait_ge(prep_turned, 5)
            for kd in range(2):
                act.copy(proj[:, kd, D:D + 2], ps[:, 2560 + 2 * kd:2562 + 2 * kd]).then_inc(prep_copied, 1)
            act.copy(bias_row[0:1, D:D + 2], ps[0:1, 3072:3074]).then_inc(prep_copied, 1)

            def node_linear(phase, src):
                base, width = phase * TILES, (258, GW_IN)[phase]
                act.wait_ge(std_ready, 2 + 2 * phase)

                def pair(i, first):
                    for s in range(2):
                        t = i * 2 + s
                        if not first:
                            act.wait_ge(xn_turned, base + t - 1)
                        act.activation(xn[s], src(t), ACT.Identity, bias=shift[:, bass.ds(t, 1)],
                                       scale=rstd[:, bass.ds(t, 1)]).then_inc(xn_ready, 1)
                    for s in range(2):
                        t = i * 2 + s
                        act.wait_ge(xn_turned, base + t + 1)
                        if not first:
                            act.wait_ge(lin_ready, base + t - 1)
                            if phase:
                                act.wait_ge(xT_out[s], i * 16)
                        act.copy(xT[s], psT[s]).then_inc(xT_ready, 1)
                    for s in range(2):
                        t = i * 2 + s
                        act.wait_ge(lin_ready, base + t + 1)
                        if not first:
                            act.wait_ge(rows_out[s], phase * 32 * NP2 + i * (32, 16)[phase])
                        act.copy(lin[s][:, 0:width], psL[s][:, 0:width]).then_inc(lin_copied, 1)

                pair(0, True)
                with act.Fori(1, NP2) as i:
                    pair(i, False)

            node_linear(0, lambda t: XR[:, bass.ds(t, 1), :].rearrange("p o d -> p (o d)"))

            act.wait_ge(idx_ready, 1)

            def stage(i, h):
                act.copy(idx_slots[:, 8 * h:8 * h + 8], GI.bitcast(I32)[:, bass.ds(i * U + 8 * h, 8)]).then_inc(idx_staged, 1)

            def gathered(i):
                for h in range(2):
                    for s in range(8 * h, 8 * h + 8):
                        act.wait_ge(landed[s], (i + 1) * 16)
                    act.dma_start(stash[bass.ds(2 * i + h, 1)].rearrange("o p s d -> p (o s) d"),
                                  first_rows[:, 8 * h:8 * h + 8, 0:D]).then_inc(stashed[h], 16)
                    act.copy(SC[:, bass.ds(i * U + 8 * h, 8)],
                             first_rows[:, 8 * h:8 * h + 8, D]).then_inc(a_kept, 1)
                    stage(i + 1, h)

            def chunk_exps(c):
                act.wait_ge(exp_ready, c + 1)
                act.activation(c_scan[11], c_scan[11], ACT.Exp)
                act.activation(joined[0:1, 0:1], joined[0:1, 0:1], ACT.Exp).then_inc(exp_done, 1)

            for h in range(2):
                stage(0, h)
            with act.Fori(0, EXP_FIRST) as i:
                gathered(i)
            with act.Fori(0, EXP_MEANWHILE) as c:
                chunk_exps(c)
                with act.Fori(0, EXP_EVERY) as i:
                    gathered(c * EXP_EVERY + EXP_FIRST + i)
            with act.Fori(EXP_FIRST + EXP_MEANWHILE * EXP_EVERY, GNN.steps // U) as i:
                gathered(i)
            with act.Fori(EXP_MEANWHILE, CHUNKS) as c:
                chunk_exps(c)

            act.wait_ge(stat_ready, 2)
            act.activation(rstd[:, :], stat[:, :, 1], ACT.Sqrt, bias=eps[:, :]).then_inc(std_ready, 1)
            node_linear(1, lambda t: ACC[:, bass.ds(t, 1), 0:D].rearrange("p o d -> p (o d)"))

            act.wait_ge(weights_in, 16 * 5)
            act.preload_act_table(ACT.Gelu)

            def gelu(n, e, first):
                if not first:
                    act.wait_ge(y_ready, n - 1)
                for f in range(4):
                    act.wait_ge(hid_ready, n * 4 + (f | 1) + 1)
                    act.activation(hidT[:, e % 2, f, :], ps[:, (e % 2) * 1024 + f * 256:(e % 2) * 1024 + (f + 1) * 256],
                                   ACT.Gelu, bias=b1_cols[:, 4 * e + f:4 * e + f + 1]).then_inc(gelu_done, 1)

            for e in range(EXPERTS):
                gelu(e, e, e < 2)
            with act.Fori(1, GROUPS) as g:
                for e in range(EXPERTS):
                    gelu(g * EXPERTS + e, e, False)

            for hd in range(HEADS):
                act.wait_ge(exp_ready, CHUNKS + 1 + hd)
                act.activation(f_scan[10], f_scan[9], ACT.Exp).then_inc(exp_done, 1)

            def keep_sums(i):
                for h in range(2):
                    act.wait_ge(agg_ready, 2 * i + h + 1)
                    act.copy(G[:, bass.ds(i * U + 8 * h, 8), 0:20],
                             ps[:, h * 512:h * 512 + 160].rearrange("p (s w) -> p s w", w=20)).then_inc(agg_done, 1)

            with act.Fori(0, GATE.steps // U) as i:
                keep_sums(i)

            act.wait_ge(exp_ready, CHUNKS + HEADS + 1)
            act.activation(mu, var, ACT.Sqrt, bias=eps[:, :]).then_inc(exp_done, 1)
            act.wait_ge(exp_ready, CHUNKS + HEADS + 2)
            act.activation(gates, scores, ACT.Exp).then_inc(exp_done, 1)

            def store(t, s, rows=P):
                act.wait_ge(fin_ready, t + 1)
                o = out[bass.ds(t * P, P), :] if rows == P else out[(TILES - 1) * P:, :]
                act.dma_start(o, mixed[0:rows, s, :]).then_inc(fin_out[s], 16)

            with act.Fori(0, 24) as i:
                for s in range(4):
                    store(4 * i + s, s)
            store(96, 0)
            store(97, 1, LAST)
            for s in range(4):
                act.wait_ge(fin_out[s], 16 * (25 if s < 2 else 24))

        @block.vector
        def _(dve):
            done, ask = Tally(dve_done), Tally(to_turn)

            def link(ins, tally=None):
                tally = tally or done
                dve.wait_ge(tally.sem, tally.add(ins))

            back = Tally(turned)

            def answer(n=1):
                dve.wait_ge(turned, back.pass_by(n))

            dve.memset(eps[:, :], EPS).then_inc(dve_done, 1)
            dve.memset(ones_row[:, :], 1.0).then_inc(dve_done, 1)
            done.local = 2
            dve.wait_ge(consts_in, 64)

            for c in range(7):
                dve.wait_ge(x_in[c], 16 if c < 6 else 32)
                with loop(dve, 2, (done, 7)) as i:
                    for s in range(7):
                        t = 14 * c + 7 * i + s
                        done.add(dve.bn_stats(bn[:, bass.ds(t, 1), :].rearrange("p o s -> p (o s)"),
                                              XR[:, bass.ds(t, 1), :].rearrange("p o d -> p (o d)")))
            dve.wait_ge(dve_done, done.n)

            def statistics():
                mean, var_ = stat[:, :, 0], stat[:, :, 1]
                link(dve.tensor_tensor(var_, bn[:, :, 1], bn[:, :, 4], ALU.subtract))
                link(dve.tensor_tensor(mean, bn[:, :, 1], bn[:, :, 4], ALU.add))
                link(dve.tensor_scalar(mean, mean, 0.5, None, ALU.mult))
                link(dve.tensor_tensor(var_, var_, var_, ALU.mult))
                link(dve.tensor_tensor(bn[:, :, 2], bn[:, :, 2], bn[:, :, 5], ALU.add))
                link(dve.tensor_scalar(bn[:, :, 2], bn[:, :, 2], 1.0 / D, None, ALU.mult))
                link(dve.scalar_tensor_tensor(var_, var_, 0.25, bn[:, :, 2], ALU.mult, ALU.add))

            def scales(std_count):
                dve.wait_ge(std_ready, std_count)
                link(dve.reciprocal(rstd[:, :], rstd[:, :]))
                dve.scalar_tensor_tensor(shift[:, :], stat[:, :, 0], -1.0, rstd[:, :], ALU.mult, ALU.mult).then_inc(std_ready, 1)

            statistics()
            dve.engine_nop().then_inc(stat_ready, 1)
            scales(1)
            dve.wait_ge(prep_copied, 7)
            dve.wait_ge(w_in, 16 * 7)
            dve.tensor_add(bias_row[0:1, D:D + 2], bias_row[0:1, D:D + 2], ba).then_inc(proj_ready, 1)

            def sort(g):
                cur = [0]
                n = g.edges // (HEADER_PARTS if g is GNN else P)
                parts = HEADER_PARTS if g is GNN else P
                r, c = (sort_bufs[i].bitcast(I32) for i in range(2))
                link(dve.tensor_scalar(c[0:parts, 0:n], c[0:parts, 0:n], 1, None, ALU.add))
                link(dve.tensor_scalar(r, r, 14, TAG, ALU.logical_shift_left, ALU.bitwise_or))
                link(dve.tensor_tensor(r, r, c, ALU.bitwise_or))

                def stage(j, tally=None):
                    (lo, hi), (olo, ohi) = halves(sort_bufs[cur[0]], j), halves(sort_bufs[1 - cur[0]], j)
                    done.add(dve.tensor_tensor(olo, lo, hi, ALU.min))
                    link(dve.tensor_tensor(ohi, lo, hi, ALU.max), tally)
                    cur[0] = 1 - cur[0]

                def directed_stage(j, k):
                    split = dict(d=2, m=1 << (k - 1 - j), b=2, l=1 << j)
                    va, vb = (sort_bufs[x].rearrange("p (h d m b l) -> p h d m b l", **split)
                              for x in (cur[0], 1 - cur[0]))
                    for d in range(2):
                        lo, hi = va[:, :, d, :, 0, :], va[:, :, d, :, 1, :]
                        done.add(dve.tensor_tensor(vb[:, :, d, :, d, :], lo, hi, ALU.min))
                        done.add(dve.tensor_tensor(vb[:, :, d, :, 1 - d, :], lo, hi, ALU.max))
                    dve.wait_ge(dve_done, done.n)
                    cur[0] = 1 - cur[0]

                def flip(k, tally=None):
                    link(dve.tensor_scalar(sort_bufs[1 - cur[0]], sort_bufs[cur[0]], signs[:, k - 11:k - 10],
                                           None, ALU.mult), tally)
                    cur[0] = 1 - cur[0]

                for k in range(1, 11):
                    for j in range(k - 1, -1, -1):
                        directed_stage(j, k)
                flip(11)
                for j in range(10, -1, -1):
                    stage(j)
                for k in range(12, 19):
                    flip(k, ask)
                    m = k - 12
                    for h in range(2):
                        answer()
                        lo, hi = halves(ps[:, h * 1024:(h + 1) * 1024], m)
                        olo, ohi = halves(sort_bufs[1 - cur[0]][:, h * 1024:(h + 1) * 1024], m)
                        sv = spare[:, h * 512:(h + 1) * 512].rearrange("p (x l) -> p x l", l=1 << m)
                        link(dve.tensor_copy(sv, hi))
                        done.add(dve.tensor_tensor(olo, lo, sv, ALU.min))
                        link(dve.tensor_tensor(ohi, lo, sv, ALU.max), ask if m == 0 and h else None)
                    cur[0] = 1 - cur[0]
                    for mm in range(m - 1, -1, -1):
                        stage(mm, None if mm else ask)
                    answer(2)
                    o = sort_bufs[1 - cur[0]]
                    link(dve.tensor_copy(spare, ps[:, 1024:2048]))
                    done.add(dve.tensor_tensor(o[:, 0:1024], ps[:, 0:1024], spare, ALU.min))
                    link(dve.tensor_tensor(o[:, 1024:2048], ps[:, 0:1024], spare, ALU.max))
                    cur[0] = 1 - cur[0]
                    for j in range(9, -1, -1):
                        stage(j, ask if k == 18 and j == 0 else None)
                answer(2)

            def spread(g, keys):
                link(dve.memset(keys, 0.0))
                n = g.cols // 16
                link(dve.tensor_copy(keys[:, 0:g.cols].rearrange("p (q c) -> p c q", c=16),
                                     ps[:, 0:2048].rearrange("p (c q) -> p c q", c=16)[:, :, 0:n]))
                bufs = [E[:, i * g.q:(i + 1) * g.q].bitcast(I32) for i in range(4)]
                cu, at = keys.bitcast(I32), -1
                for bit in range(6, -1, -1):
                    by = 1 << bit
                    mask, moving = bufs[0], bufs[1]
                    at = 2 if at != 2 else 3
                    new = bufs[at]
                    link(dve.tensor_scalar(mask, cu, 31 - 21 - bit, 31, ALU.logical_shift_left, ALU.arith_shift_right))
                    link(dve.tensor_tensor(moving, cu, mask, ALU.bitwise_and))
                    link(dve.tensor_tensor(new, cu, moving, ALU.bitwise_xor))
                    o = new if bit else keys.bitcast(I32)
                    if not bit:
                        link(dve.tensor_copy(o[:, 0:by], new[:, 0:by]))
                    link(dve.tensor_tensor(o[:, by:], new[:, by:], moving[:, :-by], ALU.bitwise_or))
                    cu = o

            dve.wait_ge(filled, 4)
            dve.wait_ge(keys_in, 48)
            sort(GNN)
            spread(GNN, KS)

            def gather_index(g, keys, dest, scratch, last):
                k_int = keys.bitcast(I32)
                e0, e1, e2 = (scratch[:, i * g.q:(i + 1) * g.q].bitcast(I32) for i in range(3))
                link(dve.tensor_scalar(e0, k_int, LOW, None, ALU.bitwise_and))
                link(dve.tensor_scalar(e1, k_int, 14, LOW, ALU.logical_shift_right, ALU.bitwise_and))
                link(dve.tensor_scalar(e2, e0, 0, None, ALU.is_equal))
                link(dve.tensor_scalar(e1, e1, 1 + PADDED if g is GNN else 1, None, ALU.add))
                link(dve.tensor_tensor(e1, e1, e2, ALU.mult))
                link(dve.tensor_tensor(e0, e0, e1, ALU.add))
                last(dve.tensor_scalar(dest.bitcast(I32), e0, -1, 0, ALU.add, ALU.max))

            for s in range(2):
                dve.wait_ge(rows_out[s], 32 * NP2)
            gather_index(GNN, KS, GI, E, lambda ins: ins.then_inc(idx_ready, 1))
            link(dve.memset(SC[:, GNN.steps:], 0.0))

            r, c = (sort_bufs[i].bitcast(I32) for i in range(2))
            link(dve.memset(r, PAD_ROW))
            dve.memset(c, 0).then_inc(filled, 4)
            dve.wait_ge(filled, 8)
            dve.wait_ge(keys_in, 96)
            sort(GATE)
            spread(GATE, FK[:, :])
            gather_index(GATE, FK[:, :], FI[:, :], E, link)

            dve.wait_ge(gate_w_in, 48)
            for w in range(2):
                link(dve.tensor_tensor(att_prod[:, :, :], gate_w[:, :, 0:HE], att[:, w:w + 1, :].broadcast_to([P, 2, HE]), ALU.mult))
                link(dve.tensor_reduce(gate_w[:, :, HE + 4 * w:HE + 4 * w + 4],
                                       att_prod[:, :, :].rearrange("p k (h e) -> p k h e", e=EXPERTS), AX.X, ALU.add))
            dve.engine_nop().then_inc(gate_w_ready, 1)

            def to_scan(g, dest, source=None):
                answer()
                link(dve.tensor_copy(dest, ps[:, 0:g.q]))

            def seg_scan(res, d0, d1, op0, op1, neutral, reverse=False, state=None):
                v = (lambda z: z[:, ::-1]) if reverse else (lambda z: z)
                end = 0 if reverse else res.shape[1] - 1
                link(dve.tensor_tensor_scan(v(res), v(d0), v(d1), neutral, op0, op1))
                link(dve.tensor_reduce(col[:, 1:2], d0, AX.X, ALU.min))
                link(dve.tensor_copy(col[:, 0:1], res[:, end:end + 1]), ask)
                answer()
                link(dve.tensor_copy(row[:, :], ps[0:1, 0:2 * P]))
                start = P if reverse else 0
                if state is None:
                    link(dve.memset(carry[0:1, start:start + 1], neutral))
                else:
                    link(dve.tensor_copy(carry[0:1, 0:1], state))
                o = carry[0:1, 0:P] if reverse else carry[0:1, 1:P + 1]
                link(dve.tensor_tensor_scan(v(o), v(row[:, P:2 * P]), v(row[:, 0:P]),
                                            neutral if state is None else state, op0, op1), ask)
                if state is not None:
                    link(dve.tensor_copy(state, carry[0:1, P:P + 1]))
                answer()
                link(dve.tensor_copy(ccol[:, :], ps[:, 0:1]))
                link(dve.tensor_tensor_scan(v(res), v(d0), v(d1), ccol[:, :], op0, op1))

            def next_first(dest, flags, after):
                n = flags.shape[1]
                link(dve.tensor_scalar(dest[:, 0:n - 1], flags[:, 1:n], -BIG, None, ALU.mult))
                link(dve.tensor_copy(col[:, 0:1], flags[:, 0:1]), ask)
                answer()
                link(dve.memset(carry[0:1, P - 1:P], after))
                link(dve.tensor_copy(carry[0:1, 0:P - 1], ps[0:1, 1:P]), ask)
                answer()
                link(dve.tensor_scalar(dest[:, n - 1:n], ps[:, 0:1], -BIG, None, ALU.mult))

            def block_of_steps(g, keys_f, dest, tmp):
                link(dve.tensor_reduce(tmp[:, 0:g.jj], keys_f.rearrange("p (j n) -> p j n", n=P), AX.X, ALU.max))
                link(dve.tensor_scalar(tmp[:, 0:g.jj].bitcast(I32), tmp[:, 0:g.jj].bitcast(I32), 21, 127,
                                       ALU.logical_shift_right, ALU.bitwise_and))
                dve.tensor_scalar(dest[:, 0:g.jj].bitcast(I32), tmp[:, 0:g.jj].bitcast(I32), TILES - 1, None,
                                  ALU.min).then_inc(blocks_ready, 1)

            def marks_of(g, kf, tmp, head, edge, reset, nhead, reset_next):
                link(dve.tensor_scalar(tmp.bitcast(I32), kf.bitcast(I32), TAG | LOW, None, ALU.bitwise_and))
                link(dve.tensor_scalar(head, tmp, TAG_FLOAT, None, ALU.is_equal))
                link(dve.tensor_scalar(edge, tmp, TAG_FLOAT, None, ALU.is_gt if g is GNN else ALU.is_ge))
                link(dve.tensor_scalar(reset, head, -BIG, None, ALU.mult))
                link(dve.tensor_scalar(nhead, head, -1.0, 1.0, ALU.mult, ALU.add))
                next_first(reset_next, head, 1.0)

            def attention(slope, head_v, edge, reset, nhead, reset_next, a_dst_in, a_src_in,
                          adst, v2, mf, mb, t1, out_exp, count, chunk=False):
                link(dve.tensor_tensor(t1, head_v, a_dst_in, ALU.mult))
                seg_scan(adst, nhead, t1, ALU.mult, ALU.add, 0.0, state=state[0:1, 0:1] if chunk else None)
                link(dve.tensor_scalar(v2, edge, 1.0, BIG, ALU.subtract, ALU.mult))
                link(dve.tensor_tensor(t1, a_src_in, edge, ALU.mult))
                link(dve.tensor_tensor(v2, v2, t1, ALU.add))
                if chunk:
                    link(dve.tensor_copy(state[0:1, 2:3], state[0:1, 1:2]))
                seg_scan(mf, reset, v2, ALU.add, ALU.max, -BIG, state=state[0:1, 1:2] if chunk else None)
                seg_scan(mb, reset_next, mf, ALU.add, ALU.max, -BIG, reverse=True)
                link(dve.tensor_tensor(mb, mb, adst, ALU.add))
                link(dve.scalar_tensor_tensor(mf, mb, slope, mb, ALU.mult, ALU.max))
                if chunk:
                    x = joined[0:1, 0:1]
                    link(dve.tensor_tensor(x, state[0:1, 2:3], adst[0:1, 0:1], ALU.add))
                    link(dve.scalar_tensor_tensor(x, x, slope, x, ALU.mult, ALU.max))
                    link(dve.tensor_tensor(x, x, mf[0:1, 0:1], ALU.subtract))
                    link(dve.tensor_tensor(x, x, nhead[0:1, 0:1], ALU.mult))
                link(dve.tensor_tensor(v2, v2, adst, ALU.add))
                link(dve.scalar_tensor_tensor(mb, v2, slope, v2, ALU.mult, ALU.max))
                dve.tensor_tensor(t1, mb, mf, ALU.subtract).then_inc(exp_ready, 1)
                dve.wait_ge(exp_done, count)
                link(dve.tensor_tensor(out_exp, out_exp, edge, ALU.mult), ask)

            KF, HD, ED, RS, RN, NH, VF, AD, V2, MF, MB, T1 = c_scan[0:12]
            for v in gbuf:
                done.add(dve.memset(v[:, :, D], 1.0))
            dve.engine_nop().then_inc(ones_set, 1)
            done.add(dve.memset(R1[:, 0:TILES * 257], 0.0))
            done.add(dve.memset(ones_row[:, :], 1.0))
            done.add(dve.memset(state[:, :], 0.0))
            dve.wait_ge(dve_done, done.n)
            link(dve.memset(state[:, 1:2], -BIG))
            hots, adds = Tally(hot_ready), Tally(added)
            adds.add(dve.memset(col[:, 0:1], 0.0), 8)

            def chunk_weights(c, kept):
                dve.wait_ge(a_kept, kept)
                link(dve.tensor_copy(c_keys, KS[:, bass.ds(c * P, P)]))
                link(dve.tensor_copy(c_scores, SC[:, bass.ds(c * P, P)]), ask)
                link(dve.tensor_scalar(T1.bitcast(I32), c_keys.bitcast(I32), 14, 127,
                                       ALU.logical_shift_right, ALU.bitwise_and))
                link(dve.tensor_copy(c_rows, T1.bitcast(I32)))
                last_key = state[0:1, 3:4]
                link(dve.tensor_scalar(joined_block[:, :], last_key.bitcast(I32), 14, 127,
                                       ALU.logical_shift_right, ALU.bitwise_and))
                link(dve.tensor_copy(joined[0:1, 1:2], joined_block[:, :]))
                link(dve.tensor_scalar(joined_block[:, :], last_key.bitcast(I32), 21, 127,
                                       ALU.logical_shift_right, ALU.bitwise_and))
                answer()
                done.add(dve.tensor_copy(VF, ps[:, 512:512 + P]))
                link(dve.tensor_copy(KF, ps[:, 0:P]))
                link(dve.tensor_scalar(T1.bitcast(I32), KF.bitcast(I32), TAG | LOW, None, ALU.bitwise_and))
                done.add(dve.tensor_scalar(HD, T1, TAG_FLOAT, None, ALU.is_equal))
                done.add(dve.tensor_scalar(ED, T1, TAG_FLOAT, None, ALU.is_gt))
                link(dve.tensor_reduce(col[:, 0:1], KF, AX.X, ALU.max))
                link(dve.tensor_copy(col[:, 1:2], HD[:, 0:1]), ask)
                done.add(dve.tensor_scalar(RS, HD, -BIG, None, ALU.mult))
                done.add(dve.tensor_scalar(NH, HD, -1.0, 1.0, ALU.mult, ALU.add))
                done.add(dve.tensor_scalar(RN[:, 0:P - 1], HD[:, 1:P], -BIG, None, ALU.mult))
                done.add(dve.memset(carry[0:1, P - 1:P], 1.0))
                answer()
                link(dve.tensor_copy(row[:, :], ps[0:1, 0:2 * P]))
                link(dve.tensor_copy(carry[0:1, 0:P - 1], row[0:1, P + 1:2 * P]), ask)
                link(dve.tensor_scalar(step_blocks[:, :], row[0:1, 0:P].bitcast(I32), 21, 127,
                                       ALU.logical_shift_right, ALU.bitwise_and))
                link(dve.tensor_reduce(row[0:1, P:P + 1], row[0:1, 0:P], AX.X, ALU.max))
                link(dve.tensor_tensor(last_key, last_key, row[0:1, P:P + 1], ALU.max))
                link(dve.tensor_scalar(step_blocks[:, :], step_blocks[:, :], TILES - 1, None, ALU.min))
                answer()
                link(dve.tensor_scalar(RN[:, P - 1:P], ps[:, 0:1], -BIG, None, ALU.mult))
                attention(0.01, HD, ED, RS, NH, RN, VF, VF, AD, V2, MF, MB, T1, T1, c + 1, chunk=True)
                answer()
                link(dve.tensor_copy(c_weights, ps[:, 0:P]))
                link(dve.tensor_copy(factor[:, 0:2], ps[:, 512:514]))
                link(dve.tensor_tensor(factor[:, 2:3], part_id[:, :], factor[:, 1:2], ALU.is_equal))
                link(dve.tensor_scalar(factor[:, 3:4], factor[:, 2:3], -1.0, 1.0, ALU.mult, ALU.add))
                link(dve.tensor_tensor(factor[:, 0:1], factor[:, 0:1], factor[:, 2:3], ALU.mult))
                done.add(dve.tensor_tensor(factor[:, 0:1], factor[:, 0:1], factor[:, 3:4], ALU.add))
                _, (b,) = nc.values_load_multi_w_load_instructions(
                    joined_block[0:1, 0:1], engines=[mybir.EngineType.DVE], min_val=0, max_val=TILES - 1)
                target = R1[:, bass.ds(b * 257, 257)]
                dve.wait_ge(dve_done, done.n)
                link(dve.tensor_scalar(target, target, factor[:, 0:1], None, ALU.mult))

            def one_hot(i, s):
                hots.add(dve.tensor_scalar(hot[:, s, :], iota_row[:, :], c_rows[:, bass.ds(i * U + s, 1)],
                                           c_weights[:, bass.ds(i * U + s, 1)], ALU.is_equal, ALU.mult))

            def add_turn(c, i, more):
                _, blocks = nc.values_load_multi_w_load_instructions(
                    step_blocks[0:1, bass.ds(i * U, U)],
                    engines=[mybir.EngineType.DVE], min_val=0, max_val=TILES - 1,
                    skip_runtime_bounds_check_because="the blocks are masked and clamped to 0..TILES - 1")
                for h in range(2):
                    for s in range(8):
                        b = blocks[8 * h + s]
                        dve.wait_ge(summed, c * P + i * U + 8 * h + s + 1)
                        target = R1[:, bass.ds(b * 257, 257)]
                        at = adds.add(dve.tensor_tensor(
                            target, target, ps[:, s * 512:s * 512 + 257], ALU.add))
                        if h == 0 or more:
                            one_hot(i + h, 8 * (1 - h) + s)
                        dve.wait_ge(added, at)

            def chunk(c, turns, kept):
                chunk_weights(c, kept)
                for s in range(8):
                    one_hot(0, s)
                with loop(dve, turns - 1, (hots, U), (adds, U)) as i:
                    add_turn(c, i, True)
                add_turn(c, turns - 1, False)

            with loop(dve, CHUNKS - 1, (done, CHUNK_DONE), (ask, CHUNK_ASKS), (back, CHUNK_ASKS), (hots, P), (adds, P)) as c:
                chunk(c, P // U, (c + 1) * 2 * P // U)
            chunk(CHUNKS - 1, LAST_STEPS // U, 2 * GNN.steps // U)

            rden = E[:, 3970:3970 + TILES]
            link(dve.tensor_scalar(rden, ACC[:, :, D], 1e-30, None, ALU.max))
            link(dve.reciprocal(rden, rden))
            used = Tally(xg_used)

            def residual(i, s):
                dve.wait_ge(xg_in[s], (i + 1) * 16)
                tiles = [14 * i + 7 * s + z for z in range(7)]
                x1 = [ACC[:, bass.ds(t, 1), 0:D].rearrange("p o d -> p (o d)") for t in tiles]
                for z, t in enumerate(tiles):
                    done.add(dve.scalar_tensor_tensor(x1[z], x1[z], rden[:, bass.ds(t, 1)], xin[s][:, z, :], ALU.mult, ALU.add))
                dve.wait_ge(dve_done, done.n)
                used.add(dve.memset(col[:, 0:1], 0.0))
                for z, t in enumerate(tiles):
                    done.add(dve.bn_stats(bn[:, bass.ds(t, 1), :].rearrange("p o s -> p (o s)"), x1[z]))

            with loop(dve, 6, (done, 28), (used, 2)) as i:
                for s in range(2):
                    residual(i, s)
            residual(6, 0)
            dve.wait_ge(xg_last, 16)
            residual(6, 1)
            dve.wait_ge(dve_done, done.n)
            statistics()
            dve.engine_nop().then_inc(stat_ready, 1)
            scales(3)

            dve.wait_ge(weights_in, 16 * 5)
            ys = Tally(y_copied)

            def y_copy(n, e, s):
                dve.wait_ge(y_ready, n + 1)
                ys.add(dve.tensor_tensor(ystage[:, s, :, e, :],
                                         ps[:, 2048 + e * 512:2560 + e * 512].rearrange("p (t d) -> p t d", t=2),
                                         b2_all[:, e:e + 1, :].broadcast_to([P, 2, D]), ALU.add))

            for g in range(2):
                for e in range(EXPERTS):
                    y_copy(g * EXPERTS + e, e, g)
            with loop(dve, GROUPS // 2 - 1, (ys, 8)) as i:
                for s in range(2):
                    dve.wait_ge(y_out[s], 16 * (i + 1))
                    for e in range(EXPERTS):
                        y_copy((2 * i + 2 + s) * EXPERTS + e, e, s)
            dve.wait_ge(y_out[0], 16 * (GROUPS // 2))
            for e in range(EXPERTS):
                y_copy((GROUPS - 1) * EXPERTS + e, e, 0)

            fKF, fH, fE, fRS, fRN, fNH, fVS, fVD, fV2, fT1, fX, fMF, fMB = f_scan
            dve.wait_ge(rows_kept, GATE_KEPT)
            for s in range(2):
                dve.wait_ge(y_out[s], 16 * (GROUPS // 2 + (1 - s)))
            link(dve.engine_nop(), ask)
            to_scan(GATE, fKF)
            marks_of(GATE, fKF, fT1, fH, fE, fRS, fNH, fRN)
            block_of_steps(GATE, fKF, fMF, fMB)
            link(dve.tensor_scalar(FI[:, :].bitcast(I32), FK[:, :].bitcast(I32), 14, 127,
                                   ALU.logical_shift_right, ALU.bitwise_and))
            link(dve.tensor_copy(FK[:, :], FI[:, :].bitcast(I32)))
            dve.wait_ge(gate_in, 32)
            link(dve.tensor_copy(fMF[0:1, :], fMB[0:1, :].bitcast(I32)))
            link(dve.tensor_tensor_scan(fMB[0:1, :], fMF[0:1, :], fMF[0:1, :], 0.0, ALU.max, ALU.max))
            link(dve.tensor_copy(fMF[0:1, :], fMB[0:1, :]))
            dve.engine_nop().then_inc(blocks_ready, 1)
            dve.wait_ge(gate_in, 48)
            link(dve.engine_nop(), ask)
            for hd in range(HEADS):
                to_scan(GATE, fVS)
                link(dve.engine_nop(), ask)
                to_scan(GATE, fVD)
                attention(0.2, fH, fE, fRS, fNH, fRN, fVD, fVS, fVD, fV2, fMF, fMB, fT1, fX, CHUNKS + 1 + hd)
                answer()
                link(dve.tensor_copy(G[:, :, HE + hd].rearrange("p (k j) -> p j k", j=GATE.jj),
                                     ps[:, 0:GATE.q].rearrange("p (j k) -> p j k", k=P)),
                     ask if hd < HEADS - 1 else None)
            for hd in range(HEADS):
                part = G[:, :, hd * 4:hd * 4 + 4]
                link(dve.tensor_tensor(part, part, G[:, :, HE + hd:HE + hd + 1].broadcast_to([P, GATE.q, 4]), ALU.mult))

            dve.engine_nop().then_inc(blocks_ready, 1)
            dve.wait_ge(gate_in, 64)
            n = GATE.steps
            link(dve.memset(keep[:, 0:1], 0.0))
            link(dve.tensor_tensor(keep[:, 1:n], block_rows[:, 1:n], block_rows[:, 0:n - 1], ALU.is_equal))
            upto = f_scan[10][:, 0:n]
            link(dve.tensor_scalar(upto, block_rows[:, 0:n], part_id[:, :], None, ALU.is_le))
            link(dve.tensor_reduce(ccol[:, :], upto, AX.X, ALU.add))
            link(dve.tensor_scalar(last_col[:, :], ccol[:, :], -1.0, None, ALU.add))
            dve.engine_nop().then_inc(blocks_ready, 1)

            hots2 = Tally(hot_ready, hots.n)

            def plain_hots(i, h):
                rows = FK[:, bass.ds(i * U + 8 * h, 8)].rearrange("p (s o) -> p s o", o=1)
                hots2.add(dve.tensor_tensor(hot[:, 8 * h:8 * h + 8, :], iota_row[:, :].rearrange("p (o n) -> p o n", o=1)
                                            .broadcast_to([P, 8, P]), rows.broadcast_to([P, 8, P]), ALU.is_equal))

            dve.engine_nop().then_inc(agg_done, 2)
            plain_hots(0, 0)
            plain_hots(0, 1)
            with loop(dve, GATE.steps // U - 1, (hots2, 2)) as i:
                for h in range(2):
                    dve.wait_ge(agg_ready, 2 * i + h + 1)
                    plain_hots(i + 1, h)
            dve.wait_ge(agg_done, 2 * (GATE.steps // U) + 2)
            for w in range(20):
                ch = G[:, 0:GATE.steps, w]
                link(dve.tensor_tensor_scan(ch, keep[:, 0:GATE.steps], ch, 0.0, ALU.mult, ALU.add))
            dve.wait_ge(gate_in, 96)
            with loop(dve, TILES // 7, (done, 7)) as i:
                _, lasts = nc.values_load_multi_w_load_instructions(
                    last_row[0:1, bass.ds(i * 7, 7)], engines=[mybir.EngineType.DVE],
                    min_val=0, max_val=GATE.steps - 1)
                for s in range(7):
                    done.add(dve.tensor_copy(sums[:, bass.ds((i * 7 + s), 1), :].rearrange("p o w -> p (o w)"),
                                             R1[:, bass.ds(lasts[s] * GW_IN, 20)]))
            dve.wait_ge(dve_done, done.n)
            dve.wait_ge(gates_need, 48)

            link(dve.tensor_scalar(den, sums[:, :, HE:HE + 4], 1e-16, None, ALU.add))
            link(dve.reciprocal(den, den))
            for hd in range(HEADS):
                link(dve.tensor_tensor(agg[:, :, hd * 4:hd * 4 + 4], sums[:, :, hd * 4:hd * 4 + 4],
                                       den[:, :, hd:hd + 1].broadcast_to([P, TILES, 4]), ALU.mult))

            def per_score(v):
                return v.rearrange("p (o n) -> p o n", o=1).broadcast_to([P, TILES, HE])

            link(dve.tensor_tensor(agg, agg, per_score(gat_bias), ALU.add))
            link(dve.tensor_reduce(mu, agg, AX.X, ALU.add))
            link(dve.tensor_scalar(mu, mu, 1.0 / HE, None, ALU.mult))
            mu3 = mu.rearrange("p (t o) -> p t o", o=1).broadcast_to([P, TILES, HE])
            link(dve.tensor_tensor(agg, agg, mu3, ALU.subtract))
            link(dve.tensor_tensor(squares, agg, agg, ALU.mult))
            link(dve.tensor_reduce(var, squares, AX.X, ALU.add))
            dve.tensor_scalar(var, var, 1.0 / HE, None, ALU.mult).then_inc(exp_ready, 1)
            dve.wait_ge(exp_done, CHUNKS + HEADS + 1)
            link(dve.reciprocal(mu, mu))
            link(dve.tensor_tensor(agg, agg, mu3, ALU.mult))
            link(dve.tensor_tensor(agg, agg, per_score(gamma), ALU.mult))
            link(dve.tensor_tensor(agg, agg, per_score(beta), ALU.add))
            link(dve.tensor_reduce(scores, agg.rearrange("p t (h e) -> p t e h", e=EXPERTS), AX.X, ALU.add))
            link(dve.tensor_scalar(scores, scores, 1.0 / HEADS, None, ALU.mult))
            link(dve.memset(beaten, 0.0))
            for i in range(EXPERTS):
                for j in range(i + 1, EXPERTS):
                    link(dve.tensor_tensor(var, scores[:, :, i], scores[:, :, j], ALU.is_ge))
                    link(dve.tensor_tensor(beaten[:, :, j], beaten[:, :, j], var, ALU.add))
                    link(dve.tensor_scalar(var, var, -1.0, 1.0, ALU.mult, ALU.add))
                    link(dve.tensor_tensor(beaten[:, :, i], beaten[:, :, i], var, ALU.add))
            link(dve.tensor_reduce(mu, scores, AX.X, ALU.max))
            mu4 = mu.rearrange("p (t o) -> p t o", o=1).broadcast_to([P, TILES, EXPERTS])
            dve.tensor_tensor(scores, scores, mu4, ALU.subtract).then_inc(exp_ready, 1)
            link(dve.tensor_scalar(beaten, beaten, 1.5, None, ALU.is_lt))
            dve.wait_ge(exp_done, CHUNKS + HEADS + 2)
            link(dve.tensor_tensor(beaten, beaten, gates, ALU.mult))
            link(dve.tensor_reduce(mu, beaten, AX.X, ALU.add))
            link(dve.reciprocal(mu, mu))
            link(dve.tensor_tensor(gates, beaten, mu4, ALU.mult))
            dve.engine_nop().then_inc(blocks_ready, 1)

            fins = Tally(fin_ready)

            def mix(t, s, n):
                dve.wait_ge(fin_in[s], 32 * n)
                for e in range(EXPERTS):
                    o = dve.scalar_tensor_tensor(mixed[:, s, :], yin[:, s, e * D:(e + 1) * D],
                                                 gates[:, bass.ds(t, 1), e:e + 1].rearrange("p o e -> p (o e)"),
                                                 x1in[:, s, :] if e == 0 else mixed[:, s, :], ALU.mult, ALU.add)
                    if e < EXPERTS - 1:
                        link(o)
                    else:
                        fins.add(o)

            with loop(dve, 24, (done, 12), (fins, 4)) as i:
                for s in range(4):
                    mix(4 * i + s, s, i + 1)
            for s in range(2):
                mix(96 + s, s, 25)

        @block.tensor
        def _(pe):
            asked = Tally(to_turn)

            def asked_for():
                pe.wait_ge(to_turn, asked.pass_by())

            pe.wait_ge(consts_in, 64)
            pe.wait_ge(w_in, 16 * 7)
            pe.wait_ge(dve_done, 2)
            for k in range(4):
                kd, kn = k % 2, k // 2
                pe.transpose(ps[:, 2048 + k * P:2048 + (k + 1) * P], w_nat[:, kn, kd * P:(kd + 1) * P],
                             ident[:, :]).then_inc(prep_turned, 1)
            for kd in range(2):
                for kn in range(2):
                    pe.matmul(ps[:, 2560 + 2 * kd:2562 + 2 * kd], w_nat[:, kn, kd * P:(kd + 1) * P], wa[:, kn, :],
                              start=kn == 0, stop=kn == 1)
            for kn in range(2):
                ins = pe.matmul(ps[0:1, 3072:3074], bcol[:, kn:kn + 1], wa[:, kn, :], start=kn == 0, stop=kn == 1)
            ins.then_inc(prep_turned, 1)
            pe.wait_ge(proj_ready, 1)

            def node_linear(phase):
                base, width = phase * TILES, (258, GW_IN)[phase]
                weights = (proj, gate_w)[phase]

                def pair(i, first):
                    for s in range(2):
                        t = i * 2 + s
                        pe.wait_ge(xn_ready, base + t + 1)
                        if not first:
                            pe.wait_ge(xT_ready, base + t - 1)
                        for k in range(2):
                            ins = pe.transpose(psT[s][:, k * P:(k + 1) * P], xn[s][:, k * P:(k + 1) * P], ident[:, :])
                        ins.then_inc(xn_turned, 1)
                    for s in range(2):
                        t = i * 2 + s
                        pe.wait_ge(xT_ready, base + t + 1)
                        if not first:
                            pe.wait_ge(lin_copied, base + t - 1)
                        for k in range(2):
                            ins = pe.matmul(psL[s][:, 0:width], xT[s][:, k * P:(k + 1) * P], weights[:, k, 0:width],
                                            start=k == 0, stop=phase == 1 and k == 1)
                        if phase == 0:
                            ins = pe.matmul(psL[s], ones_row[:, :], bias_row[:, :], start=False, stop=True)
                        ins.then_inc(lin_ready, 1)

                pair(0, True)
                with pe.Fori(1, NP2) as i:
                    pair(i, False)

            node_linear(0)
            def sort_turns():
                for c in turn_buffers():
                    asked_for()
                    for i in range(16):
                        ins = pe.transpose(ps[:, i * P:(i + 1) * P], sort_bufs[c][:, i * P:(i + 1) * P], ident[:, :])
                        if i in (7, 15):
                            ins.then_inc(turned, 1)

            def turn(source, g):
                asked_for()
                v = source.rearrange("p (k j) -> p j k", j=g.jj)
                for j in range(g.jj):
                    ins = pe.transpose(ps[:, j * P:(j + 1) * P], v[:, j, :], ident[:, :])
                ins.then_inc(turned, 1)

            def turn_back(source, g):
                asked_for()
                for j in range(g.jj):
                    ins = pe.transpose(ps[:, j * P:(j + 1) * P], source[:, j * P:(j + 1) * P], ident[:, :])
                ins.then_inc(turned, 1)

            def carries():
                asked_for()
                pe.transpose(ps[0:1, 0:P], col[:, 0:1], ident[:, :])
                pe.transpose(ps[0:1, P:2 * P], col[:, 1:2], ident[:, :]).then_inc(turned, 1)

            def carry_back(first):
                asked_for()
                pe.matmul(ps[:, 0:1], carry[0:1, first:first + P], ident[0:1, 0:1],
                          start=True, stop=True).then_inc(turned, 1)

            def first_flags():
                asked_for()
                pe.transpose(ps[0:1, 0:P], col[:, 0:1], ident[:, :]).then_inc(turned, 1)
                carry_back(0)

            def attention_turns():
                carries(); carry_back(0)
                carries(); carry_back(0)
                carries(); carry_back(1)

            sort_turns()
            sort_turns()

            def chunk(c, turns):
                asked_for()
                pe.transpose(ps[:, 0:P], c_keys, ident[:, :])
                pe.transpose(ps[:, 512:512 + P], c_scores, ident[:, :]).then_inc(turned, 1)
                carries(); carry_back(0)
                attention_turns()
                asked_for()
                pe.transpose(ps[:, 0:P], c_scan[11], ident[:, :])
                pe.matmul(ps[:, 512:514], ones_row[:, :], joined[:, :], start=True, stop=True).then_inc(turned, 1)
                with pe.Fori(0, turns) as i:
                    for s in range(32):
                        q = c * P + i * 32 + s
                        pe.wait_ge(hot_ready, q + 1)
                        if s % 8 == 0:
                            pe.wait_ge(rows_in[s // 8], (c * (P // 32) + i + 1) * 16)
                        pe.wait_ge(added, q + 1)
                        pe.matmul(ps[:, (s % 8) * 512:(s % 8) * 512 + 257], hot[:, s % U, :],
                                  gbuf[s // U][:, s % U, :], start=True, stop=True).then_inc(summed, 1)

            with loop(pe, CHUNKS - 1, (asked, CHUNK_ASKS)) as c:
                chunk(c, P // 32)
            chunk(CHUNKS - 1, LAST_STEPS // 32)

            pe.wait_ge(gate_w_ready, 1)
            pe.wait_ge(added, GNN.steps + 8)
            node_linear(1)

            pe.wait_ge(weights_in, 16 * 5)
            pe.wait_ge(lin_copied, 2 * TILES)

            def hidden(n, e, s, first):
                for f in range(4):
                    if not first:
                        pe.wait_ge(gelu_done, (n - 2) * 4 + (f | 1) + 1)
                    for k in range(2):
                        ins = pe.matmul(ps[:, (e % 2) * 1024 + f * 256:(e % 2) * 1024 + (f + 1) * 256],
                                        w1[:, k, e * HID + f * P:e * HID + (f + 1) * P],
                                        xe[:, s, :, k, :], start=k == 0, stop=k == 1)
                    ins.then_inc(hid_ready, 1)

            def outputs(n, e, first):
                pe.wait_ge(gelu_done, (n + 1) * 4)
                if not first:
                    pe.wait_ge(y_copied, n - 3)
                for t in range(2):
                    for f in range(4):
                        ins = pe.matmul(ps[:, 2048 + e * 512 + t * 256:2048 + e * 512 + (t + 1) * 256],
                                        hidT[:, e % 2, f, t * P:(t + 1) * P], w2[:, 4 * e + f, :],
                                        start=f == 0, stop=f == 3)
                ins.then_inc(y_ready, 1)

            def group(g, s, first_group, i=None):
                for e in range(EXPERTS):
                    n = g * EXPERTS + e
                    if e < EXPERTS - 1:
                        hidden(n + 1, e + 1, s, first_group and e + 1 < 2)
                    elif i is not None:
                        pe.wait_ge(xe_in[1 - s], 16 * (i + 1 + s))
                        hidden(n + 1, 0, 1 - s, False)
                    outputs(n, e, first_group)

            pe.wait_ge(xe_in[0], 16)
            hidden(0, 0, 0, True)
            group(0, 0, True, 0)
            group(1, 1, False, 0)
            with pe.Fori(1, GROUPS // 2) as i:
                for s in range(2):
                    group(i * 2 + s, s, False, i)
            group(GROUPS - 1, 0, False)

            turn(FK[:, :], GATE)
            first_flags()
            for hd in range(HEADS):
                turn(G[:, :, HE + hd], GATE)
                turn(G[:, :, HE + 4 + hd], GATE)
                attention_turns()
                turn_back(f_scan[10], GATE)
            with pe.Fori(0, GATE.steps // U) as i:
                for h in range(2):
                    pe.wait_ge(hot_ready, GNN_HOTS + 2 * i + h + 1)
                    pe.wait_ge(agg_done, 2 * i + h + 1)
                    for s in range(8):
                        ins = pe.matmul(ps[:, h * 512 + s * 20:h * 512 + (s + 1) * 20], hot[:, 8 * h + s, :],
                                        G[:, bass.ds(i * U + 8 * h + s, 1), 0:20].rearrange("p o w -> p (o w)"),
                                        start=True, stop=True)
                    ins.then_inc(agg_ready, 1)


def shape_constants():
    part = np.arange(P)

    def sign(k):
        return np.where((part >> (k - 11)) & 1, -1.0, 1.0)

    signs = np.stack([sign(11)] + [sign(k) * sign(k - 1) for k in range(12, 19)], axis=1)
    return {
        "ident": np.eye(P, dtype=np.float32),
        "iota_row": np.tile(part.astype(np.float32), (P, 1)),
        "signs": signs.astype(np.float32),
        "part_id": part.astype(np.float32)[:, None],
        "headers": np.arange(NODES, dtype=np.int32).reshape(HEADER_PARTS, HEADERS),
    }


def kernel(**inputs):
    import concourse.bacc as bacc
    from concourse.bass_utils import run_bass_kernel_spmd

    nc = bacc.Bacc("TRN2", target_bir_lowering=False, num_devices=1)
    arrays, a, consts = {}, {}, {}
    for full, array in inputs.items():
        name = full.removeprefix("L0_gnn_").removeprefix("L0_ffn_")
        array = np.ascontiguousarray(array)
        arrays[f"in_{name}"] = array
        a[name] = nc.dram_tensor(f"in_{name}", array.shape, mybir.dt.from_np(array.dtype), kind="ExternalInput").ap()
    for name, array in shape_constants().items():
        arrays[f"const_{name}"] = array
        consts[name] = nc.dram_tensor(f"const_{name}", array.shape, mybir.dt.from_np(array.dtype),
                                      kind="ExternalInput").ap()
    out = nc.dram_tensor("out", (NODES, D), FP32, kind="ExternalOutput").ap()
    program(nc, a, out, consts)
    return run_bass_kernel_spmd(nc, [arrays], core_ids=[0]).results[0]["out"]
```

```python
from contextlib import ExitStack, contextmanager

import numpy as np

import concourse.bass as bass
from concourse import mybir

FP32 = mybir.dt.float32
I32 = mybir.dt.int32
BF16 = mybir.dt.bfloat16
ALU = mybir.AluOpType
ACT = mybir.ActivationFunctionType
AX = mybir.AxisListType

P = 128
NODES = 12500
D = 256
TILES = -(-NODES // P)
PADDED = TILES * P
LAST = NODES - (TILES - 1) * P
W = 2048
HEADER_PARTS = 125
HEADERS = NODES // HEADER_PARTS
EXPERTS, HEADS, HID = 4, 4, 512
HE = HEADS * EXPERTS
EPS = 1e-5
BIG = 1e30
TAG = 0x20000000
TAG_FLOAT = float(np.array([TAG], np.int32).view(np.float32)[0])
LOW = (1 << 14) - 1
PAD_ROW = PADDED - 1
GW_IN = 24
ROW = D + 1
U = 16


class Graph:
    def __init__(self, edges):
        self.edges = edges
        self.tiles = -(-(edges + NODES) // P)
        self.cols = 16 * -(-self.tiles // 16)
        self.steps = U * -(-(self.tiles + TILES - 1) // U)
        self.jj = -(-(self.cols + TILES) // P)
        self.q = self.jj * P


GNN, GATE = Graph(212500), Graph(131072)
CHUNKS = -(-GNN.steps // P)
LAST_STEPS = GNN.steps - (CHUNKS - 1) * P
CHUNK_ASKS, CHUNK_DONE = 10, 62
EXP_FIRST, EXP_EVERY, EXP_MEANWHILE = 36, 6, 13


class Tally:

    def __init__(self, sem, start=0):
        self.sem, self.base, self.local = sem, start, 0
        self.made = 0

    def add(self, ins, k=1):
        ins.then_inc(self.sem, k)
        return self.pass_by(k)

    def pass_by(self, k=1):
        self.local += k
        self.made += k
        return self.n

    @property
    def n(self):
        return self.base + self.local


@contextmanager
def loop(eng, count, *tallies):
    starts, made = [t.n for t, _ in tallies], [t.made for t, _ in tallies]
    with eng.Fori(0, count) as i:
        for (t, per), s in zip(tallies, starts):
            t.base, t.local = s + i * per, 0
        yield i
    for (t, per), s, m in zip(tallies, starts, made):
        assert t.made - m == per, (t.made - m, per)
        t.base, t.local, t.made = s + count * per, 0, m + count * per


def halves(v, j):
    x = v.rearrange("p (x b l) -> p x b l", b=2, l=1 << j)
    return x[:, :, 0, :], x[:, :, 1, :]


def turn_buffers():
    c, order = 0, []
    for k in range(1, 11):
        c = (c + k) % 2
    c = (c + 1 + 11) % 2
    for k in range(12, 19):
        c = (c + 1) % 2
        order.append(c)
        c = (c + 1 + (k - 12)) % 2
        order.append(c)
        c = (c + 1 + 10) % 2
    order.append(c)
    return order


def program(nc, a, out, consts):
    ctx = ExitStack()
    with ctx:
        def sb(name, shape, dt=FP32):
            return ctx.enter_context(nc.sbuf_tensor(name, shape, dt))

        def sem(name):
            return ctx.enter_context(nc.semaphore(name))

        def dram(name, shape, dt=FP32):
            return nc.dram_tensor(name, shape, dt, kind="Internal").ap()

        h_table = dram("h_table", (2 * PADDED, ROW))
        stash = dram("stash", (GNN.steps // 8, P, 8, D))
        x1_rows = dram("x1_rows", (PADDED, D))
        xT_tiles = dram("xT_tiles", (TILES, P, 2 * P))
        gate_table = dram("gate_table", (PADDED, GW_IN))
        y_rows = dram("y_rows", (PADDED, EXPERTS * D))
        gate_blocks = dram("gate_blocks", (P, GATE.jj), I32)
        gate_blocks_f = dram("gate_blocks_f", (1, GATE.q))
        last_steps = dram("last_steps", (TILES, 1), I32)

        R1 = sb("R1", [P, GATE.q * GW_IN])
        WK = sb("WK", [P, 17552])
        FK = sb("FK", [P, GATE.q])
        FI = sb("FI", [P, GATE.q])
        S, E, A = WK[:, 0:4112], WK[:, 4112:11792], WK[:, 11792:17552]
        sort_bufs = [S[:, 0:W], S[:, W:2 * W]]
        spare = E[:, 0:1024]
        XR = R1[:, 0:TILES * D].rearrange("p (t d) -> p t d", d=D)
        ACC = R1[:, 0:TILES * 257].rearrange("p (t d) -> p t d", d=257)
        G = R1[:, :].rearrange("p (q w) -> p q w", w=GW_IN)
        KS = A[:, 0:GNN.q]
        GI, SC = A[:, GNN.q:2 * GNN.q], A[:, 2 * GNN.q:3 * GNN.q]
        ident, iota_row = sb("ident", [P, P]), sb("iota_row", [P, P])
        signs, part_id = sb("signs", [P, 8]), sb("part_id", [P, 1])
        stat = sb("stat", [P, TILES, 2])
        rstd, shift = sb("rstd", [P, TILES]), sb("shift", [P, TILES])
        eps = sb("eps", [P, 1])
        att, att_prod = sb("att", [P, 2, HE]), sb("att_prod", [P, 2, HE])
        gate_w = sb("gate_w", [P, 2, GW_IN])
        idx_slots = sb("idx_slots", [P, U], I32)
        waited, zero = sb("waited", [P, 2 * GNN.steps // U]), sb("zero", [P, 1])
        effects = sb("effects", [P, 3])
        ones_row = sb("ones_row", [1, P])
        state = sb("state", [1, 4])
        joined, factor = sb("joined", [1, 2]), sb("factor", [P, 4])
        joined_block = sb("joined_block", [1, 1], I32)
        step_blocks = sb("step_blocks", [1, P], I32)
        col, row, carry = sb("col", [P, 2]), sb("row", [1, 2 * P]), sb("carry", [1, P + 1])
        ccol = sb("ccol", [P, 1])
        ps = ctx.enter_context(nc.psum_tensor("ps", [P, 8 * 512], FP32))

        nb = A[:, GNN.q:]
        xn = [nb[:, s * 256:(s + 1) * 256] for s in range(2)]
        xT = [nb[:, 512 + s * 256:768 + s * 256] for s in range(2)]
        lin = [nb[:, 1024 + s * 258:1024 + (s + 1) * 258] for s in range(2)]
        w_nat = nb[:, 1540:2052].rearrange("p (k d) -> p k d", k=2)
        wa = nb[:, 2052:2056].rearrange("p (k w) -> p k w", k=2)
        bcol = nb[:, 2056:2058]
        ba = nb[0:1, 2058:2060]
        proj = nb[:, 2400:2916].rearrange("p (k n) -> p k n", k=2)
        bias_row = nb[0:1, 2916:3174]
        bn = E[:, 1024:1024 + 6 * TILES].rearrange("p (t s) -> p t s", s=6)
        psT = [ps[:, 2048 + s * 512:2048 + s * 512 + 256] for s in range(2)]
        psL = [ps[:, 3072 + s * 512:3072 + s * 512 + 258] for s in range(2)]

        consts_in, w_in = sem("consts_in"), sem("w_in")
        x_in = [sem(f"x_in{c}") for c in range(7)]
        filled, keys_in = sem("filled"), sem("keys_in")
        dve_done, to_turn, turned = sem("dve_done"), sem("to_turn"), sem("turned")
        stat_ready, std_ready = sem("stat_ready"), sem("std_ready")
        prep_turned, prep_copied, proj_ready = sem("prep_turned"), sem("prep_copied"), sem("proj_ready")
        xn_ready, xn_turned, xT_ready = sem("xn_ready"), sem("xn_turned"), sem("xT_ready")
        lin_ready, lin_copied = sem("lin_ready"), sem("lin_copied")
        rows_out = [sem(f"rows_out{s}") for s in range(2)]
        stashed = [sem(f"stashed{h}") for h in range(2)]
        rows_in = [sem(f"rows_in{h}") for h in range(4)]
        scores_kept = sem("scores_kept")
        idx_ready, idx_staged = sem("idx_ready"), sem("idx_staged")
        landed = [sem(f"landed{s}") for s in range(U)]
        rows_kept = sem("rows_kept")
        blocks_ready = sem("blocks_ready")
        hot_ready, summed, added = sem("hot_ready"), sem("summed"), sem("added")
        ones_set = sem("ones_set")
        residual_in = [sem(f"residual_in{s}") for s in range(2)]
        residual_last = sem("residual_last")
        residual_used, x1_out = sem("residual_used"), sem("x1_out")
        gate_w_in, gate_w_ready = sem("gate_w_in"), sem("gate_w_ready")
        norm_ready, norm_turned, xT7_ready = sem("norm_ready"), sem("norm_turned"), sem("xT7_ready")
        table_summed, table_ready = sem("table_summed"), sem("table_ready")
        xT7_out, table_out = ([sem(f"{n}{s}") for s in range(2)] for n in ("xT7_out", "table_out"))
        weights_in = sem("weights_in")
        xe_in = [sem(f"xe_in{s}") for s in range(2)]
        hid_ready, gelu_done = sem("hid_ready"), sem("gelu_done")
        y_ready, y_copied = sem("y_ready"), sem("y_copied")
        y_out = [sem(f"y_out{s}") for s in range(2)]
        exp_ready, exp_done = sem("exp_ready"), sem("exp_done")
        agg_ready, agg_done = sem("agg_ready"), sem("agg_done")
        head_weights, running_sums, sums_taken = sem("head_weights"), sem("running_sums"), sem("sums_taken")
        messages_ready, high_ready, rest_ready = sem("messages_ready"), sem("high_ready"), sem("rest_ready")
        middle_ready, low_ready = sem("middle_ready"), sem("low_ready")
        gate_in, gates_need = sem("gate_in"), sem("gates_need")
        fin_in = [sem(f"fin_in{s}") for s in range(6)]
        fin_ready = sem("fin_ready")
        fin_out = [sem(f"fin_out{s}") for s in range(6)]

        block = ctx.enter_context(nc.Block())
        NP2 = TILES // 2
        GATE_KEPT = 2 * GATE.steps // U

        f_scan = [WK[:, i * GATE.q:(i + 1) * GATE.q] for i in range(13)]
        R1_FREE = TILES * 257
        first_rows = R1[:, R1_FREE:R1_FREE + U * ROW].rearrange("p (s w) -> p s w", w=ROW)
        row_bufs = [v.rearrange("p (s w) -> p s w", w=257) for v in
                (S[:, 0:U * 257], E[:, 2048:2048 + U * 257])]
        hot = E[:, 0:U * P].rearrange("p (s n) -> p s n", n=P)
        c_scan = [R1[:, R1_FREE + U * ROW + i * P:R1_FREE + U * ROW + (i + 1) * P] for i in range(8)]
        c_scan += [E[:, 6160 + i * P:6160 + (i + 1) * P] for i in range(8)]
        c_keys, c_scores, c_rows, c_weights = c_scan[12:16]
        gate_slots = WK[:, 16640:16640 + U * GW_IN].rearrange("p (s w) -> p s w", w=GW_IN)
        xin = [E[:, 4096 + s * 1792:4096 + (s + 1) * 1792].rearrange("p (t d) -> p t d", d=D)
               for s in range(2)]
        SEVEN = 7
        SEVENS = TILES // SEVEN
        norm7 = [S[:, s * 2048:s * 2048 + SEVEN * D] for s in range(2)]
        xT7 = [A[:, s * 2048:s * 2048 + SEVEN * D] for s in range(2)]
        table7 = [E[:, s * 512:s * 512 + SEVEN * GW_IN] for s in range(2)]
        ps7 = [ps[:, 2048 + s * 512:2048 + s * 512 + SEVEN * GW_IN] for s in range(2)]
        w1 = WK[:, 0:4096].rearrange("p (k f) -> p k f", k=2)
        w2 = WK[:, 4096:8192].rearrange("p (c d) -> p c d", d=D)
        hidT = WK[:, 8192:10240].rearrange("p (s f n) -> p s f n", s=2, f=4)
        xe = WK[:, 10240:11264].rearrange("p (s t k n) -> p s t k n", s=2, t=2, k=2)
        ystage = WK[:, 11264:15360].rearrange("p (s t e d) -> p s t e d", s=2, t=2, e=EXPERTS)
        b2_all = WK[:, 15360:16384].rearrange("p (e d) -> p e d", e=EXPERTS)
        b1_cols = sb("b1_cols", [P, 16])
        keep, block_rows = FI, f_scan[12]
        last_col, last_row = sb("last_col", [P, 1], I32), sb("last_row", [1, TILES], I32)

        plain_hot = E[:, 0:U * P // 2].bitcast(BF16).rearrange("p (s n) -> p s n", n=P)
        parts = WK[:, 16640:17120].bitcast(BF16).rearrange("p (h s k w) -> p h s k w", h=2, k=3, w=20)
        rest = WK[:, 17120:17440].rearrange("p (h s w) -> p h s w", h=2, w=20)

        def last_sums(eng, kind, i):
            _, lasts = nc.values_load_multi_w_load_instructions(
                last_row[0:1, bass.ds(i * 7, 7)], engines=[kind], min_val=0, max_val=GATE.steps - 1,
                skip_runtime_bounds_check_because="a count of steps minus one, raised to zero at least")
            copy = eng.tensor_copy if kind == mybir.EngineType.DVE else eng.copy
            for s in range(7):
                copy(sums[:, bass.ds(i * 7 + s, 1), :].rearrange("p o w -> p (o w)"),
                     R1[:, bass.ds(lasts[s] * GW_IN, 20)]).then_inc(sums_taken, 1)

        def messages(eng, hd):
            part = G[:, :, hd * 4:hd * 4 + 4]
            return eng.tensor_tensor(part, part, G[:, :, HE + hd:HE + hd + 1].broadcast_to([P, GATE.q, 4]), ALU.mult)

        def tiles_of(first, n):
            return WK[:, first:first + TILES * n].rearrange("p (t n) -> p t n", n=n)

        sums, agg, squares = tiles_of(6400, 20), tiles_of(8400, HE), tiles_of(10000, HE)
        den, scores, gates, beaten = (tiles_of(11600 + 400 * i, 4) for i in range(4))
        mu, var = WK[:, 13200:13200 + TILES], WK[:, 13300:13300 + TILES]
        gat_bias, gamma, beta = (WK[:, 13400 + HE * i:13400 + HE * (i + 1)] for i in range(3))
        MIXED, RING = 4, 6
        mix_bufs = [R1[:, s * 5120:(s + 1) * 5120] for s in range(RING)]
        yin = [v[:, 0:4096].rearrange("p (t n) -> p t n", t=MIXED) for v in mix_bufs]
        x1in = [v[:, 4096:5120].rearrange("p (t d) -> p t d", t=MIXED) for v in mix_bufs]
        MIXES = TILES // MIXED
        GROUPS = TILES // 2

        @block.sync
        def _(sp):
            for dst_, src_ in ((ident, consts["ident"]), (iota_row, consts["iota_row"]),
                               (signs, consts["signs"]), (part_id, consts["part_id"])):
                sp.dma_start(dst_[:, :], src_).then_inc(consts_in, 16)
            sp.wait_ge(filled, 4)

            def load_keys(rows, cols, parts):
                n = rows.shape[0] // parts
                r, c = (sort_bufs[i].bitcast(I32) for i in range(2))
                sp.dma_start(r[0:parts, 0:n], rows.rearrange("(p c) -> p c", p=parts)).then_inc(keys_in, 16)
                sp.dma_start(c[0:parts, 0:n], cols.rearrange("(p c) -> p c", p=parts)).then_inc(keys_in, 16)
                sp.dma_start(r[0:HEADER_PARTS, n:n + HEADERS], consts["headers"]).then_inc(keys_in, 16)

            load_keys(a["src"], a["dst"], HEADER_PARTS)
            x_tiles = a["x"][0:(TILES - 1) * P, :].rearrange("(t p) d -> p t d", p=P)
            for c in range(7):
                n = 14 if c < 6 else 13
                sp.dma_start(XR[:, 14 * c:14 * c + n, :], x_tiles[:, 14 * c:14 * c + n, :]).then_inc(x_in[c], 16)
            sp.dma_start(XR[0:LAST, TILES - 1, :], a["x"][(TILES - 1) * P:, :]).then_inc(x_in[6], 16)
            sp.dma_start(w_nat, a["W_layer"].rearrange("(k p) d -> p k d", p=P)).then_inc(w_in, 16)
            for i, name in enumerate(("w_a2", "w_a1")):
                sp.dma_start(wa[:, :, i], a[name][0, :].rearrange("(k p) -> p k", p=P),
                         allow_slow_non_contiguous=True).then_inc(w_in, 16)
            sp.dma_start(bcol, a["b_layer"].rearrange("(k p) -> p k", p=P),
                         allow_slow_non_contiguous=True).then_inc(w_in, 16)
            sp.dma_start(bias_row[0:1, 0:D], a["b_layer"].rearrange("(o n) -> o n", o=1)).then_inc(w_in, 16)
            for i, name in enumerate(("b_a2", "b_a1")):
                sp.dma_start(ba[:, i:i + 1], a[name].rearrange("(o n) -> o n", o=1)).then_inc(w_in, 16)

            def rows(table, width, base, pair):
                for s in range(2):
                    sp.wait_ge(lin_copied, base + pair * 2 + s + 1)
                    sp.dma_start(table[bass.ds((pair * 2 + s) * P, P), :], lin[s][:, 0:width]).then_inc(rows_out[s], 16)
                    if table is h_table:
                        sp.dma_start(table[bass.ds((pair * 2 + s) * P + PADDED, P), :],
                                     lin[s][:, 1:1 + width]).then_inc(rows_out[s], 16)

            with sp.Fori(0, NP2) as i:
                rows(h_table, ROW, 0, i)
            sp.wait_ge(filled, 8)
            load_keys(a["edge_index"][1, :], a["edge_index"][0, :], P)
            sp.dma_start(gate_w[:, :, 0:HE], a["W_gat"].rearrange("(k p) n -> p k n", p=P)).then_inc(gate_w_in, 16)
            for w, name in enumerate(("att_src", "att_dst")):
                sp.dma_start(att[:, w, :], a[name].rearrange("h e -> (h e)").partition_broadcast(P)).then_inc(gate_w_in, 16)

            sp.wait_ge(ones_set, 1)

            def rows_back(j, h):
                sp.wait_ge(stashed[h % 2], (2 * j + h // 2 + 1) * 16)
                sp.dma_start(row_bufs[h // 2][:, 8 * (h % 2):8 * (h % 2) + 8, 0:D],
                             stash[bass.ds(4 * j + h, 1)].rearrange("o p s d -> p (o s) d")).then_inc(rows_in[h], 16)

            for h in range(4):
                rows_back(0, h)
            with sp.Fori(1, GNN.steps // 32) as i:
                for h in range(4):
                    sp.wait_ge(summed, (i - 1) * 32 + 8 * h + 8)
                    rows_back(i, h)

            sp.wait_ge(summed, GNN.steps)
            for s in range(2):
                sp.dma_start(xin[s], x_tiles[:, 7 * s:7 * s + 7, :]).then_inc(residual_in[s], 16)
            with sp.Fori(0, 5) as i:
                for s in range(2):
                    sp.wait_ge(residual_used, 2 * i + s + 1)
                    sp.dma_start(xin[s], x_tiles[:, bass.ds((2 * i + 2 + s) * 7, 7), :]).then_inc(residual_in[s], 16)
            sp.wait_ge(residual_used, 11)
            sp.dma_start(xin[0], x_tiles[:, 84:91, :]).then_inc(residual_in[0], 16)
            sp.wait_ge(residual_used, 12)
            sp.dma_start(xin[1][:, 0:6, :], x_tiles[:, 91:97, :]).then_inc(residual_in[1], 16)
            sp.dma_start(xin[1][0:LAST, 6, :], a["x"][(TILES - 1) * P:, :]).then_inc(residual_last, 16)
            x1_view = x1_rows.rearrange("(t p) d -> p t d", p=P)
            for c in range(7):
                sp.wait_ge(residual_used, 2 * c + 2)
                sp.dma_start(x1_view[:, 14 * c:14 * c + 14, :], ACC[:, 14 * c:14 * c + 14, 0:D]).then_inc(x1_out, 16)

            table_view = gate_table.rearrange("(t p) w -> p t w", p=P)
            with sp.Fori(0, SEVENS // 2) as i:
                for s in range(2):
                    g = 2 * i + s
                    sp.wait_ge(xT7_ready, 4 * g + 4)
                    sp.dma_start(xT_tiles[bass.ds(g * SEVEN, SEVEN), :, :].rearrange("t p n -> p t n"),
                                 xT7[s].rearrange("p (t n) -> p t n", t=SEVEN)).then_inc(xT7_out[s], 16)
                    sp.wait_ge(table_ready, g + 1)
                    sp.dma_start(table_view[:, bass.ds(g * SEVEN, SEVEN), :],
                                 table7[s].rearrange("p (t w) -> p t w", t=SEVEN)).then_inc(table_out[s], 16)

            sp.wait_ge(x1_out, 16 * 7)
            for s in range(2):
                sp.wait_ge(table_out[s], 16 * (SEVENS // 2))
                sp.wait_ge(xT7_out[s], 16 * (SEVENS // 2))
            for k in range(2):
                sp.dma_start(w1[:, k, :].rearrange("p (e f) -> p e f", e=EXPERTS),
                             a["W1"].rearrange("e (k p) f -> k p e f", p=P)[k]).then_inc(weights_in, 16)
            sp.dma_start(w2, a["W2"].rearrange("e f d -> (e f) d").rearrange("(c p) d -> p c d", p=P)).then_inc(weights_in, 16)
            sp.dma_start(b1_cols[:, :], a["b1"].rearrange("e f -> (e f)").rearrange("(c p) -> p c", p=P),
                         allow_slow_non_contiguous=True).then_inc(weights_in, 16)
            sp.dma_start(b2_all.rearrange("p e d -> p (e d)"),
                         a["b2"].rearrange("e d -> (e d)").partition_broadcast(P)).then_inc(weights_in, 16)

            def load_xe(g, s):
                sp.dma_start(xe[:, s].rearrange("p t k n -> p t (k n)"),
                             xT_tiles[bass.ds(g * 2, 2), :, :].rearrange("t p n -> p t n")).then_inc(xe_in[s], 16)

            def store_y(g, s):
                sp.dma_start(y_rows[bass.ds(g * 2 * P, 2 * P), :].rearrange("(t p) n -> p t n", p=P),
                             ystage[:, s].rearrange("p t e d -> p t (e d)")).then_inc(y_out[s], 16)

            load_xe(0, 0)
            load_xe(1, 1)

            def next_group(g, s, load):
                sp.wait_ge(y_copied, (g + 1) * EXPERTS)
                store_y(g, s)
                if load:
                    load_xe(g + 2, s)

            with sp.Fori(0, GROUPS // 2 - 1) as i:
                for s in range(2):
                    next_group(i * 2 + s, s, True)
            next_group(GROUPS - 3, 0, True)
            next_group(GROUPS - 2, 1, False)
            next_group(GROUPS - 1, 0, False)

            sp.wait_ge(blocks_ready, 1)
            sp.dma_start(gate_blocks, f_scan[11][:, 0:GATE.jj].bitcast(I32)).then_inc(gate_in, 16)
            sp.wait_ge(gate_in, 16)
            sp.dma_start(f_scan[12][0:1, :].bitcast(I32), gate_blocks.rearrange("p (o j) -> o (p j)", o=1)).then_inc(gate_in, 16)
            sp.wait_ge(blocks_ready, 2)
            sp.dma_start(gate_blocks_f, f_scan[11][0:1, :]).then_inc(gate_in, 16)
            sp.wait_ge(gate_in, 48)
            sp.dma_start(block_rows, gate_blocks_f[0, :].partition_broadcast(P)).then_inc(gate_in, 16)
            sp.wait_ge(blocks_ready, 3)
            sp.dma_start(last_steps, last_col[0:TILES, :],
                         allow_slow_non_contiguous=True).then_inc(gate_in, 16)
            sp.wait_ge(gate_in, 80)
            sp.dma_start(last_row[:, :], last_steps.rearrange("t o -> o t"),
                         allow_slow_non_contiguous=True).then_inc(gate_in, 16)
            sp.wait_ge(blocks_ready, 4)
            for ap_, name in ((gat_bias, "b_gat"), (gamma, "ln_gamma"), (beta, "ln_beta")):
                sp.dma_start(ap_, a[name].partition_broadcast(P)).then_inc(gates_need, 16)

            for s in range(2):
                sp.wait_ge(y_out[s], 16 * (GROUPS // 2 + (1 - s)))
            sp.wait_ge(blocks_ready, 5)
            sp.wait_ge(rest_ready, 2 * (GATE.steps // U) + 1)

            def load_mix(g, s, n=MIXED):
                for buf, rows_ in ((yin[s], y_rows), (x1in[s], x1_rows)):
                    sp.dma_start(buf[:, 0:n, :], rows_[bass.ds(g * MIXED * P, n * P), :].rearrange(
                        "(t p) w -> p t w", p=P)).then_inc(fin_in[s], 16)

            for s in range(RING):
                load_mix(s, s)
            with sp.Fori(1, MIXES // RING) as i:
                for s in range(RING):
                    sp.wait_ge(fin_out[s], 16 * i)
                    load_mix(RING * i + s, s)
            sp.wait_ge(fin_out[0], 16 * (MIXES // RING))
            load_mix(MIXES, 0, 2)

        @block.gpsimd
        def _(pool):
            r, c = (sort_bufs[i].bitcast(I32) for i in range(2))
            pool.memset(zero[:, :], 0.0)
            pool.memset(r, PAD_ROW).then_inc(filled, 1)
            pool.memset(c, 0).then_inc(filled, 1)
            pool.memset(XR[:, TILES - 1, :], 0.0).then_inc(filled, 2)

            def gather(s, table, dest):
                pool.indirect_dma_start(dest, None, table,
                                        bass.IndirectOffsetOnAxis(ap=idx_slots[:, s:s + 1], axis=0)
                                        ).then_inc(landed[s], 16)

            for s in range(2):
                pool.wait_ge(rows_out[s], 32 * NP2)

            def gather_half(i, h, first):
                pool.wait_ge(idx_staged, 2 * i + h + 1)
                if not first:
                    pool.wait_ge(stashed[h], i * 16)
                    pool.wait_ge(scores_kept, 2 * i + h - 1)
                n = bass.ds(2 * i + h, 1) if not first else slice(h, h + 1)
                pool.tensor_tensor(waited[:, n], zero[:, :], zero[:, :], ALU.add)
                for s in range(8 * h, 8 * h + 8):
                    gather(s, h_table, first_rows[:, s, :])

            for h in range(2):
                gather_half(0, h, True)
            with pool.Fori(1, GNN.steps // U) as i:
                for h in range(2):
                    gather_half(i, h, False)

            for s in range(2):
                pool.wait_ge(table_out[s], 16 * (SEVENS // 2))
            pool.wait_ge(x1_out, 16 * 7)
            pool.wait_ge(norm_ready, TILES)
            pool.memset(R1[:, GATE.steps * GW_IN:], 0.0)
            turns, before = GATE.steps // U, GNN.steps // U
            staged, kept = Tally(idx_staged, 2 + 2 * before), Tally(rows_kept)

            def stage_gate(i, h):
                return staged.add(pool.tensor_copy(idx_slots[:, 8 * h:8 * h + 8],
                                                   FI.bitcast(I32)[:, bass.ds(i * U + 8 * h, 8)]))

            def keep_gate(i, h):
                for s in range(8 * h, 8 * h + 8):
                    pool.wait_ge(landed[s], (i + 1 + before) * 16)
                return kept.add(pool.tensor_copy(G[:, bass.ds(i * U + 8 * h, 8), :], gate_slots[:, 8 * h:8 * h + 8, :]))

            def gather_gate(h):
                pool.tensor_tensor(waited[:, 0:1], zero[:, :], zero[:, :], ALU.add)
                for s in range(8 * h, 8 * h + 8):
                    gather(s, gate_table, gate_slots[:, s, :])

            for h in range(2):
                pool.wait_ge(idx_staged, stage_gate(0, h))
                gather_gate(h)
            with loop(pool, turns - 1, (staged, 2), (kept, 2)) as i:
                for h in range(2):
                    at = keep_gate(i, h)
                    pool.wait_ge(idx_staged, stage_gate(i + 1, h))
                    pool.wait_ge(rows_kept, at)
                    gather_gate(h)
            for h in range(2):
                keep_gate(turns - 1, h)

            for hd in range(HEADS - 1):
                pool.wait_ge(head_weights, hd + 1)
                messages(pool, hd).then_inc(messages_ready, 1)

            def rest_of(i, h):
                pool.wait_ge(high_ready, 2 * i + h + 1)
                pool.tensor_tensor(rest[:, h], G[:, bass.ds(i * U + 8 * h, 8), 0:20], parts[:, h, :, 0, :],
                                   ALU.subtract).then_inc(rest_ready, 1)

            def low(i, h):
                pool.wait_ge(middle_ready, 2 * i + h + 1)
                pool.tensor_tensor(parts[:, h, :, 2, :], rest[:, h], parts[:, h, :, 1, :],
                                   ALU.subtract).then_inc(low_ready, 1)

            rest_of(0, 0)
            with pool.Fori(0, GATE.steps // U) as i:
                low(i, 0)
                rest_of(i, 1)
                low(i, 1)
                rest_of(i + 1, 0)

        @block.scalar
        def _(act):
            act.wait_ge(stat_ready, 1)
            act.activation(rstd[:, :], stat[:, :, 1], ACT.Sqrt, bias=eps[:, :]).then_inc(std_ready, 1)

            for k in range(4):
                act.wait_ge(prep_turned, 4)
                act.copy(proj[:, k % 2, (k // 2) * P:(k // 2 + 1) * P], ps[:, 2048 + k * P:2048 + (k + 1) * P]).then_inc(prep_copied, 1)
            act.wait_ge(prep_turned, 5)
            for kd in range(2):
                act.copy(proj[:, kd, D:D + 2], ps[:, 2560 + 2 * kd:2562 + 2 * kd]).then_inc(prep_copied, 1)
            act.copy(bias_row[0:1, D:D + 2], ps[0:1, 3072:3074]).then_inc(prep_copied, 1)

            act.wait_ge(std_ready, 2)

            def normalise(dest, src, t):
                return act.activation(dest, src[:, bass.ds(t, 1), 0:D].rearrange("p o d -> p (o d)"), ACT.Identity,
                                      bias=shift[:, bass.ds(t, 1)], scale=rstd[:, bass.ds(t, 1)])

            def norm_x(t, s, first=False):
                if not first:
                    act.wait_ge(xn_turned, t - 1)
                normalise(xn[s], XR, t).then_inc(xn_ready, 1)

            def keep_xT(t, s, first=False):
                act.wait_ge(xn_turned, t + 1)
                if not first:
                    act.wait_ge(lin_ready, t - 1)
                act.copy(xT[s], psT[s]).then_inc(xT_ready, 1)

            def keep_lin(t, s, i=None):
                act.wait_ge(lin_ready, t + 1)
                if i is not None:
                    act.wait_ge(rows_out[s], i * 32)
                act.copy(lin[s], psL[s]).then_inc(lin_copied, 1)

            norm_x(0, 0, True); norm_x(1, 1, True); keep_xT(0, 0, True)
            norm_x(2, 0); keep_xT(1, 1, True); keep_lin(0, 0)
            norm_x(3, 1); keep_xT(2, 0); keep_lin(1, 1)
            with act.Fori(1, NP2 - 1) as i:
                for s in range(2):
                    norm_x(2 * i + 2 + s, s)
                    keep_xT(2 * i + 1 + s, 1 - s)
                    keep_lin(2 * i + s, s, i)
            keep_xT(TILES - 1, 1)
            keep_lin(TILES - 2, 0, NP2 - 1)
            keep_lin(TILES - 1, 1, NP2 - 1)

            act.wait_ge(idx_ready, 1)

            def stage(i, h):
                act.copy(idx_slots[:, 8 * h:8 * h + 8], GI.bitcast(I32)[:, bass.ds(i * U + 8 * h, 8)]).then_inc(idx_staged, 1)

            def gathered(i):
                for h in range(2):
                    for s in range(8 * h, 8 * h + 8):
                        act.wait_ge(landed[s], (i + 1) * 16)
                    act.dma_start(stash[bass.ds(2 * i + h, 1)].rearrange("o p s d -> p (o s) d"),
                                  first_rows[:, 8 * h:8 * h + 8, 0:D]).then_inc(stashed[h], 16)
                    act.copy(SC[:, bass.ds(i * U + 8 * h, 8)],
                             first_rows[:, 8 * h:8 * h + 8, D]).then_inc(scores_kept, 1)
                    stage(i + 1, h)

            def chunk_exps(c):
                act.wait_ge(exp_ready, c + 1)
                act.activation(c_scan[11], c_scan[11], ACT.Exp)
                act.activation(joined[0:1, 0:1], joined[0:1, 0:1], ACT.Exp).then_inc(exp_done, 1)

            for h in range(2):
                stage(0, h)
            with act.Fori(0, EXP_FIRST) as i:
                gathered(i)
            with act.Fori(0, EXP_MEANWHILE) as c:
                chunk_exps(c)
                with act.Fori(0, EXP_EVERY) as i:
                    gathered(c * EXP_EVERY + EXP_FIRST + i)
            with act.Fori(EXP_FIRST + EXP_MEANWHILE * EXP_EVERY, GNN.steps // U) as i:
                gathered(i)
            with act.Fori(EXP_MEANWHILE, CHUNKS) as c:
                chunk_exps(c)

            act.wait_ge(stat_ready, 2)
            act.activation(rstd[:, :], stat[:, :, 1], ACT.Sqrt, bias=eps[:, :]).then_inc(std_ready, 1)
            act.wait_ge(std_ready, 4)

            def normalise_seven(g, s, first):
                if not first:
                    act.wait_ge(norm_turned, 4 * g - 4)
                for z in range(SEVEN):
                    normalise(norm7[s][:, z * D:(z + 1) * D], ACC, g * SEVEN + z).then_inc(norm_ready, 1)

            def keep_table(g, s, i):
                act.wait_ge(table_summed, g + 1)
                if i is not None:
                    act.wait_ge(table_out[s], i * 16)
                act.copy(table7[s], ps7[s]).then_inc(table_ready, 1)

            normalise_seven(0, 0, True)
            normalise_seven(1, 1, True)
            keep_table(0, 0, None)
            normalise_seven(2, 0, False)
            keep_table(1, 1, None)
            normalise_seven(3, 1, False)
            with act.Fori(1, SEVENS // 2 - 1) as i:
                for s in range(2):
                    keep_table(2 * i + s, s, i)
                    normalise_seven(2 * i + 2 + s, s, False)
            for s in range(2):
                keep_table(SEVENS - 2 + s, s, SEVENS // 2 - 1)

            act.wait_ge(weights_in, 16 * 5)
            act.preload_act_table(ACT.Gelu)

            def gelu(n, e, first):
                if not first:
                    act.wait_ge(y_ready, n - 1)
                for f in range(4):
                    act.wait_ge(hid_ready, n * 4 + (f | 1) + 1)
                    act.activation(hidT[:, e % 2, f, :], ps[:, (e % 2) * 1024 + f * 256:(e % 2) * 1024 + (f + 1) * 256],
                                   ACT.Gelu, bias=b1_cols[:, 4 * e + f:4 * e + f + 1]).then_inc(gelu_done, 1)

            for e in range(EXPERTS):
                gelu(e, e, e < 2)
            with act.Fori(1, GROUPS) as g:
                for e in range(EXPERTS):
                    gelu(g * EXPERTS + e, e, False)

            for hd in range(HEADS):
                act.wait_ge(exp_ready, CHUNKS + 1 + hd)
                act.activation(f_scan[10], f_scan[9], ACT.Exp).then_inc(exp_done, 1)

            act.wait_ge(messages_ready, HEADS)

            def high(i, h, first=False):
                if not first:
                    act.wait_ge(agg_ready, 2 * i + h - 1)
                act.copy(parts[:, h, :, 0, :], G[:, bass.ds(i * U + 8 * h, 8), 0:20]).then_inc(high_ready, 1)

            def middle(i, h):
                act.wait_ge(rest_ready, 2 * i + h + 1)
                act.copy(parts[:, h, :, 1, :], rest[:, h]).then_inc(middle_ready, 1)

            def keep_sums(i, h):
                act.wait_ge(agg_ready, 2 * i + h + 1)
                act.copy(G[:, bass.ds(i * U + 8 * h, 8), 0:20],
                         ps[:, h * 512:h * 512 + 160].rearrange("p (s w) -> p s w", w=20)).then_inc(agg_done, 1)

            high(0, 0, True)
            middle(0, 0)
            high(0, 1, True)
            middle(0, 1)
            high(1, 0)
            keep_sums(0, 0)
            with act.Fori(1, GATE.steps // U) as i:
                middle(i, 0)
                high(i, 1)
                keep_sums(i - 1, 1)
                middle(i, 1)
                high(i + 1, 0)
                keep_sums(i, 0)
            keep_sums(GATE.steps // U - 1, 1)

            act.wait_ge(running_sums, 1)
            with act.Fori(0, TILES // 14) as i:
                last_sums(act, mybir.EngineType.Activation, 2 * i + 1)

            act.wait_ge(exp_ready, CHUNKS + HEADS + 1)
            act.activation(mu, var, ACT.Sqrt, bias=eps[:, :]).then_inc(exp_done, 1)
            act.wait_ge(exp_ready, CHUNKS + HEADS + 2)
            act.activation(gates, scores, ACT.Exp).then_inc(exp_done, 1)

            with act.Fori(0, MIXES // RING) as i:
                for s in range(RING):
                    g = RING * i + s
                    act.wait_ge(fin_ready, MIXED * (g + 1))
                    act.dma_start(out[bass.ds(g * MIXED * P, MIXED * P), :].rearrange("(t p) d -> p t d", p=P),
                                  x1in[s]).then_inc(fin_out[s], 16)
            act.wait_ge(fin_ready, TILES)
            act.dma_start(out[(TILES - 2) * P:(TILES - 1) * P, :], x1in[0][:, 0, :]).then_inc(fin_out[0], 16)
            act.dma_start(out[(TILES - 1) * P:, :], x1in[0][0:LAST, 1, :]).then_inc(fin_out[0], 16)
            for s in range(RING):
                act.wait_ge(fin_out[s], 16 * (MIXES // RING + (0 if s else 2)))

        @block.vector
        def _(dve):
            done, ask = Tally(dve_done), Tally(to_turn)

            def link(ins, tally=None):
                tally = tally or done
                dve.wait_ge(tally.sem, tally.add(ins))

            back = Tally(turned)

            def answer(n=1):
                dve.wait_ge(turned, back.pass_by(n))

            dve.memset(eps[:, :], EPS).then_inc(dve_done, 1)
            dve.memset(ones_row[:, :], 1.0).then_inc(dve_done, 1)
            done.local = 2
            dve.wait_ge(consts_in, 64)

            for c in range(7):
                dve.wait_ge(x_in[c], 16 if c < 6 else 32)
                with loop(dve, 2, (done, 7)) as i:
                    for s in range(7):
                        t = 14 * c + 7 * i + s
                        done.add(dve.bn_stats(bn[:, bass.ds(t, 1), :].rearrange("p o s -> p (o s)"),
                                              XR[:, bass.ds(t, 1), :].rearrange("p o d -> p (o d)")))
            dve.wait_ge(dve_done, done.n)

            def statistics():
                mean, var_ = stat[:, :, 0], stat[:, :, 1]
                link(dve.tensor_tensor(var_, bn[:, :, 1], bn[:, :, 4], ALU.subtract))
                link(dve.tensor_tensor(mean, bn[:, :, 1], bn[:, :, 4], ALU.add))
                link(dve.tensor_scalar(mean, mean, 0.5, None, ALU.mult))
                link(dve.tensor_tensor(var_, var_, var_, ALU.mult))
                link(dve.tensor_tensor(bn[:, :, 2], bn[:, :, 2], bn[:, :, 5], ALU.add))
                link(dve.tensor_scalar(bn[:, :, 2], bn[:, :, 2], 1.0 / D, None, ALU.mult))
                link(dve.scalar_tensor_tensor(var_, var_, 0.25, bn[:, :, 2], ALU.mult, ALU.add))

            def scales(std_count):
                dve.wait_ge(std_ready, std_count)
                link(dve.reciprocal(rstd[:, :], rstd[:, :]))
                dve.scalar_tensor_tensor(shift[:, :], stat[:, :, 0], -1.0, rstd[:, :], ALU.mult, ALU.mult).then_inc(std_ready, 1)

            statistics()
            dve.engine_nop().then_inc(stat_ready, 1)
            scales(1)
            dve.wait_ge(prep_copied, 7)
            dve.wait_ge(w_in, 16 * 7)
            dve.tensor_add(bias_row[0:1, D:D + 2], bias_row[0:1, D:D + 2], ba).then_inc(proj_ready, 1)

            def sort(g):
                cur = [0]
                n = g.edges // (HEADER_PARTS if g is GNN else P)
                parts = HEADER_PARTS if g is GNN else P
                r, c = (sort_bufs[i].bitcast(I32) for i in range(2))
                link(dve.tensor_scalar(c[0:parts, 0:n], c[0:parts, 0:n], 1, None, ALU.add))
                link(dve.tensor_scalar(r, r, 14, TAG, ALU.logical_shift_left, ALU.bitwise_or))
                link(dve.tensor_tensor(r, r, c, ALU.bitwise_or))

                def stage(j, tally=None):
                    (lo, hi), (olo, ohi) = halves(sort_bufs[cur[0]], j), halves(sort_bufs[1 - cur[0]], j)
                    done.add(dve.tensor_tensor(olo, lo, hi, ALU.min))
                    link(dve.tensor_tensor(ohi, lo, hi, ALU.max), tally)
                    cur[0] = 1 - cur[0]

                def directed_stage(j, k):
                    split = dict(d=2, m=1 << (k - 1 - j), b=2, l=1 << j)
                    va, vb = (sort_bufs[x].rearrange("p (h d m b l) -> p h d m b l", **split)
                              for x in (cur[0], 1 - cur[0]))
                    for d in range(2):
                        lo, hi = va[:, :, d, :, 0, :], va[:, :, d, :, 1, :]
                        done.add(dve.tensor_tensor(vb[:, :, d, :, d, :], lo, hi, ALU.min))
                        done.add(dve.tensor_tensor(vb[:, :, d, :, 1 - d, :], lo, hi, ALU.max))
                    dve.wait_ge(dve_done, done.n)
                    cur[0] = 1 - cur[0]

                def flip(k, tally=None):
                    link(dve.tensor_scalar(sort_bufs[1 - cur[0]], sort_bufs[cur[0]], signs[:, k - 11:k - 10],
                                           None, ALU.mult), tally)
                    cur[0] = 1 - cur[0]

                for k in range(1, 11):
                    for j in range(k - 1, -1, -1):
                        directed_stage(j, k)
                flip(11)
                for j in range(10, -1, -1):
                    stage(j)
                for k in range(12, 19):
                    flip(k, ask)
                    m = k - 12
                    for h in range(2):
                        answer()
                        lo, hi = halves(ps[:, h * 1024:(h + 1) * 1024], m)
                        olo, ohi = halves(sort_bufs[1 - cur[0]][:, h * 1024:(h + 1) * 1024], m)
                        sv = spare[:, h * 512:(h + 1) * 512].rearrange("p (x l) -> p x l", l=1 << m)
                        link(dve.tensor_copy(sv, hi))
                        done.add(dve.tensor_tensor(olo, lo, sv, ALU.min))
                        link(dve.tensor_tensor(ohi, lo, sv, ALU.max), ask if m == 0 and h else None)
                    cur[0] = 1 - cur[0]
                    for mm in range(m - 1, -1, -1):
                        stage(mm, None if mm else ask)
                    answer(2)
                    o = sort_bufs[1 - cur[0]]
                    link(dve.tensor_copy(spare, ps[:, 1024:2048]))
                    done.add(dve.tensor_tensor(o[:, 0:1024], ps[:, 0:1024], spare, ALU.min))
                    link(dve.tensor_tensor(o[:, 1024:2048], ps[:, 0:1024], spare, ALU.max))
                    cur[0] = 1 - cur[0]
                    for j in range(9, -1, -1):
                        stage(j, ask if k == 18 and j == 0 else None)
                answer(2)

            def spread(g, keys):
                link(dve.memset(keys, 0.0))
                n = g.cols // 16
                link(dve.tensor_copy(keys[:, 0:g.cols].rearrange("p (q c) -> p c q", c=16),
                                     ps[:, 0:2048].rearrange("p (c q) -> p c q", c=16)[:, :, 0:n]))
                bufs = [E[:, i * g.q:(i + 1) * g.q].bitcast(I32) for i in range(4)]
                cu, at = keys.bitcast(I32), -1
                for bit in range(6, -1, -1):
                    by = 1 << bit
                    mask, moving = bufs[0], bufs[1]
                    at = 2 if at != 2 else 3
                    new = bufs[at]
                    link(dve.tensor_scalar(mask, cu, 31 - 21 - bit, 31, ALU.logical_shift_left, ALU.arith_shift_right))
                    link(dve.tensor_tensor(moving, cu, mask, ALU.bitwise_and))
                    link(dve.tensor_tensor(new, cu, moving, ALU.bitwise_xor))
                    o = new if bit else keys.bitcast(I32)
                    if not bit:
                        link(dve.tensor_copy(o[:, 0:by], new[:, 0:by]))
                    link(dve.tensor_tensor(o[:, by:], new[:, by:], moving[:, :-by], ALU.bitwise_or))
                    cu = o

            dve.wait_ge(filled, 4)
            dve.wait_ge(keys_in, 48)
            sort(GNN)
            spread(GNN, KS)

            def gather_index(g, keys, dest, scratch, last):
                k_int = keys.bitcast(I32)
                e0, e1, e2 = (scratch[:, i * g.q:(i + 1) * g.q].bitcast(I32) for i in range(3))
                link(dve.tensor_scalar(e0, k_int, LOW, None, ALU.bitwise_and))
                link(dve.tensor_scalar(e1, k_int, 14, LOW, ALU.logical_shift_right, ALU.bitwise_and))
                link(dve.tensor_scalar(e2, e0, 0, None, ALU.is_equal))
                link(dve.tensor_scalar(e1, e1, 1 + PADDED if g is GNN else 1, None, ALU.add))
                link(dve.tensor_tensor(e1, e1, e2, ALU.mult))
                link(dve.tensor_tensor(e0, e0, e1, ALU.add))
                last(dve.tensor_scalar(dest.bitcast(I32), e0, -1, 0, ALU.add, ALU.max))

            for s in range(2):
                dve.wait_ge(rows_out[s], 32 * NP2)
            gather_index(GNN, KS, GI, E, lambda ins: ins.then_inc(idx_ready, 1))
            link(dve.memset(SC[:, GNN.steps:], 0.0))

            r, c = (sort_bufs[i].bitcast(I32) for i in range(2))
            link(dve.memset(r, PAD_ROW))
            dve.memset(c, 0).then_inc(filled, 4)
            dve.wait_ge(filled, 8)
            dve.wait_ge(keys_in, 96)
            sort(GATE)
            spread(GATE, FK[:, :])
            gather_index(GATE, FK[:, :], FI[:, :], E, link)

            dve.wait_ge(gate_w_in, 48)
            for w in range(2):
                link(dve.tensor_tensor(att_prod[:, :, :], gate_w[:, :, 0:HE], att[:, w:w + 1, :].broadcast_to([P, 2, HE]), ALU.mult))
                link(dve.tensor_reduce(gate_w[:, :, HE + 4 * w:HE + 4 * w + 4],
                                       att_prod[:, :, :].rearrange("p k (h e) -> p k h e", e=EXPERTS), AX.X, ALU.add))
            dve.engine_nop().then_inc(gate_w_ready, 1)

            def to_scan(g, dest, source=None):
                answer()
                link(dve.tensor_copy(dest, ps[:, 0:g.q]))

            def seg_scan(res, d0, d1, op0, op1, neutral, reverse=False, state=None, effect=None):
                v = (lambda z: z[:, ::-1]) if reverse else (lambda z: z)
                end = 0 if reverse else res.shape[1] - 1
                link(dve.tensor_tensor_scan(v(res), v(d0), v(d1), neutral, op0, op1))
                link(dve.tensor_reduce(col[:, 1:2], d0, AX.X, ALU.min) if effect is None else
                     dve.tensor_copy(col[:, 1:2], effect))
                link(dve.tensor_copy(col[:, 0:1], res[:, end:end + 1]), ask)
                answer()
                link(dve.tensor_copy(row[:, :], ps[0:1, 0:2 * P]))
                start = P if reverse else 0
                if state is None:
                    link(dve.memset(carry[0:1, start:start + 1], neutral))
                else:
                    link(dve.tensor_copy(carry[0:1, 0:1], state))
                o = carry[0:1, 0:P] if reverse else carry[0:1, 1:P + 1]
                link(dve.tensor_tensor_scan(v(o), v(row[:, P:2 * P]), v(row[:, 0:P]),
                                            neutral if state is None else state, op0, op1), ask)
                if state is not None:
                    link(dve.tensor_copy(state, carry[0:1, P:P + 1]))
                answer()
                link(dve.tensor_copy(ccol[:, :], ps[:, 0:1]))
                link(dve.tensor_tensor_scan(v(res), v(d0), v(d1), ccol[:, :], op0, op1))

            def next_first(dest, flags, after):
                n = flags.shape[1]
                link(dve.tensor_scalar(dest[:, 0:n - 1], flags[:, 1:n], -BIG, None, ALU.mult))
                link(dve.tensor_copy(col[:, 0:1], flags[:, 0:1]), ask)
                answer()
                link(dve.memset(carry[0:1, P - 1:P], after))
                link(dve.tensor_copy(carry[0:1, 0:P - 1], ps[0:1, 1:P]), ask)
                answer()
                link(dve.tensor_scalar(dest[:, n - 1:n], ps[:, 0:1], -BIG, None, ALU.mult))

            def block_of_steps(g, keys_f, dest, tmp):
                link(dve.tensor_reduce(tmp[:, 0:g.jj], keys_f.rearrange("p (j n) -> p j n", n=P), AX.X, ALU.max))
                link(dve.tensor_scalar(tmp[:, 0:g.jj].bitcast(I32), tmp[:, 0:g.jj].bitcast(I32), 21, 127,
                                       ALU.logical_shift_right, ALU.bitwise_and))
                dve.tensor_scalar(dest[:, 0:g.jj].bitcast(I32), tmp[:, 0:g.jj].bitcast(I32), TILES - 1, None,
                                  ALU.min).then_inc(blocks_ready, 1)

            def marks_of(g, kf, tmp, head, edge, reset, nhead, reset_next):
                link(dve.tensor_scalar(tmp.bitcast(I32), kf.bitcast(I32), TAG | LOW, None, ALU.bitwise_and))
                link(dve.tensor_scalar(head, tmp, TAG_FLOAT, None, ALU.is_equal))
                link(dve.tensor_scalar(edge, tmp, TAG_FLOAT, None, ALU.is_gt if g is GNN else ALU.is_ge))
                link(dve.tensor_scalar(reset, head, -BIG, None, ALU.mult))
                link(dve.tensor_scalar(nhead, head, -1.0, 1.0, ALU.mult, ALU.add))
                next_first(reset_next, head, 1.0)

            def attention(slope, head_v, edge, reset, nhead, reset_next, a_dst_in, a_src_in,
                          adst, v2, mf, mb, t1, out_exp, count, chunk=False, effects=(None,) * 3):
                link(dve.tensor_tensor(t1, head_v, a_dst_in, ALU.mult))
                seg_scan(adst, nhead, t1, ALU.mult, ALU.add, 0.0, state=state[0:1, 0:1] if chunk else None,
                         effect=effects[0])
                link(dve.tensor_scalar(v2, edge, 1.0, BIG, ALU.subtract, ALU.mult))
                link(dve.tensor_tensor(t1, a_src_in, edge, ALU.mult))
                link(dve.tensor_tensor(v2, v2, t1, ALU.add))
                if chunk:
                    link(dve.tensor_copy(state[0:1, 2:3], state[0:1, 1:2]))
                seg_scan(mf, reset, v2, ALU.add, ALU.max, -BIG, state=state[0:1, 1:2] if chunk else None,
                         effect=effects[1])
                seg_scan(mb, reset_next, mf, ALU.add, ALU.max, -BIG, reverse=True, effect=effects[2])
                link(dve.tensor_tensor(mb, mb, adst, ALU.add))
                link(dve.scalar_tensor_tensor(mf, mb, slope, mb, ALU.mult, ALU.max))
                if chunk:
                    x = joined[0:1, 0:1]
                    link(dve.tensor_tensor(x, state[0:1, 2:3], adst[0:1, 0:1], ALU.add))
                    link(dve.scalar_tensor_tensor(x, x, slope, x, ALU.mult, ALU.max))
                    link(dve.tensor_tensor(x, x, mf[0:1, 0:1], ALU.subtract))
                    link(dve.tensor_tensor(x, x, nhead[0:1, 0:1], ALU.mult))
                link(dve.tensor_tensor(v2, v2, adst, ALU.add))
                link(dve.scalar_tensor_tensor(mb, v2, slope, v2, ALU.mult, ALU.max))
                dve.tensor_tensor(t1, mb, mf, ALU.subtract).then_inc(exp_ready, 1)
                dve.wait_ge(exp_done, count)
                link(dve.tensor_tensor(out_exp, out_exp, edge, ALU.mult), ask)

            KF, HD, ED, RS, RN, NH, VF, AD, V2, MF, MB, T1 = c_scan[0:12]
            for v in row_bufs:
                done.add(dve.memset(v[:, :, D], 1.0))
            dve.engine_nop().then_inc(ones_set, 1)
            done.add(dve.memset(R1[:, 0:TILES * 257], 0.0))
            done.add(dve.memset(state[:, :], 0.0))
            dve.wait_ge(dve_done, done.n)
            link(dve.memset(state[:, 1:2], -BIG))
            hots, adds = Tally(hot_ready), Tally(added)
            adds.add(dve.memset(col[:, 0:1], 0.0), 8)

            def chunk_weights(c, kept):
                dve.wait_ge(scores_kept, kept)
                link(dve.tensor_copy(c_keys, KS[:, bass.ds(c * P, P)]))
                link(dve.tensor_copy(c_scores, SC[:, bass.ds(c * P, P)]), ask)
                link(dve.tensor_scalar(T1.bitcast(I32), c_keys.bitcast(I32), 14, 127,
                                       ALU.logical_shift_right, ALU.bitwise_and))
                link(dve.tensor_copy(c_rows, T1.bitcast(I32)))
                last_key = state[0:1, 3:4]
                link(dve.tensor_scalar(joined_block[:, :], last_key.bitcast(I32), 14, 127,
                                       ALU.logical_shift_right, ALU.bitwise_and))
                link(dve.tensor_copy(joined[0:1, 1:2], joined_block[:, :]))
                link(dve.tensor_scalar(joined_block[:, :], last_key.bitcast(I32), 21, 127,
                                       ALU.logical_shift_right, ALU.bitwise_and))
                answer()
                done.add(dve.tensor_copy(VF, ps[:, 512:512 + P]))
                link(dve.tensor_copy(KF, ps[:, 0:P]))
                link(dve.tensor_scalar(T1.bitcast(I32), KF.bitcast(I32), TAG | LOW, None, ALU.bitwise_and))
                done.add(dve.tensor_scalar(HD, T1, TAG_FLOAT, None, ALU.is_equal))
                done.add(dve.tensor_scalar(ED, T1, TAG_FLOAT, None, ALU.is_gt))
                link(dve.tensor_reduce(col[:, 0:1], KF, AX.X, ALU.max))
                link(dve.tensor_copy(col[:, 1:2], HD[:, 0:1]), ask)
                done.add(dve.tensor_scalar(RS, HD, -BIG, None, ALU.mult))
                done.add(dve.tensor_scalar(NH, HD, -1.0, 1.0, ALU.mult, ALU.add))
                done.add(dve.tensor_scalar(RN[:, 0:P - 1], HD[:, 1:P], -BIG, None, ALU.mult))
                done.add(dve.memset(carry[0:1, P - 1:P], 1.0))
                answer()
                link(dve.tensor_copy(row[:, :], ps[0:1, 0:2 * P]))
                link(dve.tensor_copy(carry[0:1, 0:P - 1], row[0:1, P + 1:2 * P]), ask)
                link(dve.tensor_scalar(step_blocks[:, :], row[0:1, 0:P].bitcast(I32), 21, 127,
                                       ALU.logical_shift_right, ALU.bitwise_and))
                link(dve.tensor_reduce(row[0:1, P:P + 1], row[0:1, 0:P], AX.X, ALU.max))
                link(dve.tensor_tensor(last_key, last_key, row[0:1, P:P + 1], ALU.max))
                link(dve.tensor_scalar(step_blocks[:, :], step_blocks[:, :], TILES - 1, None, ALU.min))
                answer()
                link(dve.tensor_scalar(RN[:, P - 1:P], ps[:, 0:1], -BIG, None, ALU.mult))
                attention(0.01, HD, ED, RS, NH, RN, VF, VF, AD, V2, MF, MB, T1, T1, c + 1, chunk=True)
                answer()
                link(dve.tensor_copy(c_weights, ps[:, 0:P]))
                link(dve.tensor_copy(factor[:, 0:2], ps[:, 512:514]))
                link(dve.tensor_tensor(factor[:, 2:3], part_id[:, :], factor[:, 1:2], ALU.is_equal))
                link(dve.tensor_scalar(factor[:, 3:4], factor[:, 2:3], -1.0, 1.0, ALU.mult, ALU.add))
                link(dve.tensor_tensor(factor[:, 0:1], factor[:, 0:1], factor[:, 2:3], ALU.mult))
                done.add(dve.tensor_tensor(factor[:, 0:1], factor[:, 0:1], factor[:, 3:4], ALU.add))
                _, (b,) = nc.values_load_multi_w_load_instructions(
                    joined_block[0:1, 0:1], engines=[mybir.EngineType.DVE], min_val=0, max_val=TILES - 1)
                target = R1[:, bass.ds(b * 257, 257)]
                dve.wait_ge(dve_done, done.n)
                link(dve.tensor_scalar(target, target, factor[:, 0:1], None, ALU.mult))

            def one_hot(i, s):
                hots.add(dve.tensor_scalar(hot[:, s, :], iota_row[:, :], c_rows[:, bass.ds(i * U + s, 1)],
                                           c_weights[:, bass.ds(i * U + s, 1)], ALU.is_equal, ALU.mult))

            def add_turn(c, i, more):
                _, blocks = nc.values_load_multi_w_load_instructions(
                    step_blocks[0:1, bass.ds(i * U, U)],
                    engines=[mybir.EngineType.DVE], min_val=0, max_val=TILES - 1,
                    skip_runtime_bounds_check_because="the blocks are masked and clamped to 0..TILES - 1")
                for h in range(2):
                    for s in range(8):
                        b = blocks[8 * h + s]
                        dve.wait_ge(summed, c * P + i * U + 8 * h + s + 1)
                        target = R1[:, bass.ds(b * 257, 257)]
                        at = adds.add(dve.tensor_tensor(
                            target, target, ps[:, s * 512:s * 512 + 257], ALU.add))
                        if h == 0 or more:
                            one_hot(i + h, 8 * (1 - h) + s)
                        dve.wait_ge(added, at)

            def chunk(c, turns, kept):
                chunk_weights(c, kept)
                for s in range(8):
                    one_hot(0, s)
                with loop(dve, turns - 1, (hots, U), (adds, U)) as i:
                    add_turn(c, i, True)
                add_turn(c, turns - 1, False)

            with loop(dve, CHUNKS - 1, (done, CHUNK_DONE), (ask, CHUNK_ASKS), (back, CHUNK_ASKS), (hots, P), (adds, P)) as c:
                chunk(c, P // U, (c + 1) * 2 * P // U)
            chunk(CHUNKS - 1, LAST_STEPS // U, 2 * GNN.steps // U)

            rden = E[:, 3970:3970 + TILES]
            link(dve.tensor_scalar(rden, ACC[:, :, D], 1e-30, None, ALU.max))
            link(dve.reciprocal(rden, rden))
            used = Tally(residual_used)

            def residual(i, s):
                dve.wait_ge(residual_in[s], (i + 1) * 16)
                tiles = [14 * i + 7 * s + z for z in range(7)]
                x1 = [ACC[:, bass.ds(t, 1), 0:D].rearrange("p o d -> p (o d)") for t in tiles]
                for z, t in enumerate(tiles):
                    done.add(dve.scalar_tensor_tensor(x1[z], x1[z], rden[:, bass.ds(t, 1)], xin[s][:, z, :], ALU.mult, ALU.add))
                dve.wait_ge(dve_done, done.n)
                used.add(dve.memset(col[:, 0:1], 0.0))
                for z, t in enumerate(tiles):
                    done.add(dve.bn_stats(bn[:, bass.ds(t, 1), :].rearrange("p o s -> p (o s)"), x1[z]))

            with loop(dve, 6, (done, 28), (used, 2)) as i:
                for s in range(2):
                    residual(i, s)
            residual(6, 0)
            dve.wait_ge(residual_last, 16)
            residual(6, 1)
            dve.wait_ge(dve_done, done.n)
            statistics()
            dve.engine_nop().then_inc(stat_ready, 1)
            scales(3)

            def keep_turned(g, s, i):
                if i is not None:
                    dve.wait_ge(table_summed, g - 1)
                    dve.wait_ge(xT7_out[s], i * 16)
                for b in range(4):
                    dve.wait_ge(norm_turned, 4 * g + b + 1)
                    part = slice(512 * b, min(512 * b + 512, SEVEN * D))
                    dve.tensor_copy(xT7[s][:, part], ps[:, part]).then_inc(xT7_ready, 1)

            for s in range(2):
                keep_turned(s, s, None)
            with dve.Fori(1, SEVENS // 2) as i:
                for s in range(2):
                    keep_turned(2 * i + s, s, i)

            dve.wait_ge(weights_in, 16 * 5)
            ys = Tally(y_copied)

            def y_copy(n, e, s):
                dve.wait_ge(y_ready, n + 1)
                ys.add(dve.tensor_tensor(ystage[:, s, :, e, :],
                                         ps[:, 2048 + e * 512:2560 + e * 512].rearrange("p (t d) -> p t d", t=2),
                                         b2_all[:, e:e + 1, :].broadcast_to([P, 2, D]), ALU.add))

            for g in range(2):
                for e in range(EXPERTS):
                    y_copy(g * EXPERTS + e, e, g)
            with loop(dve, GROUPS // 2 - 1, (ys, 8)) as i:
                for s in range(2):
                    dve.wait_ge(y_out[s], 16 * (i + 1))
                    for e in range(EXPERTS):
                        y_copy((2 * i + 2 + s) * EXPERTS + e, e, s)
            dve.wait_ge(y_out[0], 16 * (GROUPS // 2))
            for e in range(EXPERTS):
                y_copy((GROUPS - 1) * EXPERTS + e, e, 0)

            fKF, fH, fE, fRS, fRN, fNH, fVS, fVD, fV2, fT1, fX, fMF, fMB = f_scan
            for s in range(2):
                dve.wait_ge(y_out[s], 16 * (GROUPS // 2 + (1 - s)))
            link(dve.engine_nop(), ask)
            to_scan(GATE, fKF)
            marks_of(GATE, fKF, fT1, fH, fE, fRS, fNH, fRN)
            block_of_steps(GATE, fKF, fMF, fMB)
            link(dve.tensor_scalar(fX.bitcast(I32), FK[:, :].bitcast(I32), 14, 127,
                                   ALU.logical_shift_right, ALU.bitwise_and))
            link(dve.tensor_copy(FK[:, :], fX.bitcast(I32)))
            for i, d0 in enumerate((fNH, fRS, fRN)):
                done.add(dve.tensor_reduce(effects[:, i:i + 1], d0, AX.X, ALU.min))
            dve.wait_ge(dve_done, done.n)
            dve.wait_ge(gate_in, 32)
            link(dve.tensor_copy(fMF[0:1, :], fMB[0:1, :].bitcast(I32)))
            link(dve.tensor_tensor_scan(fMB[0:1, :], fMF[0:1, :], fMF[0:1, :], 0.0, ALU.max, ALU.max))
            link(dve.tensor_copy(fMF[0:1, :], fMB[0:1, :]))
            dve.engine_nop().then_inc(blocks_ready, 1)
            dve.wait_ge(gate_in, 64)
            n = GATE.steps
            upto = fX[:, 0:n]
            link(dve.tensor_scalar(upto, block_rows[:, 0:n], part_id[:, :], None, ALU.is_le))
            link(dve.tensor_reduce(ccol[:, :], upto, AX.X, ALU.add))
            link(dve.tensor_scalar(last_col[:, :], ccol[:, :], -1.0, 0.0, ALU.add, ALU.max))
            dve.engine_nop().then_inc(blocks_ready, 1)
            dve.wait_ge(rows_kept, GATE_KEPT)
            link(dve.memset(keep[:, 0:1], 0.0))
            link(dve.tensor_tensor(keep[:, 1:n], block_rows[:, 1:n], block_rows[:, 0:n - 1], ALU.is_equal))
            link(dve.engine_nop(), ask)
            for hd in range(HEADS):
                to_scan(GATE, fVS)
                link(dve.engine_nop(), ask)
                to_scan(GATE, fVD)
                attention(0.2, fH, fE, fRS, fNH, fRN, fVD, fVS, fVD, fV2, fMF, fMB, fT1, fX, CHUNKS + 1 + hd,
                          effects=[effects[:, i:i + 1] for i in range(3)])
                answer()
                link(dve.tensor_copy(G[:, :, HE + hd].rearrange("p (k j) -> p j k", j=GATE.jj),
                                     ps[:, 0:GATE.q].rearrange("p (j k) -> p j k", k=P)),
                     ask if hd < HEADS - 1 else None)
                dve.engine_nop().then_inc(head_weights, 1)
            messages(dve, HEADS - 1).then_inc(messages_ready, 1)
            dve.wait_ge(messages_ready, HEADS)

            dve.engine_nop().then_inc(blocks_ready, 1)
            hots2 = Tally(hot_ready, hots.n)

            def plain_hots(i, h):
                rows = FK[:, bass.ds(i * U + 8 * h, 8)].rearrange("p (s o) -> p s o", o=1)
                hots2.add(dve.tensor_tensor(plain_hot[:, 8 * h:8 * h + 8, :], iota_row[:, :].rearrange("p (o n) -> p o n", o=1)
                                            .broadcast_to([P, 8, P]), rows.broadcast_to([P, 8, P]), ALU.is_equal))

            dve.engine_nop().then_inc(agg_done, 2)
            plain_hots(0, 0)
            plain_hots(0, 1)
            turns = GATE.steps // U
            with loop(dve, turns - 1, (hots2, 2)) as i:
                for h in range(2):
                    dve.wait_ge(agg_ready, 2 * i + h + 1)
                    plain_hots(i + 1, h)
            dve.wait_ge(agg_done, 2 * turns + 2)
            for w in range(20):
                ch = G[:, 0:GATE.steps, w]
                link(dve.tensor_tensor_scan(ch, keep[:, 0:GATE.steps], ch, 0.0, ALU.mult, ALU.add))
            dve.wait_ge(gate_in, 96)
            dve.wait_ge(dve_done, done.n)
            dve.engine_nop().then_inc(running_sums, 1)
            with dve.Fori(0, TILES // 14) as i:
                last_sums(dve, mybir.EngineType.DVE, 2 * i)
            dve.wait_ge(sums_taken, TILES)
            dve.engine_nop().then_inc(blocks_ready, 1)
            dve.wait_ge(gates_need, 48)

            link(dve.tensor_scalar(den, sums[:, :, HE:HE + 4], 1e-16, None, ALU.add))
            link(dve.reciprocal(den, den))
            for hd in range(HEADS):
                link(dve.tensor_tensor(agg[:, :, hd * 4:hd * 4 + 4], sums[:, :, hd * 4:hd * 4 + 4],
                                       den[:, :, hd:hd + 1].broadcast_to([P, TILES, 4]), ALU.mult))

            def per_score(v):
                return v.rearrange("p (o n) -> p o n", o=1).broadcast_to([P, TILES, HE])

            link(dve.tensor_tensor(agg, agg, per_score(gat_bias), ALU.add))
            link(dve.tensor_reduce(mu, agg, AX.X, ALU.add))
            link(dve.tensor_scalar(mu, mu, 1.0 / HE, None, ALU.mult))
            mu3 = mu.rearrange("p (t o) -> p t o", o=1).broadcast_to([P, TILES, HE])
            link(dve.tensor_tensor(agg, agg, mu3, ALU.subtract))
            link(dve.tensor_tensor(squares, agg, agg, ALU.mult))
            link(dve.tensor_reduce(var, squares, AX.X, ALU.add))
            dve.tensor_scalar(var, var, 1.0 / HE, None, ALU.mult).then_inc(exp_ready, 1)
            dve.wait_ge(exp_done, CHUNKS + HEADS + 1)
            link(dve.reciprocal(mu, mu))
            link(dve.tensor_tensor(agg, agg, mu3, ALU.mult))
            link(dve.tensor_tensor(agg, agg, per_score(gamma), ALU.mult))
            link(dve.tensor_tensor(agg, agg, per_score(beta), ALU.add))
            link(dve.tensor_reduce(scores, agg.rearrange("p t (h e) -> p t e h", e=EXPERTS), AX.X, ALU.add))
            link(dve.tensor_scalar(scores, scores, 1.0 / HEADS, None, ALU.mult))
            link(dve.memset(beaten, 0.0))
            for i in range(EXPERTS):
                for j in range(i + 1, EXPERTS):
                    link(dve.tensor_tensor(var, scores[:, :, i], scores[:, :, j], ALU.is_ge))
                    link(dve.tensor_tensor(beaten[:, :, j], beaten[:, :, j], var, ALU.add))
                    link(dve.tensor_scalar(var, var, -1.0, 1.0, ALU.mult, ALU.add))
                    link(dve.tensor_tensor(beaten[:, :, i], beaten[:, :, i], var, ALU.add))
            link(dve.tensor_reduce(mu, scores, AX.X, ALU.max))
            mu4 = mu.rearrange("p (t o) -> p t o", o=1).broadcast_to([P, TILES, EXPERTS])
            dve.tensor_tensor(scores, scores, mu4, ALU.subtract).then_inc(exp_ready, 1)
            link(dve.tensor_scalar(beaten, beaten, 1.5, None, ALU.is_lt))
            dve.wait_ge(exp_done, CHUNKS + HEADS + 2)
            link(dve.tensor_tensor(beaten, beaten, gates, ALU.mult))
            link(dve.tensor_reduce(mu, beaten, AX.X, ALU.add))
            link(dve.reciprocal(mu, mu))
            link(dve.tensor_tensor(gates, beaten, mu4, ALU.mult))

            fins = Tally(fin_ready)

            def mix(g, s, n, tiles=MIXED):
                dve.wait_ge(fin_in[s], 32 * n)
                before = {}
                for e in range(EXPERTS):
                    for z in range(tiles):
                        if e:
                            dve.wait_ge(dve_done, before[z])
                        o = dve.scalar_tensor_tensor(x1in[s][:, z, :], yin[s][:, z, e * D:(e + 1) * D],
                                                     gates[:, bass.ds(g * MIXED + z, 1), e:e + 1].rearrange("p o e -> p (o e)"),
                                                     x1in[s][:, z, :], ALU.mult, ALU.add)
                        if e < EXPERTS - 1:
                            before[z] = done.add(o)
                        else:
                            fins.add(o)

            with loop(dve, MIXES // RING, (done, RING * 12), (fins, RING * MIXED)) as i:
                for s in range(RING):
                    mix(RING * i + s, s, i + 1)
            mix(MIXES, 0, MIXES // RING + 1, 2)

        @block.tensor
        def _(pe):
            asked = Tally(to_turn)

            def asked_for():
                pe.wait_ge(to_turn, asked.pass_by())

            pe.wait_ge(consts_in, 64)
            pe.wait_ge(w_in, 16 * 7)
            pe.wait_ge(dve_done, 2)
            for k in range(4):
                kd, kn = k % 2, k // 2
                pe.transpose(ps[:, 2048 + k * P:2048 + (k + 1) * P], w_nat[:, kn, kd * P:(kd + 1) * P],
                             ident[:, :]).then_inc(prep_turned, 1)
            for kd in range(2):
                for kn in range(2):
                    pe.matmul(ps[:, 2560 + 2 * kd:2562 + 2 * kd], w_nat[:, kn, kd * P:(kd + 1) * P], wa[:, kn, :],
                              start=kn == 0, stop=kn == 1)
            for kn in range(2):
                ins = pe.matmul(ps[0:1, 3072:3074], bcol[:, kn:kn + 1], wa[:, kn, :], start=kn == 0, stop=kn == 1)
            ins.then_inc(prep_turned, 1)
            pe.wait_ge(proj_ready, 1)

            def turn_x(t, s, first=False):
                pe.wait_ge(xn_ready, t + 1)
                if not first:
                    pe.wait_ge(xT_ready, t - 1)
                for k in range(2):
                    ins = pe.transpose(psT[s][:, k * P:(k + 1) * P], xn[s][:, k * P:(k + 1) * P], ident[:, :])
                ins.then_inc(xn_turned, 1)

            def project_x(t, s, first=False):
                pe.wait_ge(xT_ready, t + 1)
                if not first:
                    pe.wait_ge(lin_copied, t - 1)
                for k in range(2):
                    pe.matmul(psL[s], xT[s][:, k * P:(k + 1) * P], proj[:, k, :], start=k == 0, stop=False)
                pe.matmul(psL[s], ones_row[:, :], bias_row[:, :], start=False, stop=True).then_inc(lin_ready, 1)

            turn_x(0, 0, True); turn_x(1, 1, True)
            project_x(0, 0, True); turn_x(2, 0); project_x(1, 1, True)
            with pe.Fori(1, NP2 - 1) as i:
                for s in range(2):
                    turn_x(2 * i + 1 + s, 1 - s)
                    project_x(2 * i + s, s)
            turn_x(TILES - 1, 1)
            project_x(TILES - 2, 0)
            project_x(TILES - 1, 1)

            def sort_turns():
                for c in turn_buffers():
                    asked_for()
                    for i in range(16):
                        ins = pe.transpose(ps[:, i * P:(i + 1) * P], sort_bufs[c][:, i * P:(i + 1) * P], ident[:, :])
                        if i in (7, 15):
                            ins.then_inc(turned, 1)

            def turn(source, g):
                asked_for()
                v = source.rearrange("p (k j) -> p j k", j=g.jj)
                for j in range(g.jj):
                    ins = pe.transpose(ps[:, j * P:(j + 1) * P], v[:, j, :], ident[:, :])
                ins.then_inc(turned, 1)

            def turn_back(source, g):
                asked_for()
                for j in range(g.jj):
                    ins = pe.transpose(ps[:, j * P:(j + 1) * P], source[:, j * P:(j + 1) * P], ident[:, :])
                ins.then_inc(turned, 1)

            def carries():
                asked_for()
                pe.transpose(ps[0:1, 0:P], col[:, 0:1], ident[:, :])
                pe.transpose(ps[0:1, P:2 * P], col[:, 1:2], ident[:, :]).then_inc(turned, 1)

            def carry_back(first):
                asked_for()
                pe.matmul(ps[:, 0:1], carry[0:1, first:first + P], ident[0:1, 0:1],
                          start=True, stop=True).then_inc(turned, 1)

            def first_flags():
                asked_for()
                pe.transpose(ps[0:1, 0:P], col[:, 0:1], ident[:, :]).then_inc(turned, 1)
                carry_back(0)

            def attention_turns():
                carries(); carry_back(0)
                carries(); carry_back(0)
                carries(); carry_back(1)

            sort_turns()
            sort_turns()

            def chunk(c, turns):
                asked_for()
                pe.transpose(ps[:, 0:P], c_keys, ident[:, :])
                pe.transpose(ps[:, 512:512 + P], c_scores, ident[:, :]).then_inc(turned, 1)
                carries(); carry_back(0)
                attention_turns()
                asked_for()
                pe.transpose(ps[:, 0:P], c_scan[11], ident[:, :])
                pe.matmul(ps[:, 512:514], ones_row[:, :], joined[:, :], start=True, stop=True).then_inc(turned, 1)
                with pe.Fori(0, turns) as i:
                    for s in range(32):
                        q = c * P + i * 32 + s
                        pe.wait_ge(hot_ready, q + 1)
                        if s % 8 == 0:
                            pe.wait_ge(rows_in[s // 8], (c * (P // 32) + i + 1) * 16)
                        pe.wait_ge(added, q + 1)
                        pe.matmul(ps[:, (s % 8) * 512:(s % 8) * 512 + 257], hot[:, s % U, :],
                                  row_bufs[s // U][:, s % U, :], start=True, stop=True).then_inc(summed, 1)

            with loop(pe, CHUNKS - 1, (asked, CHUNK_ASKS)) as c:
                chunk(c, P // 32)
            chunk(CHUNKS - 1, LAST_STEPS // 32)

            pe.wait_ge(gate_w_ready, 1)
            pe.wait_ge(added, GNN.steps + 8)

            def turn_seven(g, s, first):
                for z in range(SEVEN):
                    if not first and z % 2 == 0:
                        pe.wait_ge(xT7_ready, 4 * g - 4 + z // 2 + 1)
                    pe.wait_ge(norm_ready, g * SEVEN + z + 1)
                    for k in range(2):
                        part = slice(z * D + k * P, z * D + (k + 1) * P)
                        ins = pe.transpose(ps[:, part], norm7[s][:, part], ident[:, :])
                    if z % 2 or z == SEVEN - 1:
                        ins.then_inc(norm_turned, 1)

            def project_seven(g, s, first):
                pe.wait_ge(xT7_ready, 4 * g + 4)
                if not first:
                    pe.wait_ge(table_ready, g - 1)
                for z in range(SEVEN):
                    for k in range(2):
                        ins = pe.matmul(ps7[s][:, z * GW_IN:(z + 1) * GW_IN],
                                        xT7[s][:, z * D + k * P:z * D + (k + 1) * P], gate_w[:, k, :],
                                        start=k == 0, stop=k == 1)
                ins.then_inc(table_summed, 1)

            turn_seven(0, 0, True)
            turn_seven(1, 1, False)
            project_seven(0, 0, True)
            turn_seven(2, 0, False)
            project_seven(1, 1, True)
            with pe.Fori(1, SEVENS // 2 - 1) as i:
                for s in range(2):
                    turn_seven(2 * i + 1 + s, 1 - s, False)
                    project_seven(2 * i + s, s, False)
            turn_seven(SEVENS - 1, 1, False)
            for s in range(2):
                project_seven(SEVENS - 2 + s, s, False)

            pe.wait_ge(weights_in, 16 * 5)
            pe.wait_ge(table_ready, SEVENS)

            def hidden(n, e, s, first):
                for f in range(4):
                    if not first:
                        pe.wait_ge(gelu_done, (n - 2) * 4 + (f | 1) + 1)
                    for k in range(2):
                        ins = pe.matmul(ps[:, (e % 2) * 1024 + f * 256:(e % 2) * 1024 + (f + 1) * 256],
                                        w1[:, k, e * HID + f * P:e * HID + (f + 1) * P],
                                        xe[:, s, :, k, :], start=k == 0, stop=k == 1)
                    ins.then_inc(hid_ready, 1)

            def outputs(n, e, first):
                pe.wait_ge(gelu_done, (n + 1) * 4)
                if not first:
                    pe.wait_ge(y_copied, n - 3)
                for t in range(2):
                    for f in range(4):
                        ins = pe.matmul(ps[:, 2048 + e * 512 + t * 256:2048 + e * 512 + (t + 1) * 256],
                                        hidT[:, e % 2, f, t * P:(t + 1) * P], w2[:, 4 * e + f, :],
                                        start=f == 0, stop=f == 3)
                ins.then_inc(y_ready, 1)

            def group(g, s, first_group, i=None):
                for e in range(EXPERTS):
                    n = g * EXPERTS + e
                    if e < EXPERTS - 1:
                        hidden(n + 1, e + 1, s, first_group and e + 1 < 2)
                    elif i is not None:
                        pe.wait_ge(xe_in[1 - s], 16 * (i + 1 + s))
                        hidden(n + 1, 0, 1 - s, False)
                    outputs(n, e, first_group)

            pe.wait_ge(xe_in[0], 16)
            hidden(0, 0, 0, True)
            group(0, 0, True, 0)
            group(1, 1, False, 0)
            with pe.Fori(1, GROUPS // 2) as i:
                for s in range(2):
                    group(i * 2 + s, s, False, i)
            group(GROUPS - 1, 0, False)

            turn(FK[:, :], GATE)
            first_flags()
            for hd in range(HEADS):
                turn(G[:, :, HE + hd], GATE)
                turn(G[:, :, HE + 4 + hd], GATE)
                attention_turns()
                turn_back(f_scan[10], GATE)
            with pe.Fori(0, GATE.steps // U) as i:
                for h in range(2):
                    pe.wait_ge(hot_ready, GNN.steps + 2 * i + h + 1)
                    pe.wait_ge(low_ready, 2 * i + h + 1)
                    pe.wait_ge(agg_done, 2 * i + h + 1)
                    for s in range(8):
                        for k in range(3):
                            ins = pe.matmul(ps[:, h * 512 + s * 20:h * 512 + (s + 1) * 20],
                                            plain_hot[:, 8 * h + s, :], parts[:, h, s, k, :],
                                            start=k == 0, stop=k == 2)
                    ins.then_inc(agg_ready, 1)


def shape_constants():
    part = np.arange(P)

    def sign(k):
        return np.where((part >> (k - 11)) & 1, -1.0, 1.0)

    signs = np.stack([sign(11)] + [sign(k) * sign(k - 1) for k in range(12, 19)], axis=1)
    return {
        "ident": np.eye(P, dtype=np.float32),
        "iota_row": np.tile(part.astype(np.float32), (P, 1)),
        "signs": signs.astype(np.float32),
        "part_id": part.astype(np.float32)[:, None],
        "headers": np.arange(NODES, dtype=np.int32).reshape(HEADER_PARTS, HEADERS),
    }


def kernel(**inputs):
    import concourse.bacc as bacc
    from concourse.bass_utils import run_bass_kernel_spmd

    nc = bacc.Bacc("TRN2", target_bir_lowering=False, num_devices=1)
    arrays, a, consts = {}, {}, {}
    for full, array in inputs.items():
        name = full.removeprefix("L0_gnn_").removeprefix("L0_ffn_")
        array = np.ascontiguousarray(array)
        arrays[f"in_{name}"] = array
        a[name] = nc.dram_tensor(f"in_{name}", array.shape, mybir.dt.from_np(array.dtype), kind="ExternalInput").ap()
    for name, array in shape_constants().items():
        arrays[f"const_{name}"] = array
        consts[name] = nc.dram_tensor(f"const_{name}", array.shape, mybir.dt.from_np(array.dtype),
                                      kind="ExternalInput").ap()
    out = nc.dram_tensor("out", (NODES, D), FP32, kind="ExternalOutput").ap()
    program(nc, a, out, consts)
    return run_bass_kernel_spmd(nc, [arrays], core_ids=[0]).results[0]["out"]
```
